# Optimizing a Trainium2 kernel written in Bass

```python
import numpy as np
import jax
import jax.numpy as jnp

def _softmax(x, axis=-1):
    return jax.nn.softmax(x, axis=axis)

def _gelu(x):
    return jax.nn.gelu(x, approximate=True)

def _silu(x):
    return jax.nn.silu(x)

def _sigmoid(x):
    return jax.nn.sigmoid(x)

def _layernorm(x, axis=-1, eps=1e-05):
    m = jnp.mean(x, axis=axis, keepdims=True)
    v = jnp.var(x, axis=axis, keepdims=True)
    return (x - m) / jnp.sqrt(v + eps)

def _scatter_add(tgt, idx, src, axis=0):
    return tgt.at[idx].add(src)

def _segment_sum(src, seg, n):
    return jax.ops.segment_sum(src, seg, n)
kernel_name = 'mk_xattn_ffn_d2_seqx_r8_ec252b'

def setup_inputs(seed: int=0):
    np.random.seed(seed)
    _w = jnp.asarray

    def _rec_inputs():
        import jax
        import jax.numpy as jnp
        _rk = jax.random.key(seed)
        x = 7.22e-05 + 1 * jax.random.normal(jax.random.fold_in(_rk, 1), (128, 64, 128), jnp.float32)
        _lenS = 64 - jax.random.randint(jax.random.fold_in(_rk, 7), (128,), 0, max(1, 64 // 4) + 1, jnp.int32)
        _lenS2 = 64 - jax.random.randint(jax.random.fold_in(_rk, 8), (128,), 0, max(1, 64 // 4) + 1, jnp.int32)
        _ctx_1024P = jax.random.normal(jax.random.fold_in(_rk, 11), (128, 16, 128), jnp.float32)
        _ctx_1024c = jax.random.dirichlet(jax.random.fold_in(_rk, 511), 0.3 * jnp.ones((16,), jnp.float32), (128, 64))
        _ctx_1024t = jnp.einsum('bsk,bkd->bsd', _ctx_1024c, _ctx_1024P)
        _ctx_1024t = _ctx_1024t * jax.lax.rsqrt(jnp.mean(jnp.square(_ctx_1024t)) + 1e-12) * 0.953939
        ctx_1024 = 4.13588e-05 + 0.999923 * (_ctx_1024t + 0.3 * jax.random.normal(jax.random.fold_in(_rk, 611), (128, 64, 128), jnp.float32))
        return (x, ctx_1024)
    x, ctx_1024 = _rec_inputs()

    def _L0_xattn_setup():
        import jax, jax.numpy as jnp
        import numpy as np
        EMBED_DIM = 128
        HEAD_DIM = 128
        GAMMA = 0.96875
        THETA = 10000.0
        SCALE_BASE = 512.0

        def _dup_interleave(x):
            return jnp.repeat(x, 2, axis=-1)

        def _rotate_half(x):
            x_even = x[..., ::2]
            x_odd = x[..., 1::2]
            return jnp.stack((-x_odd, x_even), axis=-1).reshape(x.shape)

        def _xpos(x, offset=0, inverse_scale=False):
            l = x.shape[-2]
            half = HEAD_DIM // 2
            scale_vec = (jnp.arange(0, HEAD_DIM, 2, dtype=jnp.float32) + 0.4 * HEAD_DIM) / (1.4 * HEAD_DIM)
            pos = jnp.arange(offset, offset + l, dtype=jnp.float32)
            scale = scale_vec[None, :] ** (pos / SCALE_BASE)[:, None]
            freqs = 1.0 / THETA ** (jnp.arange(half, dtype=jnp.float32) / half)
            sin_in = pos[:, None] * freqs[None, :]
            sin, cos = (jnp.sin(sin_in), jnp.cos(sin_in))
            if inverse_scale:
                scale = 1.0 / scale
            return x * _dup_interleave(cos * scale) + _rotate_half(x) * _dup_interleave(sin * scale)

        def _decay_mask(l, gamma):
            idx = jnp.arange(l, dtype=jnp.float32)
            diff = idx[:, None] - idx[None, :]
            return jnp.where(diff >= 0, gamma ** diff, 0.0)
        key = jax.random.key(seed)
        k1, k2, k3, k4, k5, k6 = jax.random.split(key, 6)
        B, L = (4, 256)
        s = 1.0 / np.sqrt(EMBED_DIM)
        return {'q': jax.random.normal(k1, (B, L, EMBED_DIM), dtype=jnp.float32), 'k': jax.random.normal(k2, (B, L, EMBED_DIM), dtype=jnp.float32), 'v': jax.random.normal(k3, (B, L, EMBED_DIM), dtype=jnp.float32), 'Wq': jax.random.normal(k4, (EMBED_DIM, HEAD_DIM), dtype=jnp.float32) * s, 'Wk': jax.random.normal(k5, (EMBED_DIM, HEAD_DIM), dtype=jnp.float32) * s, 'Wv': jax.random.normal(k6, (EMBED_DIM, HEAD_DIM), dtype=jnp.float32) * s}
    _L0_xattn_all = _L0_xattn_setup()
    _L0_xattn_in = {k: v for k, v in _L0_xattn_all.items() if k in ('Wq', 'Wk', 'Wv')}
    del _L0_xattn_all

    def _L0_ffn_setup():
        import jax, jax.numpy as jnp
        import numpy as np
        B, T, C = (2, 256, 128)
        E, H, TOPK = (8, 256, 2)
        key = jax.random.key(seed)
        k0, k1, k2, k3 = jax.random.split(key, 4)
        scale = 0.02
        return {'x': jax.random.normal(k0, (B, T, C), dtype=jnp.float32), 'Wg': jax.random.normal(k1, (C, E), dtype=jnp.float32) * scale, 'W1': jax.random.normal(k2, (E, C, H), dtype=jnp.float32) * scale, 'W2': jax.random.normal(k3, (E, H, C), dtype=jnp.float32) * scale}
    _L0_ffn_all = _L0_ffn_setup()
    _L0_ffn_in = {k: v for k, v in _L0_ffn_all.items() if k in ('Wg', 'W1', 'W2')}
    del _L0_ffn_all

    def _L1_xattn_setup():
        import jax, jax.numpy as jnp
        import numpy as np
        B, S, D, DFF = (4, 256, 128, 512)
        EPS = 1e-05

        def layernorm(x, gamma, beta):
            mu = jnp.mean(x, axis=-1, keepdims=True)
            var = jnp.var(x, axis=-1, keepdims=True)
            return (x - mu) * jax.lax.rsqrt(var + EPS) * gamma + beta

        def attention(Q, K, V, causal):
            d_k = Q.shape[-1]
            scores = jnp.einsum('bqd,bkd->bqk', Q, K) / jnp.sqrt(jnp.asarray(d_k, Q.dtype))
            if causal:
                q_len, k_len = (scores.shape[-2], scores.shape[-1])
                mask = jnp.tril(jnp.ones((q_len, k_len), dtype=bool))
                scores = jnp.where(mask[None], scores, jnp.asarray(-jnp.inf, scores.dtype))
            w = jax.nn.softmax(scores, axis=-1)
            return jnp.einsum('bqk,bkd->bqd', w, V)
        key = jax.random.key(seed)
        ks = jax.random.split(key, 12)
        sd = 0.02
        return {'y': jax.random.normal(ks[0], (B, S, D), jnp.float32), 'Z': jax.random.normal(ks[1], (B, S, D), jnp.float32), 'w1': jax.random.normal(ks[2], (D, DFF), jnp.float32) * sd, 'b1': jnp.zeros((DFF,), jnp.float32), 'w2': jax.random.normal(ks[3], (DFF, D), jnp.float32) * sd, 'b2': jnp.zeros((D,), jnp.float32), 'g1': jnp.ones((D,), jnp.float32), 'beta1': jnp.zeros((D,), jnp.float32), 'g2': jnp.ones((D,), jnp.float32), 'beta2': jnp.zeros((D,), jnp.float32), 'g3': jnp.ones((D,), jnp.float32), 'beta3': jnp.zeros((D,), jnp.float32)}
    _L1_xattn_all = _L1_xattn_setup()
    _L1_xattn_in = {k: v for k, v in _L1_xattn_all.items() if k in ('w1', 'b1', 'w2', 'b2', 'g1', 'beta1', 'g2', 'beta2', 'g3', 'beta3')}
    del _L1_xattn_all

    def _L1_ffn_setup():
        import jax, jax.numpy as jnp
        import numpy as np
        EPS = 1e-05

        def _layernorm(x, w, b):
            mu = jnp.mean(x, axis=-1, keepdims=True)
            var = jnp.mean((x - mu) ** 2, axis=-1, keepdims=True)
            return (x - mu) * jax.lax.rsqrt(var + EPS) * w + b

        def _rope_tables(T, D, base=10000.0):
            inv_freq = 1.0 / base ** (jnp.arange(0, D, 2, dtype=jnp.float32) / D)
            t = jnp.arange(T, dtype=jnp.float32)
            freqs = jnp.einsum('i,j->ij', t, inv_freq)
            emb = jnp.concatenate([freqs, freqs], axis=-1)
            return (jnp.cos(emb), jnp.sin(emb))

        def _rotate_half(x):
            x1, x2 = (x[..., :x.shape[-1] // 2], x[..., x.shape[-1] // 2:])
            return jnp.concatenate([-x2, x1], axis=-1)

        def _attn(x, ln_w, ln_b, conv_w, attn_w, proj_w, n_head):
            B, T, C = x.shape
            D = C // n_head
            h = _layernorm(x, ln_w, ln_b)
            hc = jnp.transpose(h, (0, 2, 1))
            hc = jnp.pad(hc, ((0, 0), (0, 0), (2, 0)))
            hc = jax.lax.conv_general_dilated(hc, conv_w, window_strides=(1,), padding='VALID', dimension_numbers=('NCH', 'OIH', 'NCH'), feature_group_count=C)
            h = jnp.transpose(hc, (0, 2, 1))
            qkv = h @ attn_w
            q, k, v = jnp.split(qkv, 3, axis=-1)
            q = q.reshape(B, T, n_head, D)
            k = k.reshape(B, T, n_head, D)
            v = v.reshape(B, T, n_head, D)
            cos, sin = _rope_tables(T, D)
            cos = cos[None, :, None, :]
            sin = sin[None, :, None, :]
            q = q * cos + _rotate_half(q) * sin
            k = k * cos + _rotate_half(k) * sin
            scores = jnp.einsum('bqhd,bkhd->bhqk', q, k) / jnp.sqrt(jnp.float32(D))
            causal = jnp.tril(jnp.ones((T, T), dtype=bool))
            scores = jnp.where(causal, scores, jnp.float32(-1e+30))
            p = jax.nn.softmax(scores, axis=-1)
            y = jnp.einsum('bhqk,bkhd->bqhd', p, v).reshape(B, T, C)
            return y @ proj_w

        def _moe(x, ln_w, ln_b, router_w, expert_wv, expert_proj):
            h = _layernorm(x, ln_w, ln_b)
            logits = h @ router_w
            expert_idx = jnp.argmax(logits, axis=-1)
            E = router_w.shape[-1]
            out = jnp.zeros_like(x)
            for e in range(E):
                gv = h @ expert_wv[e]
                gate_raw, value = jnp.split(gv, 2, axis=-1)
                y = gate_raw * jax.nn.sigmoid(gate_raw) * value @ expert_proj[e]
                out = out + jnp.where((expert_idx == e)[..., None], y, 0.0)
            return out
        C, H, E, B, T = (128, 16, 4, 4, 128)
        Dff = 4 * C
        key = jax.random.key(seed)
        ks = jax.random.split(key, 8)
        s = 0.02
        return {'x': jax.random.normal(ks[0], (B, T, C), dtype=jnp.float32), 'ln1_w': jnp.ones((C,), jnp.float32), 'ln1_b': jnp.zeros((C,), jnp.float32), 'ln2_w': jnp.ones((C,), jnp.float32), 'ln2_b': jnp.zeros((C,), jnp.float32), 'conv_w': jax.random.normal(ks[1], (C, 1, 3), dtype=jnp.float32) * 0.1, 'attn_w': jax.random.normal(ks[2], (C, 3 * C), dtype=jnp.float32) * s, 'proj_w': jax.random.normal(ks[3], (C, C), dtype=jnp.float32) * s, 'router_w': jax.random.normal(ks[4], (C, E), dtype=jnp.float32) * s, 'expert_wv': jax.random.normal(ks[5], (E, C, 2 * Dff), dtype=jnp.float32) * s, 'expert_proj': jax.random.normal(ks[6], (E, Dff, C), dtype=jnp.float32) * s}
    _L1_ffn_all = _L1_ffn_setup()
    _L1_ffn_in = {k: v for k, v in _L1_ffn_all.items() if k in ('ln1_w', 'ln1_b', 'ln2_w', 'ln2_b', 'conv_w', 'attn_w', 'proj_w', 'router_w', 'expert_wv', 'expert_proj')}
    del _L1_ffn_all
    return {'x': x, 'ctx_1024': ctx_1024, 'L0_xattn_Wq': _L0_xattn_in['Wq'], 'L0_xattn_Wk': _L0_xattn_in['Wk'], 'L0_xattn_Wv': _L0_xattn_in['Wv'], 'L0_ffn_Wg': _L0_ffn_in['Wg'], 'L0_ffn_W1': _L0_ffn_in['W1'], 'L0_ffn_W2': _L0_ffn_in['W2'], 'L1_xattn_w1': _L1_xattn_in['w1'], 'L1_xattn_b1': _L1_xattn_in['b1'], 'L1_xattn_w2': _L1_xattn_in['w2'], 'L1_xattn_b2': _L1_xattn_in['b2'], 'L1_xattn_g1': _L1_xattn_in['g1'], 'L1_xattn_beta1': _L1_xattn_in['beta1'], 'L1_xattn_g2': _L1_xattn_in['g2'], 'L1_xattn_beta2': _L1_xattn_in['beta2'], 'L1_xattn_g3': _L1_xattn_in['g3'], 'L1_xattn_beta3': _L1_xattn_in['beta3'], 'L1_ffn_ln1_w': _L1_ffn_in['ln1_w'], 'L1_ffn_ln1_b': _L1_ffn_in['ln1_b'], 'L1_ffn_ln2_w': _L1_ffn_in['ln2_w'], 'L1_ffn_ln2_b': _L1_ffn_in['ln2_b'], 'L1_ffn_conv_w': _L1_ffn_in['conv_w'], 'L1_ffn_attn_w': _L1_ffn_in['attn_w'], 'L1_ffn_proj_w': _L1_ffn_in['proj_w'], 'L1_ffn_router_w': _L1_ffn_in['router_w'], 'L1_ffn_expert_wv': _L1_ffn_in['expert_wv'], 'L1_ffn_expert_proj': _L1_ffn_in['expert_proj']}

def reference(x, ctx_1024, L0_xattn_Wq, L0_xattn_Wk, L0_xattn_Wv, L0_ffn_Wg, L0_ffn_W1, L0_ffn_W2, L1_xattn_w1, L1_xattn_b1, L1_xattn_w2, L1_xattn_b2, L1_xattn_g1, L1_xattn_beta1, L1_xattn_g2, L1_xattn_beta2, L1_xattn_g3, L1_xattn_beta3, L1_ffn_ln1_w, L1_ffn_ln1_b, L1_ffn_ln2_w, L1_ffn_ln2_b, L1_ffn_conv_w, L1_ffn_attn_w, L1_ffn_proj_w, L1_ffn_router_w, L1_ffn_expert_wv, L1_ffn_expert_proj):
    import jax
    import jax.numpy as jnp

    def _L0_xattn_ref(q, k, v, Wq, Wk, Wv):
        import jax, jax.numpy as jnp
        import numpy as np
        EMBED_DIM = 128
        HEAD_DIM = 128
        GAMMA = 0.96875
        THETA = 10000.0
        SCALE_BASE = 512.0

        def _dup_interleave(x):
            return jnp.repeat(x, 2, axis=-1)

        def _rotate_half(x):
            x_even = x[..., ::2]
            x_odd = x[..., 1::2]
            return jnp.stack((-x_odd, x_even), axis=-1).reshape(x.shape)

        def _xpos(x, offset=0, inverse_scale=False):
            l = x.shape[-2]
            half = HEAD_DIM // 2
            scale_vec = (jnp.arange(0, HEAD_DIM, 2, dtype=jnp.float32) + 0.4 * HEAD_DIM) / (1.4 * HEAD_DIM)
            pos = jnp.arange(offset, offset + l, dtype=jnp.float32)
            scale = scale_vec[None, :] ** (pos / SCALE_BASE)[:, None]
            freqs = 1.0 / THETA ** (jnp.arange(half, dtype=jnp.float32) / half)
            sin_in = pos[:, None] * freqs[None, :]
            sin, cos = (jnp.sin(sin_in), jnp.cos(sin_in))
            if inverse_scale:
                scale = 1.0 / scale
            return x * _dup_interleave(cos * scale) + _rotate_half(x) * _dup_interleave(sin * scale)

        def _decay_mask(l, gamma):
            idx = jnp.arange(l, dtype=jnp.float32)
            diff = idx[:, None] - idx[None, :]
            return jnp.where(diff >= 0, gamma ** diff, 0.0)
        qh = _xpos(q @ Wq, offset=0, inverse_scale=False)
        kh = _xpos(k @ Wk, offset=0, inverse_scale=True)
        vh = v @ Wv
        L = qh.shape[-2]
        mask = _decay_mask(L, GAMMA)
        scores = jnp.einsum('bld,bmd->blm', qh, kh) * mask[None, :, :]
        return scores @ vh

    def _L0_ffn_ref(x, Wg, W1, W2):
        import jax, jax.numpy as jnp
        import numpy as np
        B, T, C = (2, 256, 128)
        E, H, TOPK = (8, 256, 2)
        b, t, c = x.shape
        xf = x.reshape(-1, c)
        n = xf.shape[0]
        scores = xf @ Wg
        topk_scores, topk_idx = jax.lax.top_k(scores, TOPK)
        topk_probs = jax.nn.softmax(topk_scores, axis=-1)
        combine = jnp.zeros((n, E), dtype=xf.dtype)
        combine = combine.at[jnp.arange(n)[:, None], topk_idx].set(topk_probs)
        h = jnp.einsum('nc,ech->enh', xf, W1)
        h = jax.nn.silu(h)
        eo = jnp.einsum('enh,ehc->enc', h, W2)
        y = jnp.einsum('ne,enc->nc', combine, eo)
        return y.reshape(b, t, c)

    def _L1_xattn_ref(y, Z, w1, b1, w2, b2, g1, beta1, g2, beta2, g3, beta3):
        import jax, jax.numpy as jnp
        import numpy as np
        B, S, D, DFF = (4, 256, 128, 512)
        EPS = 1e-05

        def layernorm(x, gamma, beta):
            mu = jnp.mean(x, axis=-1, keepdims=True)
            var = jnp.var(x, axis=-1, keepdims=True)
            return (x - mu) * jax.lax.rsqrt(var + EPS) * gamma + beta

        def attention(Q, K, V, causal):
            d_k = Q.shape[-1]
            scores = jnp.einsum('bqd,bkd->bqk', Q, K) / jnp.sqrt(jnp.asarray(d_k, Q.dtype))
            if causal:
                q_len, k_len = (scores.shape[-2], scores.shape[-1])
                mask = jnp.tril(jnp.ones((q_len, k_len), dtype=bool))
                scores = jnp.where(mask[None], scores, jnp.asarray(-jnp.inf, scores.dtype))
            w = jax.nn.softmax(scores, axis=-1)
            return jnp.einsum('bqk,bkd->bqd', w, V)
        sa = attention(y, y, y, causal=True)
        y = layernorm(y + sa, g1, beta1)
        ca = attention(y, Z, Z, causal=False)
        y = layernorm(y + ca, g2, beta2)
        h = jax.nn.relu(jnp.einsum('bsd,df->bsf', y, w1) + b1)
        ff = jnp.einsum('bsf,fd->bsd', h, w2) + b2
        y = layernorm(y + ff, g3, beta3)
        return y

    def _L1_ffn_ref(x, ln1_w, ln1_b, ln2_w, ln2_b, conv_w, attn_w, proj_w, router_w, expert_wv, expert_proj):
        import jax, jax.numpy as jnp
        import numpy as np
        EPS = 1e-05

        def _layernorm(x, w, b):
            mu = jnp.mean(x, axis=-1, keepdims=True)
            var = jnp.mean((x - mu) ** 2, axis=-1, keepdims=True)
            return (x - mu) * jax.lax.rsqrt(var + EPS) * w + b

        def _rope_tables(T, D, base=10000.0):
            inv_freq = 1.0 / base ** (jnp.arange(0, D, 2, dtype=jnp.float32) / D)
            t = jnp.arange(T, dtype=jnp.float32)
            freqs = jnp.einsum('i,j->ij', t, inv_freq)
            emb = jnp.concatenate([freqs, freqs], axis=-1)
            return (jnp.cos(emb), jnp.sin(emb))

        def _rotate_half(x):
            x1, x2 = (x[..., :x.shape[-1] // 2], x[..., x.shape[-1] // 2:])
            return jnp.concatenate([-x2, x1], axis=-1)

        def _attn(x, ln_w, ln_b, conv_w, attn_w, proj_w, n_head):
            B, T, C = x.shape
            D = C // n_head
            h = _layernorm(x, ln_w, ln_b)
            hc = jnp.transpose(h, (0, 2, 1))
            hc = jnp.pad(hc, ((0, 0), (0, 0), (2, 0)))
            hc = jax.lax.conv_general_dilated(hc, conv_w, window_strides=(1,), padding='VALID', dimension_numbers=('NCH', 'OIH', 'NCH'), feature_group_count=C)
            h = jnp.transpose(hc, (0, 2, 1))
            qkv = h @ attn_w
            q, k, v = jnp.split(qkv, 3, axis=-1)
            q = q.reshape(B, T, n_head, D)
            k = k.reshape(B, T, n_head, D)
            v = v.reshape(B, T, n_head, D)
            cos, sin = _rope_tables(T, D)
            cos = cos[None, :, None, :]
            sin = sin[None, :, None, :]
            q = q * cos + _rotate_half(q) * sin
            k = k * cos + _rotate_half(k) * sin
            scores = jnp.einsum('bqhd,bkhd->bhqk', q, k) / jnp.sqrt(jnp.float32(D))
            causal = jnp.tril(jnp.ones((T, T), dtype=bool))
            scores = jnp.where(causal, scores, jnp.float32(-1e+30))
            p = jax.nn.softmax(scores, axis=-1)
            y = jnp.einsum('bhqk,bkhd->bqhd', p, v).reshape(B, T, C)
            return y @ proj_w

        def _moe(x, ln_w, ln_b, router_w, expert_wv, expert_proj):
            h = _layernorm(x, ln_w, ln_b)
            logits = h @ router_w
            expert_idx = jnp.argmax(logits, axis=-1)
            E = router_w.shape[-1]
            out = jnp.zeros_like(x)
            for e in range(E):
                gv = h @ expert_wv[e]
                gate_raw, value = jnp.split(gv, 2, axis=-1)
                y = gate_raw * jax.nn.sigmoid(gate_raw) * value @ expert_proj[e]
                out = out + jnp.where((expert_idx == e)[..., None], y, 0.0)
            return out
        n_head = 16
        x = x + _attn(x, ln1_w, ln1_b, conv_w, attn_w, proj_w, n_head)
        x = x + _moe(x, ln2_w, ln2_b, router_w, expert_wv, expert_proj)
        return x
    x = x + _L0_xattn_ref(_layernorm(x, axis=-1), ctx_1024, ctx_1024, L0_xattn_Wq, L0_xattn_Wk, L0_xattn_Wv)
    x = x + _L0_ffn_ref(_layernorm(x, axis=-1), L0_ffn_Wg, L0_ffn_W1, L0_ffn_W2)
    x = x + _L1_xattn_ref(_layernorm(x, axis=-1), ctx_1024, L1_xattn_w1, L1_xattn_b1, L1_xattn_w2, L1_xattn_b2, L1_xattn_g1, L1_xattn_beta1, L1_xattn_g2, L1_xattn_beta2, L1_xattn_g3, L1_xattn_beta3)
    x = x + _L1_ffn_ref(_layernorm(x, axis=-1), L1_ffn_ln1_w, L1_ffn_ln1_b, L1_ffn_ln2_w, L1_ffn_ln2_b, L1_ffn_conv_w, L1_ffn_attn_w, L1_ffn_proj_w, L1_ffn_router_w, L1_ffn_expert_wv, L1_ffn_expert_proj)
    return x

_drawn_inputs = setup_inputs


def setup_inputs(seed=0):
    import zlib

    import numpy as np

    out = dict(_drawn_inputs(seed))
    spreads = {'L1_xattn_b1': (0.0, 0.8),
     'L1_xattn_b2': (0.0, 0.8),
     'L1_xattn_g1': (1.0, 0.6),
     'L1_xattn_beta1': (0.0, 0.8),
     'L1_xattn_g2': (1.0, 0.6),
     'L1_xattn_beta2': (0.0, 0.8),
     'L1_xattn_g3': (1.0, 0.6),
     'L1_xattn_beta3': (0.0, 0.8),
     'L1_ffn_ln1_w': (1.0, 0.6),
     'L1_ffn_ln1_b': (0.0, 0.8),
     'L1_ffn_ln2_w': (1.0, 0.6),
     'L1_ffn_ln2_b': (0.0, 0.8)}
    factors = {'L0_ffn_Wg': 8.0,
     'L0_ffn_W1': 8.0,
     'L0_ffn_W2': 8.0,
     'L1_xattn_w1': 8.0,
     'L1_xattn_w2': 8.0,
     'L1_ffn_conv_w': 8.0,
     'L1_ffn_attn_w': 8.0,
     'L1_ffn_proj_w': 8.0,
     'L1_ffn_router_w': 8.0,
     'L1_ffn_expert_wv': 8.0,
     'L1_ffn_expert_proj': 8.0}
    for name, (base, spread) in spreads.items():
        noise = np.random.default_rng([zlib.crc32(name.encode()), seed]).standard_normal(out[name].shape)
        drawn = base * np.exp(spread * noise) if base else spread * noise
        out[name] = jnp.asarray(drawn.astype(out[name].dtype))
    for name, factor in factors.items():
        out[name] = (out[name] * factor).astype(out[name].dtype)
    return out
```

```python
import concourse.bass as bass
from concourse import mybir
from contextlib import ExitStack

F32 = mybir.dt.float32
BF16 = mybir.dt.bfloat16
ALU = mybir.AluOpType
ACT = mybir.ActivationFunctionType
AX = mybir.AxisListType

P = 128
C = 128
BATCHES = 128
SEQ = 64
TOK = BATCHES * SEQ
RT = TOK // P
GR = 4
GT = GR * P
NG = TOK // GT
GB = GT // SEQ
EPS = 1e-5
MASKED = -1e30


def pipelined(eng, depth, step):
    head = depth + (NG - depth) % 2
    for s in range(head):
        step(s, s % 2)
    with eng.Fori(head, NG - 1, 2) as s:
        step(s, head % 2)
        step(s + 1, (head + 1) % 2)
    for s in range(NG, NG + depth):
        step(s, s % 2)


def live(t):
    return not isinstance(t, int) or 0 <= t < NG


def group(t):
    return bass.ds(t * GR, GR)


class Count:

    def __init__(self, sem, per=1):
        self.sem, self.per = sem, per

    def start(self, eng):
        eng.sem_inc(self.sem, 2 * self.per)

    def at(self, t, done=None):
        if isinstance(t, int) and t >= NG:
            t, done = NG - 1, self.per
        return (t + 2) * self.per + (self.per if done is None else done)


class Machine:

    def __init__(self, nc, ctx):
        self.nc, self.ctx = nc, ctx

    def sb(self, name, shape, dt=F32):
        return self.ctx.enter_context(self.nc.sbuf_tensor(name, shape, dt))

    def psum(self, name, shape=(P, 512), dt=F32):
        return self.ctx.enter_context(self.nc.psum_tensor(name, list(shape), dt))

    def sem(self, name):
        return self.ctx.enter_context(self.nc.semaphore(name))

    def count(self, name, per=1):
        return Count(self.sem(name), per)


def tiles(buf, r):
    return buf[:, r * P:(r + 1) * P]


def over_batches(table):
    return table.unsqueeze(1).broadcast_to([P, GB, SEQ])


def by_batch(buf):
    return buf.rearrange("p (b s) -> p b s", s=SEQ)


def newton_rsqrt(vec, link, var, guess, a, b, out):
    link(vec.scalar_tensor_tensor(a, var, EPS, guess, ALU.add, ALU.mult))
    link(vec.scalar_tensor_tensor(b, a, -0.5, guess, ALU.mult, ALU.mult))
    link(vec.scalar_tensor_tensor(out, b, 1.5, guess, ALU.add, ALU.mult))


def moments(vec, link, st, tmp, mean, var):
    total, apart, squares, spread = tmp
    vec.tensor_tensor(total, st[:, :, 1], st[:, :, 4], ALU.add)
    vec.tensor_tensor(apart, st[:, :, 1], st[:, :, 4], ALU.subtract)
    link(vec.tensor_tensor(squares, st[:, :, 2], st[:, :, 5], ALU.add))
    vec.tensor_scalar(mean, total, 0.5, None, ALU.mult)
    link(vec.scalar_tensor_tensor(spread, apart, 0.25, apart, ALU.mult, ALU.mult))
    link(vec.scalar_tensor_tensor(var, squares, 1.0 / C, spread, ALU.mult, ALU.add))


def constants(m, k, dram, phase):
    k.loads = []

    def load(name, shape, src):
        t = m.sb(name, shape)
        k.loads.append((t, src))
        return t

    def row(name, key):
        return load(name, [P, P], dram[key].unsqueeze(0).broadcast_to([P, P]))

    if phase == "A":
        k.wq = load("wq", [P, P], dram["L0_xattn_Wq"])
        k.wk = load("wk", [P, P], dram["L0_xattn_Wk"])
        k.wv = load("wv", [P, P], dram["L0_xattn_Wv"])
        k.rope_a = load("rope_a", [P, 4, SEQ], dram["rope_a"])
        k.decay = load("decay", [P, P], dram["decay"])
        k.wq_rot, k.wk_rot = m.sb("wq_rot", [P, P]), m.sb("wk_rot", [P, P])
    if phase == "B":
        k.gate_w = load("gate1_w", [P, 8], dram["L0_ffn_Wg"])
        k.up_w = load("up1_w", [P, 8, 256], dram["L0_ffn_W1"].rearrange("e c h -> c e h"))
        k.down_w = load("down1_w", [P, 8, 2, P], dram["L0_ffn_W2"].rearrange("e (k h) c -> h e k c", h=P))
    if phase == "C":
        k.w1 = load("w1", [P, 512], dram["L1_xattn_w1"])
        k.w2 = load("w2", [P, 4, P], dram["L1_xattn_w2"].rearrange("(k h) c -> h k c", h=P))
        k.b1 = load("b1", [P, 4], dram["L1_xattn_b1"].rearrange("(k h) -> h k", h=P))
        k.b2 = row("b2", "L1_xattn_b2")
        k.gamma = [row(f"gamma{i}", f"L1_xattn_g{i}") for i in (1, 2, 3)]
        k.beta = [row(f"beta{i}", f"L1_xattn_beta{i}") for i in (1, 2, 3)]
        k.masks = load("masks_c", [P, 2, GT], dram["masks"][:, 0:2, :])
        k.masks_bf = m.sb("masks_c_bf", [P, 2, GT], BF16)
    if phase == "D":
        k.ln1_w = load("ln1_w", [P, 1], dram["L1_ffn_ln1_w"].unsqueeze(1))
        k.ln1_b = load("ln1_b", [P, 1], dram["L1_ffn_ln1_b"].unsqueeze(1))
        k.conv = load("conv", [P, 3], dram["L1_ffn_conv_w"].rearrange("c a k -> c (a k)"))
        k.qkv = load("qkv", [P, 3, P], dram["L1_ffn_attn_w"].rearrange("c (j n) -> c j n", j=3))
        k.qk_rot = m.sb("qk_rot", [P, 2, P])
        k.rope_d = load("rope_d", [P, 2, SEQ], dram["rope_d"])
        k.proj = load("proj", [P, P], dram["L1_ffn_proj_w"])
        k.masks = load("masks_d", [P, 1, GT], dram["masks"][:, 2:3, :])
        k.masks_bf = m.sb("masks_d_bf", [P, 1, GT], BF16)
    if phase == "E":
        k.ln2_w = load("ln2_w", [P, 1], dram["L1_ffn_ln2_w"].unsqueeze(1))
        k.ln2_b = load("ln2_b", [P, 1], dram["L1_ffn_ln2_b"].unsqueeze(1))
        k.gate_w = load("gate2_w", [P, 4], dram["L1_ffn_router_w"])
        k.up_w = load("up2_w", [P, 4, 1024], dram["L1_ffn_expert_wv"].rearrange("e c h -> c e h"))
        k.down_w = load("down2_w", [P, 4, 4, P], dram["L1_ffn_expert_proj"].rearrange("e (k h) c -> h e k c", h=P))


def prepare(nc, k, phase):
    if phase == "A":
        for w, rot in ((k.wq, k.wq_rot), (k.wk, k.wk_rot)):
            src, dst = (z[:, :].rearrange("p (i two) -> p i two", two=2) for z in (w, rot))
            nc.scalar.mul(dst[:, :, 0], src[:, :, 1], -1.0)
            nc.scalar.copy(dst[:, :, 1], src[:, :, 0])
    if phase == "D":
        for j in range(2):
            src, dst = (z[:, j, :].rearrange("p (h two d) -> p h two d", two=2, d=4) for z in (k.qkv, k.qk_rot))
            nc.scalar.mul(dst[:, :, 0, :], src[:, :, 1, :], -1.0)
            nc.scalar.copy(dst[:, :, 1, :], src[:, :, 0, :])
    if phase in "CD":
        nc.scalar.copy(k.masks_bf[:, :, :], k.masks[:, :, :])


def load_phase(m, k, dram):
    nc = m.nc
    CH = 8
    x_loaded = [m.sem(f"x_loaded{n}") for n in range(RT // CH)]
    zeroed, made = m.sem("ident_zeroed"), m.sem("ident_made")
    xs = dram["x"].rearrange("(r two) s c -> (two s) r c", two=2)
    with nc.Block() as block:
        @block.sync
        def _(sp):
            for n, loaded in enumerate(x_loaded):
                sp.dma_start(k.x[:, n * CH:(n + 1) * CH, :], xs[:, n * CH:(n + 1) * CH, :]).then_inc(loaded, 16)

        @block.gpsimd
        def _(pool):
            nc.gpsimd.memset(k.ident[:, :], 0.0).then_inc(zeroed, 1)
            nc.gpsimd.memset(k.ident_bf[:, :], 0.0).then_inc(zeroed, 1)
            nc.gpsimd.memset(k.eps[:, :], EPS)
            pool.wait_ge(zeroed, 2)
            for t in (k.ident, k.ident_bf):
                nc.gpsimd.affine_select(out=t[:, :], in_=t[:, :], compare_op=ALU.not_equal, fill=1.0, base=0,
                                        pattern=[[-1, P]], channel_multiplier=1).then_inc(made, 1)

        @block.vector
        def _(dve):
            for r in range(RT):
                if r % CH == 0:
                    dve.wait_ge(x_loaded[r // CH], 16)
                nc.vector.bn_stats(k.stats[:, r, :], k.x[:, r, :])


def statistics(m, k, phase):
    nc = m.nc
    twice = phase == "D"
    steps, guessed, loaded = (m.sem(f"stats_{phase}_{n}") for n in ("steps", "guessed", "loaded"))
    st, w = k.stats, k.work
    with nc.Block() as block:
        @block.sync
        def _(sp):
            with nc.allow_non_contiguous_dma(reason="columns of small vectors"):
                for t, src in k.loads:
                    sp.dma_start(t[:], src).then_inc(loaded, 16)

        @block.vector
        def _(dve):
            n = [0]

            def link(ins):
                n[0] += 1
                ins.then_inc(steps, 1)
                dve.wait_ge(steps, n[0])

            v = nc.vector
            moments(v, link, st, [w[:, i, :] for i in range(4)], k.mean[:, :], w[:, 4, :])
            dve.wait_ge(guessed, 2)
            newton_rsqrt(v, link, w[:, 4, :], w[:, 6, :], w[:, 7, :], w[:, 8, :], k.rstd[:, :])
            if twice:
                link(v.tensor_tensor(w[:, 0, :], k.rstd[:, :], k.rstd[:, :], ALU.mult))
                link(v.tensor_tensor(w[:, 1, :], w[:, 0, :], w[:, 4, :], ALU.mult))
                dve.wait_ge(guessed, 4)
                newton_rsqrt(v, link, w[:, 1, :], w[:, 3, :], w[:, 7, :], w[:, 8, :], w[:, 9, :])
                link(v.tensor_tensor(k.rstd2[:, :], w[:, 9, :], k.rstd[:, :], ALU.mult))

        @block.scalar
        def _(act):
            if phase != "B" and phase != "E":
                nc.scalar.preload_act_table_set("natural_log_exp_and_others")
            act.wait_ge(steps, 3)
            nc.scalar.activation(w[:, 5, :], w[:, 4, :], ACT.Ln, bias=k.eps[:, 0:1]).then_inc(guessed, 1)
            act.wait_ge(guessed, 1)
            nc.scalar.activation(w[:, 6, :], w[:, 5, :], ACT.Exp, scale=-0.5).then_inc(guessed, 1)
            if twice:
                act.wait_ge(steps, 8)
                nc.scalar.activation(w[:, 2, :], w[:, 1, :], ACT.Ln, bias=k.eps[:, 0:1]).then_inc(guessed, 1)
                act.wait_ge(guessed, 3)
                nc.scalar.activation(w[:, 3, :], w[:, 2, :], ACT.Exp, scale=-0.5).then_inc(guessed, 1)
            act.wait_ge(loaded, 16 * len(k.loads))
            prepare(nc, k, phase)


def phase_a(m, k, dram):
    nc = m.nc
    ctx = dram["ctx_1024"].rearrange("(r two) s c -> (two s) r c", two=2)
    xn, z = m.sb("a_xn", [P, 2, GT]), m.sb("a_z", [P, 2, GT])
    xT, zT = m.sb("a_xT", [P, 2, GT]), m.sb("a_zT", [P, 2, GT])
    v = m.sb("a_v", [P, 2, GT])
    part = m.sb("a_part", [P, 4, GT])
    qk = m.sb("a_qk", [P, 2, 2, GT])
    pm = m.sb("a_pm", [P, 2, GT])
    bank_t, bank_v, bank_s, bank_o = k.bank[0], k.bank[5], k.bank[6], k.bank[7]
    bank_qk = k.bank[1:5]

    z_loaded = [m.sem(f"a_z_loaded{b}") for b in range(2)]
    normed = m.count("a_normed")
    turned = m.count("a_turned", 2)
    copied = m.count("a_copied", 2)
    projected = m.count("a_projected", 5)
    v_copied = m.count("a_v_copied")
    rotated = m.count("a_rotated", 4)
    summed = m.count("a_summed", 2)
    scored = m.count("a_scored")
    masked = m.count("a_masked")
    mixed = m.count("a_mixed")
    added = m.count("a_added")

    with nc.Block() as block:
        @block.sync
        def _(sp):
            def step(s, odd):
                sp.wait_ge(turned.sem, turned.at(s - 2))
                sp.dma_start(z[:, odd, :].rearrange("p (r c) -> p r c", c=C), ctx[:, group(s), :]
                             ).then_inc(z_loaded[odd], 16)
            pipelined(sp, 0, step)

        @block.vector
        def _(dve):
            for c in (normed, rotated, masked, added):
                c.start(dve)

            def norm(t, b):
                if not live(t):
                    return
                dve.wait_ge(turned.sem, turned.at(t - 2))
                for r in range(GR):
                    i = bass.ds(t * GR + r, 1)
                    last = nc.vector.tensor_scalar(tiles(xn[:, b, :], r), k.x[:, i, :], k.mean[:, i], k.rstd[:, i],
                                                   ALU.subtract, ALU.mult)
                last.then_inc(normed.sem, 1)

            def rotate(t, b):
                if not live(t):
                    return
                for j in range(4):
                    dve.wait_ge(projected.sem, projected.at(t, j + 1))
                    if j % 2 == 0:
                        dve.wait_ge(summed.sem, summed.at(t - 1, j // 2 + 1))
                    nc.vector.tensor_tensor(by_batch(part[:, j, :]), by_batch(bank_qk[j][:, :]),
                                            over_batches(k.rope_a[:, j, :]), ALU.mult).then_inc(rotated.sem, 1)

            def mask(t, b):
                if not live(t):
                    return
                dve.wait_ge(scored.sem, scored.at(t))
                dve.wait_ge(mixed.sem, mixed.at(t - 2))
                nc.vector.tensor_tensor(pm[:, b, :].rearrange("p (r q) -> p r q", q=P),
                                        bank_s[:, :].rearrange("p (r q) -> p r q", q=P),
                                        k.decay[:, :].unsqueeze(1).broadcast_to([P, GR, P]), ALU.mult
                                        ).then_inc(masked.sem, 1)

            def add(t, b):
                if not live(t):
                    return
                dve.wait_ge(mixed.sem, mixed.at(t))
                x = k.x[:, group(t), :]
                nc.vector.tensor_tensor(x, bank_o[:, :].rearrange("p (r c) -> p r c", c=C), x, ALU.add
                                        ).then_inc(added.sem, 1)
                dve.wait_ge(added.sem, added.at(t))
                for r in range(GR):
                    i = bass.ds(t * GR + r, 1)
                    nc.vector.bn_stats(k.stats[:, i, :], k.x[:, i, :])

            def step(s, odd):
                rotate(s - 2, odd)
                mask(s - 3, 1 - odd)
                norm(s, odd)
                add(s - 3, 1 - odd)
            pipelined(dve, 3, step)

        @block.tensor
        def _(pe):
            for c in (turned, projected, scored, mixed):
                c.start(pe)

            def turn(t, b):
                if not live(t):
                    return
                pe.wait_ge(normed.sem, normed.at(t))
                pe.wait_ge(copied.sem, copied.at(t - 1))
                for r in range(GR):
                    last = nc.tensor.transpose(tiles(bank_t, r), tiles(xn[:, b, :], r), k.ident[:, :])
                last.then_inc(turned.sem, 1)

            def turn_z(t, b):
                if not live(t):
                    return
                pe.wait_ge(z_loaded[b], (t - b) * 8 + 16)
                pe.wait_ge(copied.sem, copied.at(t, 1))
                for r in range(GR):
                    last = nc.tensor.transpose(tiles(bank_t, r), tiles(z[:, b, :], r), k.ident[:, :])
                last.then_inc(turned.sem, 1)

            def project(t, b):
                if not live(t):
                    return
                pe.wait_ge(copied.sem, copied.at(t))
                for j, (w, src) in enumerate(((k.wq, xT), (k.wq_rot, xT), (k.wk, zT), (k.wk_rot, zT))):
                    pe.wait_ge(rotated.sem, rotated.at(t - 1, j + 1))
                    nc.tensor.matmul(bank_qk[j][:, :], w[:, :], src[:, b, :], start=True, stop=True
                                     ).then_inc(projected.sem, 1)
                pe.wait_ge(v_copied.sem, v_copied.at(t - 1))
                for r in range(GR):
                    last = nc.tensor.matmul(tiles(bank_v, r), tiles(zT[:, b, :], r), k.wv[:, :], start=True, stop=True)
                last.then_inc(projected.sem, 1)

            def score(t, b):
                if not live(t):
                    return
                pe.wait_ge(summed.sem, summed.at(t))
                pe.wait_ge(masked.sem, masked.at(t - 1))
                for r in range(GR):
                    last = nc.tensor.matmul(tiles(bank_s, r), tiles(qk[:, b, 1, :], r), tiles(qk[:, b, 0, :], r),
                                            start=True, stop=True)
                last.then_inc(scored.sem, 1)

            def mix(t, b):
                if not live(t):
                    return
                pe.wait_ge(masked.sem, masked.at(t))
                pe.wait_ge(v_copied.sem, v_copied.at(t))
                pe.wait_ge(added.sem, added.at(t - 1))
                for r in range(GR):
                    last = nc.tensor.matmul(tiles(bank_o, r), tiles(pm[:, b, :], r), tiles(v[:, b, :], r),
                                            start=True, stop=True)
                last.then_inc(mixed.sem, 1)

            def step(s, odd):
                project(s - 2, odd)
                turn(s - 1, 1 - odd)
                score(s - 3, 1 - odd)
                turn_z(s - 1, 1 - odd)
                mix(s - 3, 1 - odd)
            pipelined(pe, 3, step)

        @block.scalar
        def _(act):
            for c in (copied, v_copied):
                c.start(act)

            def copy_turned(t, b):
                if not live(t):
                    return
                act.wait_ge(projected.sem, projected.at(t - 2))
                for j, dst in enumerate((xT, zT)):
                    act.wait_ge(turned.sem, turned.at(t, j + 1))
                    nc.scalar.copy(dst[:, b, :], bank_t[:, :]).then_inc(copied.sem, 1)

            def copy_v(t, b):
                if not live(t):
                    return
                act.wait_ge(projected.sem, projected.at(t))
                act.wait_ge(mixed.sem, mixed.at(t - 2))
                nc.scalar.copy(v[:, b, :], bank_v[:, :]).then_inc(v_copied.sem, 1)

            def step(s, odd):
                copy_v(s - 2, odd)
                copy_turned(s - 1, 1 - odd)
            pipelined(act, 2, step)

        @block.gpsimd
        def _(pool):
            summed.start(pool)

            def step(s, odd):
                for j in range(2):
                    pool.wait_ge(rotated.sem, rotated.at(s, 2 * j + 2))
                    pool.wait_ge(scored.sem, scored.at(s - 2))
                    nc.gpsimd.tensor_tensor(qk[:, odd, j, :], part[:, 2 * j, :], part[:, 2 * j + 1, :], ALU.add
                                            ).then_inc(summed.sem, 1)
            pipelined(pool, 0, step)


class LayerNorm:

    def __init__(self, m, k, name, steps, first):
        self.m, self.k, self.nc, self.first = m, k, m.nc, first
        self.rows = m.sb(name + "_rows", [P, GT])
        self.unit = m.sb(name + "_unit", [P, GT])
        self.scaled = m.sb(name + "_scaled", [P, GT])
        self.stats = m.sb(name + "_stats", [P, GR, 6])
        self.mean, self.var = m.sb(name + "_mean", [P, GR]), m.sb(name + "_var", [P, GR])
        self.tmp = m.sb(name + "_tmp", [P, 6, GR])
        self.done = m.count(name + "_done", steps)
        self.guessed = m.count(name + "_guessed", 2)
        self.affine = m.count(name + "_affine", 2)

    def take(self, dve, t):
        c, nc = self.done, self.nc
        for r in range(GR):
            last = nc.vector.bn_stats(self.stats[:, r, :], tiles(self.rows, r))
        last.then_inc(c.sem, 1)
        dve.wait_ge(c.sem, c.at(t, self.first + 1))
        n = [self.first + 1]

        def link(ins):
            n[0] += 1
            ins.then_inc(c.sem, 1)
            dve.wait_ge(c.sem, c.at(t, n[0]))

        moments(nc.vector, link, self.stats, [self.tmp[:, i, :] for i in range(2, 6)], self.mean[:, :], self.var[:, :])

    def guess(self, act, t):
        act.wait_ge(self.done.sem, self.done.at(t, self.first + 4))
        self.nc.scalar.activation(self.tmp[:, 0, :], self.var[:, :], ACT.Ln, bias=self.k.eps[:, 0:1]
                                  ).then_inc(self.guessed.sem, 1)
        act.wait_ge(self.guessed.sem, self.guessed.at(t, 1))
        self.nc.scalar.activation(self.tmp[:, 1, :], self.tmp[:, 0, :], ACT.Exp, scale=-0.5
                                  ).then_inc(self.guessed.sem, 1)

    def apply(self, dve, t):
        c, nc, w = self.done, self.nc, self.tmp
        n = [self.first + 4]

        def link(ins):
            n[0] += 1
            ins.then_inc(c.sem, 1)
            dve.wait_ge(c.sem, c.at(t, n[0]))

        dve.wait_ge(self.guessed.sem, self.guessed.at(t))
        newton_rsqrt(nc.vector, link, self.var[:, :], w[:, 1, :], w[:, 2, :], w[:, 3, :], w[:, 4, :])
        dve.wait_ge(self.affine.sem, self.affine.at(t - 1, 1))
        for r in range(GR):
            last = nc.vector.tensor_scalar(tiles(self.unit, r), tiles(self.rows, r), self.mean[:, r:r + 1],
                                           w[:, 4, r:r + 1], ALU.subtract, ALU.mult)
        last.then_inc(c.sem, 1)

    def scale_shift(self, pool, t, out, gamma, beta, free):
        def by_tile(a):
            return a.rearrange("p (r c) -> p r c", c=C)

        def row(a):
            return a[:, :].unsqueeze(1).broadcast_to([P, GR, C])

        a = self.affine
        pool.wait_ge(self.done.sem, self.done.at(t))
        self.nc.gpsimd.tensor_tensor(by_tile(self.scaled[:, :]), by_tile(self.unit[:, :]), row(gamma), ALU.mult
                                     ).then_inc(a.sem, 1)
        pool.wait_ge(a.sem, a.at(t, 1))
        free()
        self.nc.gpsimd.tensor_tensor(by_tile(out), by_tile(self.scaled[:, :]), row(beta), ALU.add).then_inc(a.sem, 1)


class Attention:

    SCALE = float(C) ** -0.5

    def __init__(self, m, k, name, mask, bank_s, bank_pt, bank_o):
        self.nc, self.k, self.mask = m.nc, k, mask
        self.bank_s, self.bank_pt, self.bank_o = bank_s, bank_pt, bank_o
        self.p, self.pT = m.sb(name + "_p", [P, GT]), m.sb(name + "_pT", [P, GT])
        self.top = m.sb(name + "_top", [P, 2, GR])
        self.sums = m.sb(name + "_sums", [P, GR])
        self.inverse = m.sb(name + "_inverse", [P, GR])
        self.scored = m.count(name + "_scored")
        self.topped = m.count(name + "_topped", 2)
        self.powered = m.count(name + "_powered")
        self.turned = m.count(name + "_turned")
        self.copied = m.count(name + "_copied")
        self.mixed = m.count(name + "_mixed")

    def score(self, pe, t, qT, kT):
        nc = self.nc
        pe.wait_ge(self.powered.sem, self.powered.at(t - 1))
        nc.tensor.matmul(self.bank_s[:, :], self.k.ident_bf[:, :], self.mask, start=True, stop=False)
        for r in range(GR):
            last = nc.tensor.matmul(tiles(self.bank_s, r), tiles(qT, r), tiles(kT, r), start=False, stop=r == GR - 1)
        last.then_inc(self.scored.sem, 1)

    def find_top(self, dve, t):
        nc, c = self.nc, self.topped
        dve.wait_ge(self.scored.sem, self.scored.at(t))
        nc.vector.tensor_reduce(self.top[:, 0, :], self.bank_s[:, :].rearrange("p (r q) -> p r q", q=P), AX.X, ALU.max
                                ).then_inc(c.sem, 1)
        dve.wait_ge(c.sem, c.at(t, 1))
        dve.wait_ge(self.powered.sem, self.powered.at(t - 1))
        nc.vector.tensor_scalar(self.top[:, 1, :], self.top[:, 0, :], -self.SCALE, None, ALU.mult).then_inc(c.sem, 1)

    def power(self, act, t):
        nc = self.nc
        act.wait_ge(self.topped.sem, self.topped.at(t))
        act.wait_ge(self.turned.sem, self.turned.at(t - 1))
        for r in range(GR):
            last = nc.scalar.activation(tiles(self.p, r), tiles(self.bank_s, r), ACT.Exp, bias=self.top[:, 1, r:r + 1],
                                        scale=self.SCALE, accum_out=self.sums[:, r:r + 1])
        last.then_inc(self.powered.sem, 1)

    def turn(self, pe, t, bank_free):
        pe.wait_ge(self.powered.sem, self.powered.at(t))
        bank_free()
        for r in range(GR):
            last = self.nc.tensor.transpose(tiles(self.bank_pt, r), tiles(self.p, r), self.k.ident[:, :])
        last.then_inc(self.turned.sem, 1)

    def copy(self, act, t):
        act.wait_ge(self.turned.sem, self.turned.at(t))
        act.wait_ge(self.mixed.sem, self.mixed.at(t - 1))
        self.nc.scalar.copy(self.pT[:, :], self.bank_pt[:, :]).then_inc(self.copied.sem, 1)

    def mix(self, pe, t, v, bank_free):
        pe.wait_ge(self.copied.sem, self.copied.at(t))
        bank_free()
        for r in range(GR):
            last = self.nc.tensor.matmul(tiles(self.bank_o, r), tiles(self.pT, r), tiles(v, r), start=True, stop=True)
        last.then_inc(self.mixed.sem, 1)

    def finish(self, dve, t, rows, residual, count):
        nc = self.nc
        dve.wait_ge(self.mixed.sem, self.mixed.at(t))
        nc.vector.reciprocal(self.inverse[:, :], self.sums[:, :]).then_inc(count.sem, 1)
        dve.wait_ge(count.sem, count.at(t, 1))
        for r in range(GR):
            last = nc.vector.scalar_tensor_tensor(tiles(rows, r), tiles(self.bank_o, r), self.inverse[:, r:r + 1],
                                                  tiles(residual, r), ALU.mult, ALU.add)
        last.then_inc(count.sem, 1)
        dve.wait_ge(count.sem, count.at(t, 2))


def phase_c(m, k, dram):
    nc = m.nc
    ctx = dram["ctx_1024"].rearrange("(r two) s c -> (two s) r c", two=2)
    NK = 4
    y, z, y1, y2 = (m.sb("c_" + n, [P, 2, GT]) for n in ("y", "z", "y1", "y2"))
    yT, zT, y1T, y2T = (m.sb("c_" + n, [P, GT]) for n in ("yT", "zT", "y1T", "y2T"))
    hidden = m.sb("c_hidden", [P, NK, GT])
    y2b = m.sb("c_y2b", [P, GT])
    y3 = m.sb("c_y3", [P, GT])
    bank_t, bank_t2, bank_sa, bank_sc, bank_pt, bank_o, bank_h, bank_f = k.bank

    own = Attention(m, k, "c_self", k.masks_bf[:, 0, :], bank_sa, bank_pt, bank_o)
    cross = Attention(m, k, "c_cross", k.masks_bf[:, 1, :], bank_sc, bank_pt, bank_o)
    ln1 = LayerNorm(m, k, "c_ln1", 10, 2)
    ln2 = LayerNorm(m, k, "c_ln2", 10, 2)
    ln3 = LayerNorm(m, k, "c_ln3", 9, 1)
    z_loaded = [m.sem(f"c_z_loaded{b}") for b in range(2)]
    normed = m.count("c_normed")
    turned = {n: m.count("c_turned_" + n) for n in ("y", "z", "y1", "y2")}
    copied = {n: m.count("c_copied_" + n) for n in ("y", "z", "y1", "y2")}
    raised = m.count("c_raised", NK)
    bent = m.count("c_bent", NK)
    lowered = m.count("c_lowered")
    biased = m.count("c_biased")
    added = m.count("c_added")

    with nc.Block() as block:
        @block.sync
        def _(sp):
            def step(s, odd):
                sp.wait_ge(cross.mixed.sem, cross.mixed.at(s - 2))
                sp.dma_start(z[:, odd, :].rearrange("p (r c) -> p r c", c=C), ctx[:, group(s), :]
                             ).then_inc(z_loaded[odd], 16)
            pipelined(sp, 0, step)

        @block.vector
        def _(dve):
            for c in (normed, own.topped, cross.topped, ln1.done, ln2.done, ln3.done):
                c.start(dve)

            def step(s, odd):
                even = 1 - odd
                if live(s - 4):
                    t = s - 4
                    dve.wait_ge(lowered.sem, lowered.at(t))
                    dve.wait_ge(biased.sem, biased.at(t))
                    nc.vector.tensor_tensor(ln3.rows[:, :], bank_f[:, :], y2b[:, :], ALU.add).then_inc(ln3.done.sem, 1)
                    dve.wait_ge(ln3.done.sem, ln3.done.at(t, 1))
                    ln3.take(dve, t)
                if live(s - 1):
                    own.find_top(dve, s - 1)
                if live(s - 4):
                    ln3.apply(dve, s - 4)
                if live(s - 2):
                    cross.find_top(dve, s - 2)
                if live(s):
                    dve.wait_ge(own.mixed.sem, own.mixed.at(s - 2))
                    for r in range(GR):
                        i = bass.ds(s * GR + r, 1)
                        last = nc.vector.tensor_scalar(tiles(y[:, odd, :], r), k.x[:, i, :], k.mean[:, i],
                                                       k.rstd[:, i], ALU.subtract, ALU.mult)
                    last.then_inc(normed.sem, 1)
                if live(s - 1):
                    own.finish(dve, s - 1, ln1.rows, y[:, even, :], ln1.done)
                    ln1.take(dve, s - 1)
                    ln1.apply(dve, s - 1)
                if live(s - 2):
                    cross.finish(dve, s - 2, ln2.rows, y1[:, odd, :], ln2.done)
                    ln2.take(dve, s - 2)
                if live(s - 4):
                    dve.wait_ge(added.sem, added.at(s - 4))
                    for r in range(GR):
                        i = bass.ds((s - 4) * GR + r, 1)
                        nc.vector.bn_stats(k.stats[:, i, :], k.x[:, i, :])
                if live(s - 2):
                    ln2.apply(dve, s - 2)
            pipelined(dve, 4, step)

        @block.tensor
        def _(pe):
            for c in (*turned.values(), own.scored, own.turned, own.mixed, cross.scored, cross.turned, cross.mixed,
                      raised, lowered):
                c.start(pe)

            def turn(name, t, src, bank, other, other_t):
                pe.wait_ge(copied[other].sem, copied[other].at(other_t))
                for r in range(GR):
                    last = nc.tensor.transpose(tiles(bank, r), tiles(src, r), k.ident[:, :])
                last.then_inc(turned[name].sem, 1)

            def up(t, j):
                if not live(t):
                    return
                pe.wait_ge(copied["y2"].sem, copied["y2"].at(t))
                pe.wait_ge(bent.sem, bent.at(t, j))
                nc.tensor.matmul(bank_h[:, :], k.w1[:, j * P:(j + 1) * P], y2T[:, :], start=True, stop=True
                                 ).then_inc(raised.sem, 1)

            def step(s, odd):
                even = 1 - odd
                if live(s - 1):
                    pe.wait_ge(normed.sem, normed.at(s - 1))
                    turn("y", s - 1, y[:, even, :], bank_t, "y1", s - 3)
                if live(s - 2):
                    pe.wait_ge(z_loaded[odd], (s - 2 - odd) * 8 + 16)
                    turn("z", s - 2, z[:, odd, :], bank_t2, "y2", s - 4)
                if live(s - 1):
                    pe.wait_ge(copied["y"].sem, copied["y"].at(s - 1))
                    own.score(pe, s - 1, yT, yT)
                if live(s - 2):
                    pe.wait_ge(ln1.affine.sem, ln1.affine.at(s - 2))
                    turn("y1", s - 2, y1[:, odd, :], bank_t, "y", s - 1)
                    pe.wait_ge(copied["z"].sem, copied["z"].at(s - 2))
                    pe.wait_ge(copied["y1"].sem, copied["y1"].at(s - 2))
                    cross.score(pe, s - 2, y1T, zT)
                if live(s - 3):
                    pe.wait_ge(ln2.affine.sem, ln2.affine.at(s - 3))
                    turn("y2", s - 3, y2[:, even, :], bank_t2, "z", s - 2)
                up(s - 3, 0)
                if live(s - 1):
                    own.turn(pe, s - 1, lambda: pe.wait_ge(cross.copied.sem, cross.copied.at(s - 3)))
                up(s - 3, 1)
                if live(s - 1):
                    own.mix(pe, s - 1, y[:, even, :], lambda: pe.wait_ge(ln2.done.sem, ln2.done.at(s - 3, 2)))
                if live(s - 2):
                    cross.turn(pe, s - 2, lambda: pe.wait_ge(own.copied.sem, own.copied.at(s - 1)))
                up(s - 3, 2)
                if live(s - 2):
                    cross.mix(pe, s - 2, z[:, odd, :], lambda: pe.wait_ge(ln1.done.sem, ln1.done.at(s - 1, 2)))
                up(s - 3, 3)
                if live(s - 3):
                    pe.wait_ge(ln3.done.sem, ln3.done.at(s - 4, 1))
                    for j in range(NK):
                        pe.wait_ge(bent.sem, bent.at(s - 3, j + 1))
                        for r in range(GR):
                            last = nc.tensor.matmul(tiles(bank_f, r), tiles(hidden[:, j, :], r), k.w2[:, j, :],
                                                    start=j == 0 and r == 0, stop=j == NK - 1,
                                                    skip_group_check=True)
                    last.then_inc(lowered.sem, 1)
            pipelined(pe, 3, step)

        @block.scalar
        def _(act):
            for c in (*copied.values(), own.powered, own.copied, cross.powered, cross.copied, bent,
                      ln1.guessed, ln2.guessed, ln3.guessed):
                c.start(act)

            def copy(name, t, dst, bank, reader, count):
                if not live(t):
                    return
                act.wait_ge(turned[name].sem, turned[name].at(t))
                act.wait_ge(reader.sem, count)
                nc.scalar.copy(dst[:, :], bank[:, :]).then_inc(copied[name].sem, 1)

            def relu(t, j):
                if not live(t):
                    return
                act.wait_ge(raised.sem, raised.at(t, j + 1))
                act.wait_ge(lowered.sem, lowered.at(t - 1))
                nc.scalar.activation(hidden[:, j, :], bank_h[:, :], ACT.Relu, bias=k.b1[:, j:j + 1]
                                     ).then_inc(bent.sem, 1)

            def step(s, odd):
                copy("y", s - 1, yT, bank_t, own.scored, own.scored.at(s - 2))
                copy("z", s - 2, zT, bank_t2, cross.scored, cross.scored.at(s - 3))
                copy("y1", s - 2, y1T, bank_t, cross.scored, cross.scored.at(s - 3))
                if live(s - 4):
                    ln3.guess(act, s - 4)
                if live(s - 1):
                    own.power(act, s - 1)
                copy("y2", s - 3, y2T, bank_t2, raised, raised.at(s - 4))
                relu(s - 3, 0)
                if live(s - 1):
                    own.copy(act, s - 1)
                if live(s - 2):
                    cross.power(act, s - 2)
                relu(s - 3, 1)
                if live(s - 1):
                    ln1.guess(act, s - 1)
                if live(s - 2):
                    cross.copy(act, s - 2)
                relu(s - 3, 2)
                if live(s - 2):
                    ln2.guess(act, s - 2)
                relu(s - 3, 3)
            pipelined(act, 4, step)

        @block.gpsimd
        def _(pool):
            for c in (ln1.affine, ln2.affine, ln3.affine, biased, added):
                c.start(pool)

            def step(s, odd):
                even = 1 - odd
                if live(s - 4):
                    t = s - 4
                    ln3.scale_shift(pool, t, y3[:, :], k.gamma[2], k.beta[2], lambda: None)
                    pool.wait_ge(ln3.affine.sem, ln3.affine.at(t))
                    x = k.x[:, group(t), :]
                    nc.gpsimd.tensor_tensor(x, x, y3[:, :].rearrange("p (r c) -> p r c", c=C), ALU.add
                                            ).then_inc(added.sem, 1)
                if live(s - 3):
                    t = s - 3
                    pool.wait_ge(ln2.affine.sem, ln2.affine.at(t))
                    pool.wait_ge(ln3.done.sem, ln3.done.at(t - 1, 1))
                    nc.gpsimd.tensor_tensor(y2b[:, :].rearrange("p (r c) -> p r c", c=C),
                                            y2[:, even, :].rearrange("p (r c) -> p r c", c=C),
                                            k.b2[:, :].unsqueeze(1).broadcast_to([P, GR, C]), ALU.add
                                            ).then_inc(biased.sem, 1)
                if live(s - 1):
                    ln1.scale_shift(pool, s - 1, y1[:, even, :], k.gamma[0], k.beta[0],
                                    lambda: pool.wait_ge(ln2.done.sem, ln2.done.at(s - 3, 2)))
                if live(s - 2):
                    ln2.scale_shift(pool, s - 2, y2[:, odd, :], k.gamma[1], k.beta[1],
                                    lambda: pool.wait_ge(turned["y2"].sem, turned["y2"].at(s - 4)))
            pipelined(pool, 4, step)


def phase_d(m, k, dram):
    nc = m.nc
    HEADS, HD = 16, 8
    UNITS = 2 * GR
    PAIRS = HEADS // 2
    VW = 2 * HD + 2
    SCALE = float(HD) ** -0.5
    xn, hT, cT = m.sb("d_xn", [P, GT]), m.sb("d_hT", [P, GT]), m.sb("d_cT", [P, GT])
    cTT = m.sb("d_cTT", [P, GB * P])
    part = m.sb("d_part", [P, 4, GT])
    kT, qT = m.sb("d_kT", [P, GT]), m.sb("d_qT", [P, 2, GT])
    keys = m.sb("d_keys", [P, 2, GB, HEADS, SEQ])
    vals = m.sb("d_vals", [P, 2, GB, PAIRS, VW])
    prob, probT = m.sb("d_prob", [P, 2, 512]), m.sb("d_probT", [P, 2, 512])
    top = m.sb("d_top", [P, 2, 8])
    inverse = m.sb("d_inverse", [P, PAIRS, 2])
    o, oT, u = m.sb("d_o", [P, GT]), m.sb("d_oT", [P, GT]), m.sb("d_u", [P, GT])
    bank_t, bank_l, bank_r, bank_s, bank_pt, bank_o = k.bank[0], k.bank[1], k.bank[2], k.bank[3:5], k.bank[5:7], k.bank[7]

    blank = m.sem("d_blank")
    normed = m.count("d_normed")
    turned = m.count("d_turned")
    h_copied = m.count("d_h_copied")
    conved = m.count("d_conved", 3)
    doubled = m.count("d_doubled")
    projected = m.count("d_projected", 5)
    rotated = m.count("d_rotated", 4)
    summed = m.count("d_summed", 2)
    keys_in = [m.sem(f"d_keys_in{b}") for b in range(2)]
    v_copied = m.count("d_v_copied")
    scored = m.count("d_scored", UNITS)
    topped = m.count("d_topped", 2 * UNITS)
    powered = m.count("d_powered", UNITS)
    p_turned = m.count("d_p_turned", UNITS)
    p_copied = m.count("d_p_copied", UNITS)
    mixed = m.count("d_mixed", UNITS)
    divided = m.count("d_divided", 2 * GR)
    o_turned = m.count("d_o_turned")
    o_copied = m.count("d_o_copied")
    out = m.count("d_out")
    updated = m.count("d_updated", 2)
    added = m.count("d_added")

    with nc.Block() as block:
        @block.sync
        def _(sp):
            sp.wait_ge(blank, 3)

            def step(s, odd):
                t, b = s, odd
                sp.wait_ge(summed.sem, summed.at(t, 1))
                sp.wait_ge(scored.sem, scored.at(t - 2))
                for h in range(HEADS):
                    rows = slice(h * HD, (h + 1) * HD)
                    sp.dma_start(keys[rows, b, :, h, :], by_batch(kT[rows, :])).then_inc(keys_in[b], 16)
            pipelined(sp, 0, step)

        @block.vector
        def _(dve):
            nc.vector.memset(vals[:], 0.0).then_inc(blank, 1)
            for c in (normed, conved, rotated, topped, divided, updated):
                c.start(dve)

            def norm(t):
                if not live(t):
                    return
                dve.wait_ge(turned.sem, turned.at(t - 1))
                for r in range(GR):
                    i = bass.ds(t * GR + r, 1)
                    last = nc.vector.tensor_scalar(tiles(xn, r), k.x[:, i, :], k.mean[:, i], k.rstd2[:, i],
                                                   ALU.subtract, ALU.mult)
                last.then_inc(normed.sem, 1)

            def convolve(t):
                if not live(t):
                    return
                h, c = by_batch(hT[:, :]), by_batch(cT[:, :])
                dve.wait_ge(h_copied.sem, h_copied.at(t))
                dve.wait_ge(projected.sem, projected.at(t - 1, 4))
                dve.wait_ge(doubled.sem, doubled.at(t - 1))
                nc.vector.tensor_scalar(c, h, k.conv[:, 2:3], None, ALU.mult).then_inc(conved.sem, 1)
                for lag in (1, 2):
                    dve.wait_ge(conved.sem, conved.at(t, lag))
                    nc.vector.scalar_tensor_tensor(c[:, :, lag:], h[:, :, :SEQ - lag], k.conv[:, 2 - lag:3 - lag],
                                                   c[:, :, lag:], ALU.mult, ALU.add).then_inc(conved.sem, 1)

            def rotate(t, first):
                if not live(t):
                    return
                for j in (first, first + 1):
                    dve.wait_ge(projected.sem, projected.at(t, j + 1))
                    dve.wait_ge(summed.sem, summed.at(t - 1, first // 2 + 1))
                    nc.vector.tensor_tensor(by_batch(part[:, j, :]), by_batch((bank_l, bank_r)[j % 2][:, :]),
                                            over_batches(k.rope_d[:, j % 2, :]), ALU.mult).then_inc(rotated.sem, 1)

            def shift(t, n):
                if not live(t):
                    return
                scores = bank_s[n % 2][:, :].rearrange("p (h s) -> p h s", s=SEQ)
                dve.wait_ge(scored.sem, scored.at(t, n + 1))
                nc.vector.tensor_reduce(top[:, n % 2, :], scores, AX.X, ALU.max).then_inc(topped.sem, 1)
                dve.wait_ge(topped.sem, topped.at(t, 2 * n + 1))
                dve.wait_ge(p_turned.sem, p_turned.at(t, n - 1))
                nc.vector.tensor_tensor(prob[:, n % 2, :].rearrange("p (h s) -> p h s", s=SEQ), scores,
                                        top[:, n % 2, :].unsqueeze(2).broadcast_to([P, 8, SEQ]), ALU.subtract
                                        ).then_inc(topped.sem, 1)

            def divide(t, r):
                if not live(t):
                    return
                got = bank_o[:, 0:PAIRS * VW].rearrange("p (j w) -> p j w", w=VW)
                dve.wait_ge(mixed.sem, mixed.at(t, 2 * r + 2))
                nc.vector.reciprocal(inverse[:, :, :], got[:, :, 2 * HD:]).then_inc(divided.sem, 1)
                dve.wait_ge(divided.sem, divided.at(t, 2 * r + 1))
                if r == 0:
                    dve.wait_ge(o_turned.sem, o_turned.at(t - 1))
                nc.vector.tensor_tensor(tiles(o, r).rearrange("p (j e d) -> p j e d", j=PAIRS, e=2),
                                        got[:, :, 0:2 * HD].rearrange("p j (e d) -> p j e d", e=2),
                                        inverse[:, :, :].unsqueeze(3).broadcast_to([P, PAIRS, 2, HD]), ALU.mult
                                        ).then_inc(divided.sem, 1)

            def unit_rows(t):
                if not live(t):
                    return
                for r in range(GR):
                    i = bass.ds(t * GR + r, 1)
                    last = nc.vector.tensor_scalar(tiles(u, r), k.x[:, i, :], k.mean[:, i], k.rstd[:, i],
                                                   ALU.subtract, ALU.mult)
                last.then_inc(updated.sem, 1)

            def update(t):
                if not live(t):
                    return
                dve.wait_ge(out.sem, out.at(t))
                dve.wait_ge(updated.sem, updated.at(t, 1))
                dst = k.u[:, group(t), :]
                nc.vector.tensor_tensor(dst, bank_t[:, :].rearrange("p (r c) -> p r c", c=C),
                                        u[:, :].rearrange("p (r c) -> p r c", c=C), ALU.add).then_inc(updated.sem, 1)

            def take(t):
                if not live(t):
                    return
                dve.wait_ge(updated.sem, updated.at(t))
                for r in range(GR):
                    i = bass.ds(t * GR + r, 1)
                    nc.vector.bn_stats(k.stats[:, i, :], k.u[:, i, :])

            def step(s, odd):
                t = s - 2
                shift(t, 0)
                divide(s - 3, 3)
                convolve(s - 1)
                shift(t, 1)
                unit_rows(s - 3)
                shift(t, 2)
                update(s - 3)
                rotate(s - 1, 0)
                shift(t, 3)
                divide(t, 0)
                shift(t, 4)
                norm(s)
                shift(t, 5)
                divide(t, 1)
                rotate(s - 1, 2)
                shift(t, 6)
                take(s - 3)
                shift(t, 7)
                divide(t, 2)
            pipelined(dve, 3, step)

        @block.tensor
        def _(pe):
            for c in (turned, projected, scored, p_turned, mixed, o_turned, out):
                c.start(pe)
            pe.wait_ge(blank, 3)

            def turn(t):
                if not live(t):
                    return
                pe.wait_ge(normed.sem, normed.at(t))
                pe.wait_ge(updated.sem, updated.at(t - 3))
                for r in range(GR):
                    last = nc.tensor.transpose(tiles(bank_t, r), tiles(xn, r), k.ident[:, :])
                last.then_inc(turned.sem, 1)

            def project(t, first):
                if not live(t):
                    return
                j = 1 - first // 2
                if first == 0:
                    pe.wait_ge(conved.sem, conved.at(t))
                    pe.wait_ge(v_copied.sem, v_copied.at(t - 1))
                else:
                    pe.wait_ge(rotated.sem, rotated.at(t, 2))
                nc.tensor.matmul(bank_l[:, :], k.qkv[:, j, :], cT[:, :], start=True, stop=True).then_inc(projected.sem, 1)
                nc.tensor.matmul(bank_r[:, :], k.qk_rot[:, j, :], cT[:, :], start=True, stop=True
                                 ).then_inc(projected.sem, 1)

            def values(t):
                if not live(t):
                    return
                pe.wait_ge(rotated.sem, rotated.at(t))
                pe.wait_ge(doubled.sem, doubled.at(t))
                for i in range(GB):
                    bank = (bank_l, bank_r)[i // 4]
                    last = nc.tensor.matmul(tiles(bank, i % 4), tiles(cTT, i), k.qkv[:, 2, :], start=True, stop=True)
                last.then_inc(projected.sem, 1)

            def score(t, b, n):
                if not live(t):
                    return
                r, half = n // 2, n % 2
                bank = bank_s[n % 2]
                if n == 0:
                    pe.wait_ge(summed.sem, summed.at(t))
                    pe.wait_ge(keys_in[b], (t - b) * 8 * HEADS + 16 * HEADS)
                pe.wait_ge(topped.sem, topped.at(t, 2 * n - 2))
                nc.tensor.matmul(bank[:, :], k.ident_bf[:, :], k.masks_bf[:, 0, :], start=True, stop=False,
                                 skip_group_check=True)
                for e in range(2):
                    i = 2 * r + e
                    last = nc.tensor.matmul(bank[e * SEQ:(e + 1) * SEQ, :], qT[:, b, i * SEQ:(i + 1) * SEQ],
                                            keys[:, b, i, half * 8:half * 8 + 8, :], start=False, stop=True,
                                            tile_position=(0, e * SEQ), skip_group_check=True)
                last.then_inc(scored.sem, 1)

            def turn_prob(t, n):
                if not live(t):
                    return
                pe.wait_ge(powered.sem, powered.at(t, n + 1))
                pe.wait_ge(p_copied.sem, p_copied.at(t, n - 1))
                for j in range(4):
                    last = nc.tensor.transpose(tiles(bank_pt[n % 2], j), tiles(prob[:, n % 2, :], j), k.ident[:, :])
                last.then_inc(p_turned.sem, 1)

            def mix(t, b, n):
                if not live(t):
                    return
                r, half = n // 2, n % 2
                pe.wait_ge(p_copied.sem, p_copied.at(t, n + 1))
                if n == 0:
                    pe.wait_ge(v_copied.sem, v_copied.at(t))
                if half == 0:
                    pe.wait_ge(divided.sem, divided.at(t, 2 * r))
                for j in range(4):
                    pair = half * 4 + j
                    for e in range(2):
                        last = nc.tensor.matmul(bank_o[e * SEQ:(e + 1) * SEQ, pair * VW:(pair + 1) * VW],
                                                probT[:, n % 2, j * P + e * SEQ:j * P + (e + 1) * SEQ],
                                                vals[:, b, 2 * r + e, pair, :], start=True, stop=True,
                                                tile_position=(0, e * SEQ))
                last.then_inc(mixed.sem, 1)

            def turn_out(t):
                if not live(t):
                    return
                pe.wait_ge(divided.sem, divided.at(t))
                pe.wait_ge(h_copied.sem, h_copied.at(t + 2))
                for r in range(GR):
                    last = nc.tensor.transpose(tiles(bank_t, r), tiles(o, r), k.ident[:, :])
                last.then_inc(o_turned.sem, 1)

            def project_out(t):
                if not live(t):
                    return
                pe.wait_ge(o_copied.sem, o_copied.at(t))
                for r in range(GR):
                    last = nc.tensor.matmul(tiles(bank_t, r), tiles(oT, r), k.proj[:, :], start=True, stop=True)
                last.then_inc(out.sem, 1)

            def step(s, odd):
                t, b = s - 2, odd
                score(t, b, 0)
                turn(s - 1)
                score(t, b, 1)
                turn_out(s - 3)
                turn_prob(t, 0)
                for n in range(2, UNITS):
                    score(t, b, n)
                    if n == 2:
                        project_out(s - 3)
                    mix(t, b, n - 2)
                    if n == 3:
                        project(s - 1, 0)
                    if n == 5:
                        project(s - 1, 2)
                    turn_prob(t, n - 1)
                mix(t, b, UNITS - 2)
                values(s - 1)
                turn_prob(t, UNITS - 1)
                mix(t, b, UNITS - 1)
            pipelined(pe, 3, step)

        @block.scalar
        def _(act):
            for c in (h_copied, doubled, v_copied, powered, p_copied, o_copied):
                c.start(act)
            act.wait_ge(blank, 3)

            def copy_h(t):
                if not live(t):
                    return
                act.wait_ge(turned.sem, turned.at(t))
                act.wait_ge(conved.sem, conved.at(t - 1))
                nc.scalar.activation(hT[:, :], bank_t[:, :], ACT.Identity, bias=k.ln1_b[:, 0:1], scale=k.ln1_w[:, 0:1]
                                     ).then_inc(h_copied.sem, 1)

            def double(t):
                if not live(t):
                    return
                act.wait_ge(conved.sem, conved.at(t))
                act.wait_ge(projected.sem, projected.at(t - 1))
                nc.scalar.copy(cTT[:, :].rearrange("p (b e s) -> p b e s", e=2, s=SEQ),
                               by_batch(cT[:, :]).unsqueeze(2).broadcast_to([P, GB, 2, SEQ])).then_inc(doubled.sem, 1)

            def copy_v(t, b):
                if not live(t):
                    return
                act.wait_ge(projected.sem, projected.at(t))
                act.wait_ge(mixed.sem, mixed.at(t - 2))
                for n, bank in enumerate((bank_l, bank_r)):
                    for e in range(2):
                        rows = slice(e * SEQ, (e + 1) * SEQ)
                        got = bank[rows, :].rearrange("p (i j e d) -> p i j e d", i=4, j=PAIRS, e=2)
                        last = nc.scalar.copy(vals[rows, b, 4 * n:4 * n + 4, :, e * HD:(e + 1) * HD], got[:, :, :, e, :])
                last.then_inc(v_copied.sem, 1)

            def power(t, n):
                if not live(t):
                    return
                act.wait_ge(topped.sem, topped.at(t, 2 * n + 2))
                nc.scalar.activation(prob[:, n % 2, :], prob[:, n % 2, :], ACT.Exp, scale=SCALE).then_inc(powered.sem, 1)

            def copy_prob(t, n):
                if not live(t):
                    return
                act.wait_ge(p_turned.sem, p_turned.at(t, n + 1))
                act.wait_ge(mixed.sem, mixed.at(t, n - 1))
                nc.scalar.copy(probT[:, n % 2, :], bank_pt[n % 2][:, :]).then_inc(p_copied.sem, 1)

            def copy_out(t):
                if not live(t):
                    return
                act.wait_ge(o_turned.sem, o_turned.at(t))
                act.wait_ge(out.sem, out.at(t - 1))
                nc.scalar.copy(oT[:, :], bank_t[:, :]).then_inc(o_copied.sem, 1)

            def step(s, odd):
                t = s - 2
                copy_h(s - 1)
                power(t, 0)
                copy_out(s - 3)
                copy_prob(t, 0)
                for n in range(1, UNITS):
                    power(t, n)
                    if n == 2:
                        double(s - 1)
                    if n < UNITS - 1:
                        copy_prob(t, n)
                copy_v(s - 1, 1 - odd)
                copy_prob(t, UNITS - 1)
            pipelined(act, 3, step)

        @block.gpsimd
        def _(pool):
            nc.gpsimd.memset(keys[:], 0.0).then_inc(blank, 1)
            pool.wait_ge(blank, 2)
            for e in range(2):
                last = nc.gpsimd.memset(vals[e * SEQ:(e + 1) * SEQ, :, :, :, 2 * HD + e], 1.0)
            last.then_inc(blank, 1)
            for c in (summed, added):
                c.start(pool)

            def sum_parts(t, b):
                if not live(t):
                    return
                pool.wait_ge(rotated.sem, rotated.at(t, 2))
                if isinstance(t, int):
                    if t > 0:
                        pool.wait_ge(keys_in[1 - b], 16 * HEADS * ((t - 1) // 2 + 1))
                else:
                    pool.wait_ge(keys_in[1 - b], (t - 1 - (1 - b)) * 8 * HEADS + 16 * HEADS)
                nc.gpsimd.tensor_tensor(kT[:, :], part[:, 0, :], part[:, 1, :], ALU.add).then_inc(summed.sem, 1)
                pool.wait_ge(rotated.sem, rotated.at(t))
                pool.wait_ge(scored.sem, scored.at(t - 2))
                nc.gpsimd.tensor_tensor(qT[:, b, :], part[:, 2, :], part[:, 3, :], ALU.add).then_inc(summed.sem, 1)

            def add(t):
                if not live(t):
                    return
                pool.wait_ge(updated.sem, updated.at(t))
                x = k.x[:, group(t), :]
                nc.gpsimd.tensor_tensor(x, x, k.u[:, group(t), :], ALU.add).then_inc(added.sem, 1)

            def step(s, odd):
                sum_parts(s - 1, 1 - odd)
                add(s - 3)
            pipelined(pool, 3, step)


def gate(m, k, rows, experts, top2, affine):
    nc = m.nc
    E = experts
    name = f"gate{E}"
    xn, xT = m.sb(name + "_xn", [P, GT]), m.sb(name + "_xT", [P, 2, GT])
    score = m.sb(name + "_score", [P, RT, E])
    k.share = m.sb(name + "_share", [P, RT, E])
    bank_t, bank_l = k.bank[0], k.bank[1:3]
    normed, turned, copied = (m.count(f"{name}_{n}") for n in ("normed", "turned", "copied"))
    scored, kept = (m.count(f"{name}_{n}") for n in ("scored", "kept"))

    with nc.Block() as block:
        @block.vector
        def _(dve):
            normed.start(dve)
            kept.start(dve)

            def step(s, odd):
                if live(s):
                    dve.wait_ge(turned.sem, turned.at(s - 1))
                    for r in range(GR):
                        i = bass.ds(s * GR + r, 1)
                        last = nc.vector.tensor_scalar(tiles(xn, r), rows[:, i, :], k.mean[:, i], k.rstd[:, i],
                                                       ALU.subtract, ALU.mult)
                    last.then_inc(normed.sem, 1)
                if live(s - 2):
                    dve.wait_ge(scored.sem, scored.at(s - 2))
                    nc.vector.tensor_copy(score[:, group(s - 2), :],
                                          bank_l[odd][:, 0:GR * E].rearrange("p (r e) -> p r e", e=E)
                                          ).then_inc(kept.sem, 1)
            pipelined(dve, 2, step)

        @block.tensor
        def _(pe):
            turned.start(pe)
            scored.start(pe)

            def step(s, odd):
                if live(s):
                    pe.wait_ge(normed.sem, normed.at(s))
                    pe.wait_ge(copied.sem, copied.at(s - 1))
                    for r in range(GR):
                        last = nc.tensor.transpose(tiles(bank_t, r), tiles(xn, r), k.ident[:, :])
                    last.then_inc(turned.sem, 1)
                if live(s - 1):
                    b = 1 - odd
                    pe.wait_ge(copied.sem, copied.at(s - 1))
                    pe.wait_ge(kept.sem, kept.at(s - 3))
                    for r in range(GR):
                        last = nc.tensor.matmul(bank_l[b][:, r * E:(r + 1) * E], tiles(xT[:, b, :], r), k.gate_w[:, :],
                                                start=True, stop=True)
                    last.then_inc(scored.sem, 1)
            pipelined(pe, 1, step)

        @block.scalar
        def _(act):
            copied.start(act)

            def step(s, odd):
                act.wait_ge(turned.sem, turned.at(s))
                act.wait_ge(scored.sem, scored.at(s - 2))
                if affine:
                    ins = nc.scalar.activation(xT[:, odd, :], bank_t[:, :], ACT.Identity, bias=k.ln2_b[:, 0:1],
                                               scale=k.ln2_w[:, 0:1])
                else:
                    ins = nc.scalar.copy(xT[:, odd, :], bank_t[:, :])
                ins.then_inc(copied.sem, 1)
            pipelined(act, 0, step)

    w = m.sb(name + "_work", [P, 4, RT, E])
    n = m.sb(name + "_narrow", [P, 6, RT])
    prefer = m.sb(name + "_prefer", [P, E])
    ready = m.sem(name + "_prefer_ready")
    chosen, powered = m.sem(name + "_chosen"), m.sem(name + "_powered")
    with nc.Block() as block:
        @block.gpsimd
        def _(pool):
            nc.gpsimd.iota(prefer[:, :], [[-1, E]], base=E, channel_multiplier=0, allow_small_or_imprecise_dtypes=True
                           ).then_inc(ready, 1)

        @block.vector
        def _(dve):
            v, at = nc.vector, [0]

            def link(ins):
                at[0] += 1
                ins.then_inc(chosen, 1)
                dve.wait_ge(chosen, at[0])

            def wide(a):
                return a.unsqueeze(2).broadcast_to([P, RT, E])

            def pick(scores, top, out):
                link(v.tensor_reduce(top, scores, AX.X, ALU.max))
                link(v.tensor_tensor(w[:, 2, :, :], scores, wide(top), ALU.is_equal))
                link(v.tensor_tensor(w[:, 2, :, :], w[:, 2, :, :], prefer[:, :].unsqueeze(1).broadcast_to([P, RT, E]),
                                     ALU.mult))
                link(v.tensor_reduce(n[:, 5, :], w[:, 2, :, :], AX.X, ALU.max))
                link(v.tensor_tensor(out, w[:, 2, :, :], wide(n[:, 5, :]), ALU.is_equal))

            dve.wait_ge(ready, 1)
            if not top2:
                pick(score[:, :, :], n[:, 0, :], k.share[:, :, :])
                return
            pick(score[:, :, :], n[:, 0, :], w[:, 0, :, :])
            link(v.scalar_tensor_tensor(w[:, 3, :, :], w[:, 0, :, :], -3e38, score[:, :, :], ALU.mult, ALU.add))
            pick(w[:, 3, :, :], n[:, 1, :], w[:, 1, :, :])
            link(v.tensor_tensor(n[:, 2, :], n[:, 1, :], n[:, 0, :], ALU.subtract))
            dve.wait_ge(powered, 1)
            link(v.tensor_scalar(n[:, 4, :], n[:, 3, :], 1.0, None, ALU.add))
            link(v.reciprocal(n[:, 0, :], n[:, 4, :]))
            link(v.tensor_tensor(n[:, 1, :], n[:, 0, :], n[:, 3, :], ALU.mult))
            link(v.tensor_tensor(w[:, 0, :, :], w[:, 0, :, :], wide(n[:, 0, :]), ALU.mult))
            link(v.tensor_tensor(w[:, 1, :, :], w[:, 1, :, :], wide(n[:, 1, :]), ALU.mult))
            link(v.tensor_tensor(k.share[:, :, :], w[:, 0, :, :], w[:, 1, :, :], ALU.add))

        if top2:
            @block.scalar
            def _(act):
                act.wait_ge(chosen, 12)
                nc.scalar.activation(n[:, 3, :], n[:, 2, :], ACT.Exp).then_inc(powered, 1)


def experts_dense(m, k, rows, experts, NK, gated, affine):
    nc = m.nc
    E = experts
    name = f"moe{E}"
    xn, xT = m.sb(name + "_xn", [P, GT]), m.sb(name + "_xT", [P, 2, GT])
    gate_out = m.sb(name + "_silu", [P, 2, GT])
    hidden = m.sb(name + "_hidden", [P, 2, NK, GT])
    part = m.sb(name + "_part", [P, 2, GT])
    total = m.sb(name + "_total", [P, 2, GT])
    bank_t, bank_g, bank_u, bank_y = k.bank[0], k.bank[1:3], k.bank[3:5], k.bank[5:7]
    normed, turned, copied = (m.count(f"{name}_{n}") for n in ("normed", "turned", "copied"))
    raised = m.count(name + "_raised", E * NK)
    silued = m.count(name + "_silued", E * NK)
    bent = m.count(name + "_bent", E * NK) if gated else silued
    lowered = m.count(name + "_lowered", E)
    weighted = m.count(name + "_weighted", E)
    added = m.count(name + "_added", E)

    with nc.Block() as block:
        @block.vector
        def _(dve):
            normed.start(dve)
            weighted.start(dve)
            if gated:
                bent.start(dve)

            def step(s, odd):
                t = s - 2
                if live(s):
                    dve.wait_ge(turned.sem, turned.at(s - 1))
                    for r in range(GR):
                        i = bass.ds(s * GR + r, 1)
                        last = nc.vector.tensor_scalar(tiles(xn, r), rows[:, i, :], k.mean[:, i], k.rstd[:, i],
                                                       ALU.subtract, ALU.mult)
                    last.then_inc(normed.sem, 1)

                def weigh(e):
                    dve.wait_ge(lowered.sem, lowered.at(t, e + 1))
                    dve.wait_ge(added.sem, added.at(t, e - 2) if e > 2 else added.at(t - 1))
                    dst = part[:, e % 2, :] if e else total[:, odd, :]
                    nc.vector.tensor_tensor(dst.rearrange("p (r c) -> p r c", c=C),
                                            bank_y[e % 2][:, :].rearrange("p (r c) -> p r c", c=C),
                                            k.share[:, group(t), e:e + 1].broadcast_to([P, GR, C]), ALU.mult
                                            ).then_inc(weighted.sem, 1)
                if not live(t):
                    return
                for e in range(E):
                    if gated:
                        for j in range(NK):
                            i = e * NK + j
                            dve.wait_ge(silued.sem, silued.at(t, i + 1))
                            if j == 0:
                                dve.wait_ge(lowered.sem, lowered.at(t, e - 1))
                            nc.vector.tensor_tensor(hidden[:, e % 2, j, :], gate_out[:, i % 2, :], bank_u[i % 2][:, :],
                                                    ALU.mult).then_inc(bent.sem, 1)
                    if e > 0:
                        weigh(e - 1)
                weigh(E - 1)
            pipelined(dve, 2, step)

        @block.tensor
        def _(pe):
            for c in (turned, raised, lowered):
                c.start(pe)

            def step(s, odd):
                t = s - 2
                if live(s - 1):
                    pe.wait_ge(normed.sem, normed.at(s - 1))
                    pe.wait_ge(copied.sem, copied.at(s - 2))
                    for r in range(GR):
                        last = nc.tensor.transpose(tiles(bank_t, r), tiles(xn, r), k.ident[:, :])
                    last.then_inc(turned.sem, 1)
                if not live(t):
                    return
                pe.wait_ge(copied.sem, copied.at(t))

                def up(e, j):
                    i = e * NK + j
                    if gated:
                        pe.wait_ge(bent.sem, bent.at(t, i - 1))
                    else:
                        pe.wait_ge(silued.sem, silued.at(t, i - 1))
                    last = nc.tensor.matmul(bank_g[i % 2][:, :], k.up_w[:, e, j * P:(j + 1) * P], xT[:, odd, :],
                                            start=True, stop=True)
                    if gated:
                        last = nc.tensor.matmul(bank_u[i % 2][:, :], k.up_w[:, e, (NK + j) * P:(NK + j + 1) * P],
                                                xT[:, odd, :], start=True, stop=True)
                    last.then_inc(raised.sem, 1)

                def down(e, j):
                    if j == 0:
                        pe.wait_ge(weighted.sem, weighted.at(t, e - 1))
                    pe.wait_ge(bent.sem, bent.at(t, e * NK + j + 1))
                    for r in range(GR):
                        last = nc.tensor.matmul(tiles(bank_y[e % 2], r), tiles(hidden[:, e % 2, j, :], r),
                                                k.down_w[:, e, j, :], start=j == 0 and r == 0, stop=j == NK - 1,
                                                skip_group_check=True)
                    if j == NK - 1:
                        last.then_inc(lowered.sem, 1)

                for e in range(E + 1):
                    for j in range(NK):
                        if e < E:
                            up(e, j)
                        if e > 0:
                            down(e - 1, j)
            pipelined(pe, 2, step)

        @block.scalar
        def _(act):
            copied.start(act)
            silued.start(act)

            def step(s, odd):
                t = s - 2
                if live(s - 1):
                    b = 1 - odd
                    act.wait_ge(turned.sem, turned.at(s - 1))
                    act.wait_ge(raised.sem, raised.at(s - 3))
                    if affine:
                        ins = nc.scalar.activation(xT[:, b, :], bank_t[:, :], ACT.Identity, bias=k.ln2_b[:, 0:1],
                                                   scale=k.ln2_w[:, 0:1])
                    else:
                        ins = nc.scalar.copy(xT[:, b, :], bank_t[:, :])
                    ins.then_inc(copied.sem, 1)
                if not live(t):
                    return
                for i in range(E * NK):
                    e, j = i // NK, i % NK
                    act.wait_ge(raised.sem, raised.at(t, i + 1))
                    if gated:
                        act.wait_ge(bent.sem, bent.at(t, i - 1))
                        dst = gate_out[:, i % 2, :]
                    else:
                        if j == 0:
                            act.wait_ge(lowered.sem, lowered.at(t, e - 1))
                        dst = hidden[:, e % 2, j, :]
                    nc.scalar.activation(dst, bank_g[i % 2][:, :], ACT.Silu).then_inc(silued.sem, 1)
            pipelined(act, 2, step)

        @block.gpsimd
        def _(pool):
            added.start(pool)

            def step(s, odd):
                for e in range(1, E):
                    pool.wait_ge(added.sem, added.at(s, e - 1))
                    pool.wait_ge(weighted.sem, weighted.at(s, e + 1))
                    nc.gpsimd.tensor_tensor(total[:, odd, :], total[:, odd, :], part[:, e % 2, :], ALU.add
                                            ).then_inc(added.sem, 1)
                pool.wait_ge(added.sem, added.at(s, E - 1))
                x = k.x[:, group(s), :]
                nc.gpsimd.tensor_tensor(x, x, total[:, odd, :].rearrange("p (r c) -> p r c", c=C), ALU.add
                                        ).then_inc(added.sem, 1)
            pipelined(pool, 0, step)


def take_rows(m, k, rows):
    with m.nc.Block() as block:
        @block.vector
        def _(dve):
            for r in range(RT):
                m.nc.vector.bn_stats(k.stats[:, r, :], rows[:, r, :])


def phase_b(m, k, dram):
    gate(m, k, k.x, 8, True, False)
    experts_dense(m, k, k.x, 8, 2, False, False)
    take_rows(m, k, k.x)


def phase_e(m, k, dram):
    gate(m, k, k.u, 4, False, True)
    experts_dense(m, k, k.u, 4, 4, True, True)


PHASES = {"A": phase_a, "B": phase_b, "C": phase_c, "D": phase_d, "E": phase_e}


def build(nc, dram, out, phases="ABCDE"):
    with ExitStack() as ctx:
        m = Machine(nc, ctx)

        class Kept:
            pass
        k = Kept()
        k.x = m.sb("x_rows", [P, RT, C])
        k.u = m.sb("u_rows", [P, RT, C])
        k.stats = m.sb("stats", [P, RT, 6])
        k.mean = m.sb("mean", [P, RT])
        k.rstd = m.sb("rstd", [P, RT])
        k.rstd2 = m.sb("rstd2", [P, RT])
        k.work = m.sb("work", [P, 10, RT])
        k.eps = m.sb("eps", [P, 1])
        k.bank = [m.psum(f"bank{i}") for i in range(8)]
        k.ident = m.sb("ident", [P, P])
        k.ident_bf = m.sb("ident_bf", [P, P], BF16)
        load_phase(m, k, dram)
        for phase in phases:
            with ExitStack() as own:
                mine = Machine(nc, own)
                constants(mine, k, dram, phase)
                statistics(m, k, phase)
                PHASES[phase](mine, k, dram)
        stored = m.sem("stored")
        with nc.Block() as block:
            @block.sync
            def _(sp):
                sp.dma_start(out.rearrange("(r two) s c -> (two s) r c", two=2), k.x[:, :, :]).then_inc(stored, 16)
                sp.wait_ge(stored, 16)




def shape_tables():
    import numpy as np
    f32 = np.float32
    pos = np.arange(SEQ, dtype=f32)
    half = C // 2
    scale = ((np.arange(0, C, 2, dtype=f32) + f32(0.4 * C)) / f32(1.4 * C))[None, :] ** (pos / f32(512.0))[:, None]
    freqs = f32(1.0) / f32(10000.0) ** (np.arange(half, dtype=f32) / f32(half))
    angle = pos[:, None] * freqs[None, :]
    cos, sin = np.cos(angle), np.sin(angle)
    rope_a = np.stack([np.repeat(t, 2, axis=1).T for t in (cos * scale, sin * scale, cos / scale, sin / scale)], 1)
    tok = np.arange(P)
    same = (tok[:, None] // SEQ) == (tok[None, :] // SEQ)
    diff = (tok[None, :] - tok[:, None]).astype(f32)
    decay = np.where(same & (diff >= 0), f32(0.96875) ** np.maximum(diff, 0), f32(0.0)).astype(f32)
    causal = tok[:, None] >= tok[None, :]
    self_mask = np.where(same & causal, f32(0), f32(MASKED))
    cross_mask = np.where(same, f32(0), f32(MASKED))
    head_mask = np.where((tok[:, None] % SEQ) >= np.arange(SEQ)[None, :], f32(0), f32(MASKED))
    masks = np.stack([np.tile(self_mask, (1, GR)), np.tile(cross_mask, (1, GR)), np.tile(head_mask, (1, 8))], 1)
    inv = f32(1.0) / f32(10000.0) ** (np.arange(0, 8, 2, dtype=f32) / f32(8))
    emb = np.concatenate([pos[:, None] * inv[None, :]] * 2, axis=1)
    rope_d = np.stack([np.tile(np.cos(emb).T, (16, 1)), np.tile(np.sin(emb).T, (16, 1))], 1)
    return {n: np.ascontiguousarray(t.astype(f32)) for n, t in
            (("rope_a", rope_a), ("decay", decay), ("masks", masks), ("rope_d", rope_d))}


def kernel(**inputs):
    import numpy as np
    import concourse.bacc as bacc
    from concourse.bass_utils import run_bass_kernel_spmd

    nc = bacc.Bacc("TRN2", target_bir_lowering=False, num_devices=1)
    arrays = {n: np.ascontiguousarray(a) for n, a in inputs.items()} | shape_tables()
    dram = {n: nc.dram_tensor(n + "_dram", a.shape, mybir.dt.from_np(a.dtype), kind="ExternalInput").ap()
            for n, a in arrays.items()}
    out = nc.dram_tensor("out_dram", [BATCHES, SEQ, C], F32, kind="ExternalOutput").ap()
    build(nc, dram, out)
    got = run_bass_kernel_spmd(nc, [{n + "_dram": a for n, a in arrays.items()}], core_ids=[0])
    return got.results[0]["out_dram"]
```

```python
import concourse.bass as bass
from concourse import mybir
from contextlib import ExitStack

F32 = mybir.dt.float32
BF16 = mybir.dt.bfloat16
ALU = mybir.AluOpType
ACT = mybir.ActivationFunctionType
AX = mybir.AxisListType

P = 128
C = 128
BATCHES = 128
SEQ = 64
TOK = BATCHES * SEQ
RT = TOK // P
GR = 4
GT = GR * P
NG = TOK // GT
GB = GT // SEQ
EPS = 1e-5
MASKED = -1e30


def pipelined(eng, depth, step, n=NG, unroll=2):
    head = depth + (n - depth) % unroll
    for s in range(head):
        step(s, s % unroll)
    with eng.Fori(head, n - unroll + 1, unroll) as s:
        for i in range(unroll):
            step(s + i, (head + i) % unroll)
    for s in range(n, n + depth):
        step(s, s % unroll)


def live(t, n=NG):
    return not isinstance(t, int) or 0 <= t < n


def group(t):
    return bass.ds(t * GR, GR)


class Count:

    def __init__(self, sem, per=1, n=NG):
        self.sem, self.per, self.n = sem, per, n

    def start(self, eng):
        eng.sem_inc(self.sem, 2 * self.per)

    def at(self, t, done=None):
        if isinstance(t, int) and t >= self.n:
            t, done = self.n - 1, self.per
        return (t + 2) * self.per + (self.per if done is None else done)


class Machine:

    def __init__(self, nc, ctx):
        self.nc, self.ctx, self.sems = nc, ctx, []

    def sb(self, name, shape, dt=F32):
        return self.ctx.enter_context(self.nc.sbuf_tensor(name, shape, dt))

    def psum(self, name, shape=(P, 512), dt=F32):
        return self.ctx.enter_context(self.nc.psum_tensor(name, list(shape), dt))

    def sem(self, name):
        self.sems.append(self.nc.alloc_semaphore(name))
        return self.sems[-1]

    def clear(self):
        self.nc.all_engine_barrier()
        self.nc.clear_and_free_semaphores(self.sems)
        self.nc.all_engine_barrier()

    def count(self, name, per=1, n=NG):
        return Count(self.sem(name), per, n)


def tiles(buf, r):
    return buf[:, r * P:(r + 1) * P]


def over_batches(table):
    return table.unsqueeze(1).broadcast_to([P, GB, SEQ])


def by_batch(buf):
    return buf.rearrange("p (b s) -> p b s", s=SEQ)


def newton_rsqrt(vec, link, var, guess, a, b, out):
    link(vec.scalar_tensor_tensor(a, var, EPS, guess, ALU.add, ALU.mult))
    link(vec.scalar_tensor_tensor(b, a, -0.5, guess, ALU.mult, ALU.mult))
    link(vec.scalar_tensor_tensor(out, b, 1.5, guess, ALU.add, ALU.mult))


def moments(vec, link, st, tmp, mean, var):
    total, apart, squares, spread = tmp
    vec.tensor_tensor(total, st[:, :, 1], st[:, :, 4], ALU.add)
    vec.tensor_tensor(apart, st[:, :, 1], st[:, :, 4], ALU.subtract)
    link(vec.tensor_tensor(squares, st[:, :, 2], st[:, :, 5], ALU.add))
    vec.tensor_scalar(mean, total, 0.5, None, ALU.mult)
    link(vec.scalar_tensor_tensor(spread, apart, 0.25, apart, ALU.mult, ALU.mult))
    link(vec.scalar_tensor_tensor(var, squares, 1.0 / C, spread, ALU.mult, ALU.add))


def constants(m, k, dram, phase):
    k.loads = []

    def load(name, shape, src):
        t = m.sb(name, shape)
        k.loads.append((t, src))
        return t

    def row(name, key):
        return load(name, [P, P], dram[key].unsqueeze(0).broadcast_to([P, P]))

    if phase == "A":
        k.wq = load("wq", [P, P], dram["L0_xattn_Wq"])
        k.wk = load("wk", [P, P], dram["L0_xattn_Wk"])
        k.wv = load("wv", [P, P], dram["L0_xattn_Wv"])
        k.rope_a = load("rope_a", [P, 4, SEQ], dram["rope_a"])
        k.decay = load("decay", [P, P], dram["decay"])
        k.wq_rot, k.wk_rot = m.sb("wq_rot", [P, P]), m.sb("wk_rot", [P, P])
    if phase == "B":
        k.gate_w = load("gate1_w", [P, 8], dram["L0_ffn_Wg"])
    if phase == "C":
        k.w1 = load("w1", [P, 512], dram["L1_xattn_w1"])
        k.w2 = load("w2", [P, 4, P], dram["L1_xattn_w2"].rearrange("(k h) c -> h k c", h=P))
        k.b1 = load("b1", [P, 4], dram["L1_xattn_b1"].rearrange("(k h) -> h k", h=P))
        k.b2 = row("b2", "L1_xattn_b2")
        k.gamma = [row(f"gamma{i}", f"L1_xattn_g{i}") for i in (1, 2, 3)]
        k.beta = [row(f"beta{i}", f"L1_xattn_beta{i}") for i in (1, 2, 3)]
        k.masks = load("masks_c", [P, 2, GT], dram["masks"][:, 0:2, :])
        k.masks_bf = m.sb("masks_c_bf", [P, 2, GT], BF16)
    if phase == "D":
        k.ln1_w = load("ln1_w", [P, 1], dram["L1_ffn_ln1_w"].unsqueeze(1))
        k.ln1_b = load("ln1_b", [P, 1], dram["L1_ffn_ln1_b"].unsqueeze(1))
        k.conv = load("conv", [P, 3], dram["L1_ffn_conv_w"].rearrange("c a k -> c (a k)"))
        k.qkv = load("qkv", [P, 3, P], dram["L1_ffn_attn_w"].rearrange("c (j n) -> c j n", j=3))
        k.qk_rot = m.sb("qk_rot", [P, 2, P])
        k.rope_d = load("rope_d", [P, 2, SEQ], dram["rope_d"])
        k.proj = load("proj", [P, P], dram["L1_ffn_proj_w"])
        k.masks = load("masks_d", [P, 1, GT], dram["masks"][:, 2:3, :])
        k.masks_bf = m.sb("masks_d_bf", [P, 1, GT], BF16)
    if phase == "E":
        k.ln2_w = load("ln2_w", [P, 1], dram["L1_ffn_ln2_w"].unsqueeze(1))
        k.ln2_b = load("ln2_b", [P, 1], dram["L1_ffn_ln2_b"].unsqueeze(1))
        k.gate_w = load("gate2_w", [P, 4], dram["L1_ffn_router_w"])


def prepare(nc, k, phase):
    if phase == "A":
        for w, rot in ((k.wq, k.wq_rot), (k.wk, k.wk_rot)):
            src, dst = (z[:, :].rearrange("p (i two) -> p i two", two=2) for z in (w, rot))
            nc.scalar.mul(dst[:, :, 0], src[:, :, 1], -1.0)
            nc.scalar.copy(dst[:, :, 1], src[:, :, 0])
    if phase == "D":
        for j in range(2):
            src, dst = (z[:, j, :].rearrange("p (h two d) -> p h two d", two=2, d=4) for z in (k.qkv, k.qk_rot))
            nc.scalar.mul(dst[:, :, 0, :], src[:, :, 1, :], -1.0)
            nc.scalar.copy(dst[:, :, 1, :], src[:, :, 0, :])
    if phase in "CD":
        nc.scalar.copy(k.masks_bf[:, :, :], k.masks[:, :, :])


def load_phase(m, k, dram):
    nc = m.nc
    CH = 8
    x_loaded = [m.sem(f"x_loaded{n}") for n in range(RT // CH)]
    zeroed, made = m.sem("ident_zeroed"), m.sem("ident_made")
    xs = dram["x"].rearrange("(r two) s c -> (two s) r c", two=2)
    with nc.Block() as block:
        @block.sync
        def _(sp):
            for n, loaded in enumerate(x_loaded):
                sp.dma_start(k.x[:, n * CH:(n + 1) * CH, :], xs[:, n * CH:(n + 1) * CH, :]).then_inc(loaded, 16)

        @block.gpsimd
        def _(pool):
            nc.gpsimd.memset(k.ident[:, :], 0.0).then_inc(zeroed, 1)
            nc.gpsimd.memset(k.ident_bf[:, :], 0.0).then_inc(zeroed, 1)
            nc.gpsimd.memset(k.eps[:, :], EPS)
            pool.wait_ge(zeroed, 2)
            for t in (k.ident, k.ident_bf):
                nc.gpsimd.affine_select(out=t[:, :], in_=t[:, :], compare_op=ALU.not_equal, fill=1.0, base=0,
                                        pattern=[[-1, P]], channel_multiplier=1).then_inc(made, 1)

        @block.vector
        def _(dve):
            for r in range(RT):
                if r % CH == 0:
                    dve.wait_ge(x_loaded[r // CH], 16)
                nc.vector.bn_stats(k.stats[:, r, :], k.x[:, r, :])


def statistics(m, k, phase):
    nc = m.nc
    twice = phase == "D"
    steps, guessed, loaded = (m.sem(f"stats_{phase}_{n}") for n in ("steps", "guessed", "loaded"))
    st, w = k.stats, k.work
    with nc.Block() as block:
        @block.sync
        def _(sp):
            with nc.allow_non_contiguous_dma(reason="columns of small vectors"):
                for t, src in k.loads:
                    sp.dma_start(t[:], src).then_inc(loaded, 16)

        @block.vector
        def _(dve):
            n = [0]

            def link(ins):
                n[0] += 1
                ins.then_inc(steps, 1)
                dve.wait_ge(steps, n[0])

            v = nc.vector
            moments(v, link, st, [w[:, i, :] for i in range(4)], k.mean[:, :], w[:, 4, :])
            dve.wait_ge(guessed, 2)
            newton_rsqrt(v, link, w[:, 4, :], w[:, 6, :], w[:, 7, :], w[:, 8, :], k.rstd[:, :])
            if twice:
                link(v.tensor_tensor(w[:, 0, :], k.rstd[:, :], k.rstd[:, :], ALU.mult))
                link(v.tensor_tensor(w[:, 1, :], w[:, 0, :], w[:, 4, :], ALU.mult))
                dve.wait_ge(guessed, 4)
                newton_rsqrt(v, link, w[:, 1, :], w[:, 3, :], w[:, 7, :], w[:, 8, :], w[:, 9, :])
                link(v.tensor_tensor(k.rstd2[:, :], w[:, 9, :], k.rstd[:, :], ALU.mult))

        @block.scalar
        def _(act):
            if phase != "B" and phase != "E":
                nc.scalar.preload_act_table_set("natural_log_exp_and_others")
            act.wait_ge(steps, 3)
            nc.scalar.activation(w[:, 5, :], w[:, 4, :], ACT.Ln, bias=k.eps[:, 0:1]).then_inc(guessed, 1)
            act.wait_ge(guessed, 1)
            nc.scalar.activation(w[:, 6, :], w[:, 5, :], ACT.Exp, scale=-0.5).then_inc(guessed, 1)
            if twice:
                act.wait_ge(steps, 8)
                nc.scalar.activation(w[:, 2, :], w[:, 1, :], ACT.Ln, bias=k.eps[:, 0:1]).then_inc(guessed, 1)
                act.wait_ge(guessed, 3)
                nc.scalar.activation(w[:, 3, :], w[:, 2, :], ACT.Exp, scale=-0.5).then_inc(guessed, 1)
            act.wait_ge(loaded, 16 * len(k.loads))
            prepare(nc, k, phase)


def phase_a(m, k, dram):
    nc = m.nc
    ctx = dram["ctx_1024"].rearrange("(r two) s c -> (two s) r c", two=2)
    xn, z = m.sb("a_xn", [P, 2, GT]), m.sb("a_z", [P, 2, GT])
    xT, zT = m.sb("a_xT", [P, 2, GT]), m.sb("a_zT", [P, 2, GT])
    v = m.sb("a_v", [P, 2, GT])
    part = m.sb("a_part", [P, 4, GT])
    qk = m.sb("a_qk", [P, 2, 2, GT])
    pm = m.sb("a_pm", [P, 2, GT])
    bank_t, bank_v, bank_s, bank_o = k.bank[0], k.bank[5], k.bank[6], k.bank[7]
    bank_qk = k.bank[1:5]

    z_loaded = [m.sem(f"a_z_loaded{b}") for b in range(2)]
    normed = m.count("a_normed")
    turned = m.count("a_turned", 2)
    copied = m.count("a_copied", 2)
    projected = m.count("a_projected", 5)
    v_copied = m.count("a_v_copied")
    rotated = m.count("a_rotated", 4)
    summed = m.count("a_summed", 2)
    scored = m.count("a_scored")
    masked = m.count("a_masked")
    mixed = m.count("a_mixed")
    added = m.count("a_added")

    with nc.Block() as block:
        @block.sync
        def _(sp):
            def step(s, odd):
                sp.wait_ge(turned.sem, turned.at(s - 2))
                sp.dma_start(z[:, odd, :].rearrange("p (r c) -> p r c", c=C), ctx[:, group(s), :]
                             ).then_inc(z_loaded[odd], 16)
            pipelined(sp, 0, step)

        @block.vector
        def _(dve):
            for c in (normed, rotated, masked, added):
                c.start(dve)

            def norm(t, b):
                if not live(t):
                    return
                dve.wait_ge(turned.sem, turned.at(t - 2))
                for r in range(GR):
                    i = bass.ds(t * GR + r, 1)
                    last = nc.vector.tensor_scalar(tiles(xn[:, b, :], r), k.x[:, i, :], k.mean[:, i], k.rstd[:, i],
                                                   ALU.subtract, ALU.mult)
                last.then_inc(normed.sem, 1)

            def rotate(t, b):
                if not live(t):
                    return
                for j in range(4):
                    dve.wait_ge(projected.sem, projected.at(t, j + 1))
                    if j % 2 == 0:
                        dve.wait_ge(summed.sem, summed.at(t - 1, j // 2 + 1))
                    nc.vector.tensor_tensor(by_batch(part[:, j, :]), by_batch(bank_qk[j][:, :]),
                                            over_batches(k.rope_a[:, j, :]), ALU.mult).then_inc(rotated.sem, 1)

            def mask(t, b):
                if not live(t):
                    return
                dve.wait_ge(scored.sem, scored.at(t))
                dve.wait_ge(mixed.sem, mixed.at(t - 2))
                nc.vector.tensor_tensor(pm[:, b, :].rearrange("p (r q) -> p r q", q=P),
                                        bank_s[:, :].rearrange("p (r q) -> p r q", q=P),
                                        k.decay[:, :].unsqueeze(1).broadcast_to([P, GR, P]), ALU.mult
                                        ).then_inc(masked.sem, 1)

            def add(t, b):
                if not live(t):
                    return
                dve.wait_ge(mixed.sem, mixed.at(t))
                x = k.x[:, group(t), :]
                nc.vector.tensor_tensor(x, bank_o[:, :].rearrange("p (r c) -> p r c", c=C), x, ALU.add
                                        ).then_inc(added.sem, 1)
                dve.wait_ge(added.sem, added.at(t))
                for r in range(GR):
                    i = bass.ds(t * GR + r, 1)
                    nc.vector.bn_stats(k.stats[:, i, :], k.x[:, i, :])

            def step(s, odd):
                rotate(s - 2, odd)
                mask(s - 3, 1 - odd)
                norm(s, odd)
                add(s - 3, 1 - odd)
            pipelined(dve, 3, step)

        @block.tensor
        def _(pe):
            for c in (turned, projected, scored, mixed):
                c.start(pe)

            def turn(t, b):
                if not live(t):
                    return
                pe.wait_ge(normed.sem, normed.at(t))
                pe.wait_ge(copied.sem, copied.at(t - 1))
                for r in range(GR):
                    last = nc.tensor.transpose(tiles(bank_t, r), tiles(xn[:, b, :], r), k.ident[:, :])
                last.then_inc(turned.sem, 1)

            def turn_z(t, b):
                if not live(t):
                    return
                pe.wait_ge(z_loaded[b], (t - b) * 8 + 16)
                pe.wait_ge(copied.sem, copied.at(t, 1))
                for r in range(GR):
                    last = nc.tensor.transpose(tiles(bank_t, r), tiles(z[:, b, :], r), k.ident[:, :])
                last.then_inc(turned.sem, 1)

            def project(t, b):
                if not live(t):
                    return
                pe.wait_ge(copied.sem, copied.at(t))
                for j, (w, src) in enumerate(((k.wq, xT), (k.wq_rot, xT), (k.wk, zT), (k.wk_rot, zT))):
                    pe.wait_ge(rotated.sem, rotated.at(t - 1, j + 1))
                    nc.tensor.matmul(bank_qk[j][:, :], w[:, :], src[:, b, :], start=True, stop=True
                                     ).then_inc(projected.sem, 1)
                pe.wait_ge(v_copied.sem, v_copied.at(t - 1))
                for r in range(GR):
                    last = nc.tensor.matmul(tiles(bank_v, r), tiles(zT[:, b, :], r), k.wv[:, :], start=True, stop=True)
                last.then_inc(projected.sem, 1)

            def score(t, b):
                if not live(t):
                    return
                pe.wait_ge(summed.sem, summed.at(t))
                pe.wait_ge(masked.sem, masked.at(t - 1))
                for r in range(GR):
                    last = nc.tensor.matmul(tiles(bank_s, r), tiles(qk[:, b, 1, :], r), tiles(qk[:, b, 0, :], r),
                                            start=True, stop=True)
                last.then_inc(scored.sem, 1)

            def mix(t, b):
                if not live(t):
                    return
                pe.wait_ge(masked.sem, masked.at(t))
                pe.wait_ge(v_copied.sem, v_copied.at(t))
                pe.wait_ge(added.sem, added.at(t - 1))
                for r in range(GR):
                    last = nc.tensor.matmul(tiles(bank_o, r), tiles(pm[:, b, :], r), tiles(v[:, b, :], r),
                                            start=True, stop=True)
                last.then_inc(mixed.sem, 1)

            def step(s, odd):
                project(s - 2, odd)
                turn(s - 1, 1 - odd)
                score(s - 3, 1 - odd)
                turn_z(s - 1, 1 - odd)
                mix(s - 3, 1 - odd)
            pipelined(pe, 3, step)

        @block.scalar
        def _(act):
            for c in (copied, v_copied):
                c.start(act)

            def copy_turned(t, b):
                if not live(t):
                    return
                act.wait_ge(projected.sem, projected.at(t - 2))
                for j, dst in enumerate((xT, zT)):
                    act.wait_ge(turned.sem, turned.at(t, j + 1))
                    nc.scalar.copy(dst[:, b, :], bank_t[:, :]).then_inc(copied.sem, 1)

            def copy_v(t, b):
                if not live(t):
                    return
                act.wait_ge(projected.sem, projected.at(t))
                act.wait_ge(mixed.sem, mixed.at(t - 2))
                nc.scalar.copy(v[:, b, :], bank_v[:, :]).then_inc(v_copied.sem, 1)

            def step(s, odd):
                copy_v(s - 2, odd)
                copy_turned(s - 1, 1 - odd)
            pipelined(act, 2, step)

        @block.gpsimd
        def _(pool):
            summed.start(pool)

            def step(s, odd):
                for j in range(2):
                    pool.wait_ge(rotated.sem, rotated.at(s, 2 * j + 2))
                    pool.wait_ge(scored.sem, scored.at(s - 2))
                    nc.gpsimd.tensor_tensor(qk[:, odd, j, :], part[:, 2 * j, :], part[:, 2 * j + 1, :], ALU.add
                                            ).then_inc(summed.sem, 1)
            pipelined(pool, 0, step)


class LayerNorm:

    def __init__(self, m, k, name, steps, first):
        self.m, self.k, self.nc, self.first = m, k, m.nc, first
        self.rows = m.sb(name + "_rows", [P, GT])
        self.unit = m.sb(name + "_unit", [P, GT])
        self.scaled = m.sb(name + "_scaled", [P, GT])
        self.stats = m.sb(name + "_stats", [P, GR, 6])
        self.mean, self.var = m.sb(name + "_mean", [P, GR]), m.sb(name + "_var", [P, GR])
        self.tmp = m.sb(name + "_tmp", [P, 6, GR])
        self.done = m.count(name + "_done", steps)
        self.guessed = m.count(name + "_guessed", 2)
        self.affine = m.count(name + "_affine", 2)

    def take(self, dve, t):
        c, nc = self.done, self.nc
        for r in range(GR):
            last = nc.vector.bn_stats(self.stats[:, r, :], tiles(self.rows, r))
        last.then_inc(c.sem, 1)
        dve.wait_ge(c.sem, c.at(t, self.first + 1))
        n = [self.first + 1]

        def link(ins):
            n[0] += 1
            ins.then_inc(c.sem, 1)
            dve.wait_ge(c.sem, c.at(t, n[0]))

        moments(nc.vector, link, self.stats, [self.tmp[:, i, :] for i in range(2, 6)], self.mean[:, :], self.var[:, :])

    def guess(self, act, t):
        act.wait_ge(self.done.sem, self.done.at(t, self.first + 4))
        self.nc.scalar.activation(self.tmp[:, 0, :], self.var[:, :], ACT.Ln, bias=self.k.eps[:, 0:1]
                                  ).then_inc(self.guessed.sem, 1)
        act.wait_ge(self.guessed.sem, self.guessed.at(t, 1))
        self.nc.scalar.activation(self.tmp[:, 1, :], self.tmp[:, 0, :], ACT.Exp, scale=-0.5
                                  ).then_inc(self.guessed.sem, 1)

    def apply(self, dve, t):
        c, nc, w = self.done, self.nc, self.tmp
        n = [self.first + 4]

        def link(ins):
            n[0] += 1
            ins.then_inc(c.sem, 1)
            dve.wait_ge(c.sem, c.at(t, n[0]))

        dve.wait_ge(self.guessed.sem, self.guessed.at(t))
        newton_rsqrt(nc.vector, link, self.var[:, :], w[:, 1, :], w[:, 2, :], w[:, 3, :], w[:, 4, :])
        dve.wait_ge(self.affine.sem, self.affine.at(t - 1, 1))
        for r in range(GR):
            last = nc.vector.tensor_scalar(tiles(self.unit, r), tiles(self.rows, r), self.mean[:, r:r + 1],
                                           w[:, 4, r:r + 1], ALU.subtract, ALU.mult)
        last.then_inc(c.sem, 1)

    def scale_shift(self, pool, t, out, gamma, beta, free):
        def by_tile(a):
            return a.rearrange("p (r c) -> p r c", c=C)

        def row(a):
            return a[:, :].unsqueeze(1).broadcast_to([P, GR, C])

        a = self.affine
        pool.wait_ge(self.done.sem, self.done.at(t))
        self.nc.gpsimd.tensor_tensor(by_tile(self.scaled[:, :]), by_tile(self.unit[:, :]), row(gamma), ALU.mult
                                     ).then_inc(a.sem, 1)
        pool.wait_ge(a.sem, a.at(t, 1))
        free()
        self.nc.gpsimd.tensor_tensor(by_tile(out), by_tile(self.scaled[:, :]), row(beta), ALU.add).then_inc(a.sem, 1)


class Attention:

    SCALE = float(C) ** -0.5

    def __init__(self, m, k, name, mask, bank_s, bank_pt, bank_o):
        self.nc, self.k, self.mask = m.nc, k, mask
        self.bank_s, self.bank_pt, self.bank_o = bank_s, bank_pt, bank_o
        self.p, self.pT = m.sb(name + "_p", [P, GT]), m.sb(name + "_pT", [P, GT])
        self.top = m.sb(name + "_top", [P, 2, GR])
        self.sums = m.sb(name + "_sums", [P, GR])
        self.inverse = m.sb(name + "_inverse", [P, GR])
        self.scored = m.count(name + "_scored")
        self.topped = m.count(name + "_topped", 2)
        self.powered = m.count(name + "_powered")
        self.turned = m.count(name + "_turned")
        self.copied = m.count(name + "_copied")
        self.mixed = m.count(name + "_mixed")

    def score(self, pe, t, qT, kT):
        nc = self.nc
        pe.wait_ge(self.powered.sem, self.powered.at(t - 1))
        nc.tensor.matmul(self.bank_s[:, :], self.k.ident_bf[:, :], self.mask, start=True, stop=False)
        for r in range(GR):
            last = nc.tensor.matmul(tiles(self.bank_s, r), tiles(qT, r), tiles(kT, r), start=False, stop=r == GR - 1)
        last.then_inc(self.scored.sem, 1)

    def find_top(self, dve, t):
        nc, c = self.nc, self.topped
        dve.wait_ge(self.scored.sem, self.scored.at(t))
        nc.vector.tensor_reduce(self.top[:, 0, :], self.bank_s[:, :].rearrange("p (r q) -> p r q", q=P), AX.X, ALU.max
                                ).then_inc(c.sem, 1)
        dve.wait_ge(c.sem, c.at(t, 1))
        dve.wait_ge(self.powered.sem, self.powered.at(t - 1))
        nc.vector.tensor_scalar(self.top[:, 1, :], self.top[:, 0, :], -self.SCALE, None, ALU.mult).then_inc(c.sem, 1)

    def power(self, act, t):
        nc = self.nc
        act.wait_ge(self.topped.sem, self.topped.at(t))
        act.wait_ge(self.turned.sem, self.turned.at(t - 1))
        for r in range(GR):
            last = nc.scalar.activation(tiles(self.p, r), tiles(self.bank_s, r), ACT.Exp, bias=self.top[:, 1, r:r + 1],
                                        scale=self.SCALE, accum_out=self.sums[:, r:r + 1])
        last.then_inc(self.powered.sem, 1)

    def turn(self, pe, t, bank_free):
        pe.wait_ge(self.powered.sem, self.powered.at(t))
        bank_free()
        for r in range(GR):
            last = self.nc.tensor.transpose(tiles(self.bank_pt, r), tiles(self.p, r), self.k.ident[:, :])
        last.then_inc(self.turned.sem, 1)

    def copy(self, act, t):
        act.wait_ge(self.turned.sem, self.turned.at(t))
        act.wait_ge(self.mixed.sem, self.mixed.at(t - 1))
        self.nc.scalar.copy(self.pT[:, :], self.bank_pt[:, :]).then_inc(self.copied.sem, 1)

    def mix(self, pe, t, v, bank_free):
        pe.wait_ge(self.copied.sem, self.copied.at(t))
        bank_free()
        for r in range(GR):
            last = self.nc.tensor.matmul(tiles(self.bank_o, r), tiles(self.pT, r), tiles(v, r), start=True, stop=True)
        last.then_inc(self.mixed.sem, 1)

    def finish(self, dve, t, rows, residual, count):
        nc = self.nc
        dve.wait_ge(self.mixed.sem, self.mixed.at(t))
        nc.vector.reciprocal(self.inverse[:, :], self.sums[:, :]).then_inc(count.sem, 1)
        dve.wait_ge(count.sem, count.at(t, 1))
        for r in range(GR):
            last = nc.vector.scalar_tensor_tensor(tiles(rows, r), tiles(self.bank_o, r), self.inverse[:, r:r + 1],
                                                  tiles(residual, r), ALU.mult, ALU.add)
        last.then_inc(count.sem, 1)
        dve.wait_ge(count.sem, count.at(t, 2))


def phase_c(m, k, dram):
    nc = m.nc
    ctx = dram["ctx_1024"].rearrange("(r two) s c -> (two s) r c", two=2)
    NK = 4
    y, z, y1, y2 = (m.sb("c_" + n, [P, 2, GT]) for n in ("y", "z", "y1", "y2"))
    yT, zT, y1T, y2T = (m.sb("c_" + n, [P, GT]) for n in ("yT", "zT", "y1T", "y2T"))
    hidden = m.sb("c_hidden", [P, NK, GT])
    y2b = m.sb("c_y2b", [P, GT])
    y3 = m.sb("c_y3", [P, GT])
    bank_t, bank_t2, bank_sa, bank_sc, bank_pt, bank_o, bank_h, bank_f = k.bank

    own = Attention(m, k, "c_self", k.masks_bf[:, 0, :], bank_sa, bank_pt, bank_o)
    cross = Attention(m, k, "c_cross", k.masks_bf[:, 1, :], bank_sc, bank_pt, bank_o)
    ln1 = LayerNorm(m, k, "c_ln1", 10, 2)
    ln2 = LayerNorm(m, k, "c_ln2", 10, 2)
    ln3 = LayerNorm(m, k, "c_ln3", 9, 1)
    z_loaded = [m.sem(f"c_z_loaded{b}") for b in range(2)]
    normed = m.count("c_normed")
    turned = {n: m.count("c_turned_" + n) for n in ("y", "z", "y1", "y2")}
    copied = {n: m.count("c_copied_" + n) for n in ("y", "z", "y1", "y2")}
    raised = m.count("c_raised", NK)
    bent = m.count("c_bent", NK)
    lowered = m.count("c_lowered")
    biased = m.count("c_biased")
    added = m.count("c_added")

    with nc.Block() as block:
        @block.sync
        def _(sp):
            def step(s, odd):
                sp.wait_ge(cross.mixed.sem, cross.mixed.at(s - 2))
                sp.dma_start(z[:, odd, :].rearrange("p (r c) -> p r c", c=C), ctx[:, group(s), :]
                             ).then_inc(z_loaded[odd], 16)
            pipelined(sp, 0, step)

        @block.vector
        def _(dve):
            for c in (normed, own.topped, cross.topped, ln1.done, ln2.done, ln3.done):
                c.start(dve)

            def step(s, odd):
                even = 1 - odd
                if live(s - 4):
                    t = s - 4
                    dve.wait_ge(lowered.sem, lowered.at(t))
                    dve.wait_ge(biased.sem, biased.at(t))
                    nc.vector.tensor_tensor(ln3.rows[:, :], bank_f[:, :], y2b[:, :], ALU.add).then_inc(ln3.done.sem, 1)
                    dve.wait_ge(ln3.done.sem, ln3.done.at(t, 1))
                    ln3.take(dve, t)
                if live(s - 1):
                    own.find_top(dve, s - 1)
                if live(s - 4):
                    ln3.apply(dve, s - 4)
                if live(s - 2):
                    cross.find_top(dve, s - 2)
                if live(s):
                    dve.wait_ge(own.mixed.sem, own.mixed.at(s - 2))
                    for r in range(GR):
                        i = bass.ds(s * GR + r, 1)
                        last = nc.vector.tensor_scalar(tiles(y[:, odd, :], r), k.x[:, i, :], k.mean[:, i],
                                                       k.rstd[:, i], ALU.subtract, ALU.mult)
                    last.then_inc(normed.sem, 1)
                if live(s - 1):
                    own.finish(dve, s - 1, ln1.rows, y[:, even, :], ln1.done)
                    ln1.take(dve, s - 1)
                    ln1.apply(dve, s - 1)
                if live(s - 2):
                    cross.finish(dve, s - 2, ln2.rows, y1[:, odd, :], ln2.done)
                    ln2.take(dve, s - 2)
                if live(s - 4):
                    dve.wait_ge(added.sem, added.at(s - 4))
                    for r in range(GR):
                        i = bass.ds((s - 4) * GR + r, 1)
                        nc.vector.bn_stats(k.stats[:, i, :], k.x[:, i, :])
                if live(s - 2):
                    ln2.apply(dve, s - 2)
            pipelined(dve, 4, step)

        @block.tensor
        def _(pe):
            for c in (*turned.values(), own.scored, own.turned, own.mixed, cross.scored, cross.turned, cross.mixed,
                      raised, lowered):
                c.start(pe)

            def turn(name, t, src, bank, other, other_t):
                pe.wait_ge(copied[other].sem, copied[other].at(other_t))
                for r in range(GR):
                    last = nc.tensor.transpose(tiles(bank, r), tiles(src, r), k.ident[:, :])
                last.then_inc(turned[name].sem, 1)

            def up(t, j):
                if not live(t):
                    return
                pe.wait_ge(copied["y2"].sem, copied["y2"].at(t))
                pe.wait_ge(bent.sem, bent.at(t, j))
                nc.tensor.matmul(bank_h[:, :], k.w1[:, j * P:(j + 1) * P], y2T[:, :], start=True, stop=True
                                 ).then_inc(raised.sem, 1)

            def step(s, odd):
                even = 1 - odd
                if live(s - 1):
                    pe.wait_ge(normed.sem, normed.at(s - 1))
                    turn("y", s - 1, y[:, even, :], bank_t, "y1", s - 3)
                if live(s - 2):
                    pe.wait_ge(z_loaded[odd], (s - 2 - odd) * 8 + 16)
                    turn("z", s - 2, z[:, odd, :], bank_t2, "y2", s - 4)
                if live(s - 1):
                    pe.wait_ge(copied["y"].sem, copied["y"].at(s - 1))
                    own.score(pe, s - 1, yT, yT)
                if live(s - 2):
                    pe.wait_ge(ln1.affine.sem, ln1.affine.at(s - 2))
                    turn("y1", s - 2, y1[:, odd, :], bank_t, "y", s - 1)
                    pe.wait_ge(copied["z"].sem, copied["z"].at(s - 2))
                    pe.wait_ge(copied["y1"].sem, copied["y1"].at(s - 2))
                    cross.score(pe, s - 2, y1T, zT)
                if live(s - 3):
                    pe.wait_ge(ln2.affine.sem, ln2.affine.at(s - 3))
                    turn("y2", s - 3, y2[:, even, :], bank_t2, "z", s - 2)
                up(s - 3, 0)
                if live(s - 1):
                    own.turn(pe, s - 1, lambda: pe.wait_ge(cross.copied.sem, cross.copied.at(s - 3)))
                up(s - 3, 1)
                if live(s - 1):
                    own.mix(pe, s - 1, y[:, even, :], lambda: pe.wait_ge(ln2.done.sem, ln2.done.at(s - 3, 2)))
                if live(s - 2):
                    cross.turn(pe, s - 2, lambda: pe.wait_ge(own.copied.sem, own.copied.at(s - 1)))
                up(s - 3, 2)
                if live(s - 2):
                    cross.mix(pe, s - 2, z[:, odd, :], lambda: pe.wait_ge(ln1.done.sem, ln1.done.at(s - 1, 2)))
                up(s - 3, 3)
                if live(s - 3):
                    pe.wait_ge(ln3.done.sem, ln3.done.at(s - 4, 1))
                    for j in range(NK):
                        pe.wait_ge(bent.sem, bent.at(s - 3, j + 1))
                        for r in range(GR):
                            last = nc.tensor.matmul(tiles(bank_f, r), tiles(hidden[:, j, :], r), k.w2[:, j, :],
                                                    start=j == 0 and r == 0, stop=j == NK - 1,
                                                    skip_group_check=True)
                    last.then_inc(lowered.sem, 1)
            pipelined(pe, 3, step)

        @block.scalar
        def _(act):
            for c in (*copied.values(), own.powered, own.copied, cross.powered, cross.copied, bent,
                      ln1.guessed, ln2.guessed, ln3.guessed):
                c.start(act)

            def copy(name, t, dst, bank, reader, count):
                if not live(t):
                    return
                act.wait_ge(turned[name].sem, turned[name].at(t))
                act.wait_ge(reader.sem, count)
                nc.scalar.copy(dst[:, :], bank[:, :]).then_inc(copied[name].sem, 1)

            def relu(t, j):
                if not live(t):
                    return
                act.wait_ge(raised.sem, raised.at(t, j + 1))
                act.wait_ge(lowered.sem, lowered.at(t - 1))
                nc.scalar.activation(hidden[:, j, :], bank_h[:, :], ACT.Relu, bias=k.b1[:, j:j + 1]
                                     ).then_inc(bent.sem, 1)

            def step(s, odd):
                copy("y", s - 1, yT, bank_t, own.scored, own.scored.at(s - 2))
                copy("z", s - 2, zT, bank_t2, cross.scored, cross.scored.at(s - 3))
                copy("y1", s - 2, y1T, bank_t, cross.scored, cross.scored.at(s - 3))
                if live(s - 4):
                    ln3.guess(act, s - 4)
                if live(s - 1):
                    own.power(act, s - 1)
                copy("y2", s - 3, y2T, bank_t2, raised, raised.at(s - 4))
                relu(s - 3, 0)
                if live(s - 1):
                    own.copy(act, s - 1)
                if live(s - 2):
                    cross.power(act, s - 2)
                relu(s - 3, 1)
                if live(s - 1):
                    ln1.guess(act, s - 1)
                if live(s - 2):
                    cross.copy(act, s - 2)
                relu(s - 3, 2)
                if live(s - 2):
                    ln2.guess(act, s - 2)
                relu(s - 3, 3)
            pipelined(act, 4, step)

        @block.gpsimd
        def _(pool):
            for c in (ln1.affine, ln2.affine, ln3.affine, biased, added):
                c.start(pool)

            def step(s, odd):
                even = 1 - odd
                if live(s - 4):
                    t = s - 4
                    ln3.scale_shift(pool, t, y3[:, :], k.gamma[2], k.beta[2], lambda: None)
                    pool.wait_ge(ln3.affine.sem, ln3.affine.at(t))
                    x = k.x[:, group(t), :]
                    nc.gpsimd.tensor_tensor(x, x, y3[:, :].rearrange("p (r c) -> p r c", c=C), ALU.add
                                            ).then_inc(added.sem, 1)
                if live(s - 3):
                    t = s - 3
                    pool.wait_ge(ln2.affine.sem, ln2.affine.at(t))
                    pool.wait_ge(ln3.done.sem, ln3.done.at(t - 1, 1))
                    nc.gpsimd.tensor_tensor(y2b[:, :].rearrange("p (r c) -> p r c", c=C),
                                            y2[:, even, :].rearrange("p (r c) -> p r c", c=C),
                                            k.b2[:, :].unsqueeze(1).broadcast_to([P, GR, C]), ALU.add
                                            ).then_inc(biased.sem, 1)
                if live(s - 1):
                    ln1.scale_shift(pool, s - 1, y1[:, even, :], k.gamma[0], k.beta[0],
                                    lambda: pool.wait_ge(ln2.done.sem, ln2.done.at(s - 3, 2)))
                if live(s - 2):
                    ln2.scale_shift(pool, s - 2, y2[:, odd, :], k.gamma[1], k.beta[1],
                                    lambda: pool.wait_ge(turned["y2"].sem, turned["y2"].at(s - 4)))
            pipelined(pool, 4, step)


def phase_d(m, k, dram):
    nc = m.nc
    HEADS, HD = 16, 8
    UNITS = 2 * GR
    PAIRS = HEADS // 2
    VW = 2 * HD + 2
    SCALE = float(HD) ** -0.5
    xn, hT, cT = m.sb("d_xn", [P, GT]), m.sb("d_hT", [P, GT]), m.sb("d_cT", [P, GT])
    cTT = m.sb("d_cTT", [P, GB * P])
    part = m.sb("d_part", [P, 4, GT])
    kT, qT = m.sb("d_kT", [P, GT]), m.sb("d_qT", [P, 2, GT])
    keys = m.sb("d_keys", [P, 2, GB, HEADS, SEQ])
    vals = m.sb("d_vals", [P, 2, GB, PAIRS, VW])
    prob, probT = m.sb("d_prob", [P, 2, 512]), m.sb("d_probT", [P, 2, 512])
    top = m.sb("d_top", [P, 2, 8])
    inverse = m.sb("d_inverse", [P, PAIRS, 2])
    o, oT, u = m.sb("d_o", [P, GT]), m.sb("d_oT", [P, GT]), m.sb("d_u", [P, GT])
    bank_t, bank_l, bank_r, bank_s, bank_pt, bank_o = k.bank[0], k.bank[1], k.bank[2], k.bank[3:5], k.bank[5:7], k.bank[7]

    blank = m.sem("d_blank")
    normed = m.count("d_normed")
    turned = m.count("d_turned")
    h_copied = m.count("d_h_copied")
    conved = m.count("d_conved", 3)
    doubled = m.count("d_doubled")
    projected = m.count("d_projected", 5)
    rotated = m.count("d_rotated", 4)
    summed = m.count("d_summed", 2)
    keys_in = [m.sem(f"d_keys_in{b}") for b in range(2)]
    v_copied = m.count("d_v_copied")
    scored = m.count("d_scored", UNITS)
    topped = m.count("d_topped", 2 * UNITS)
    powered = m.count("d_powered", UNITS)
    p_turned = m.count("d_p_turned", UNITS)
    p_copied = m.count("d_p_copied", UNITS)
    mixed = m.count("d_mixed", UNITS)
    divided = m.count("d_divided", 2 * GR)
    o_turned = m.count("d_o_turned")
    o_copied = m.count("d_o_copied")
    out = m.count("d_out")
    updated = m.count("d_updated", 2)
    added = m.count("d_added")

    with nc.Block() as block:
        @block.sync
        def _(sp):
            sp.wait_ge(blank, 3)

            def step(s, odd):
                t, b = s, odd
                sp.wait_ge(summed.sem, summed.at(t, 1))
                sp.wait_ge(scored.sem, scored.at(t - 2))
                for h in range(HEADS):
                    rows = slice(h * HD, (h + 1) * HD)
                    sp.dma_start(keys[rows, b, :, h, :], by_batch(kT[rows, :])).then_inc(keys_in[b], 16)
            pipelined(sp, 0, step)

        @block.vector
        def _(dve):
            nc.vector.memset(vals[:], 0.0).then_inc(blank, 1)
            for c in (normed, conved, rotated, topped, divided, updated):
                c.start(dve)

            def norm(t):
                if not live(t):
                    return
                dve.wait_ge(turned.sem, turned.at(t - 1))
                for r in range(GR):
                    i = bass.ds(t * GR + r, 1)
                    last = nc.vector.tensor_scalar(tiles(xn, r), k.x[:, i, :], k.mean[:, i], k.rstd2[:, i],
                                                   ALU.subtract, ALU.mult)
                last.then_inc(normed.sem, 1)

            def convolve(t):
                if not live(t):
                    return
                h, c = by_batch(hT[:, :]), by_batch(cT[:, :])
                dve.wait_ge(h_copied.sem, h_copied.at(t))
                dve.wait_ge(projected.sem, projected.at(t - 1, 4))
                dve.wait_ge(doubled.sem, doubled.at(t - 1))
                nc.vector.tensor_scalar(c, h, k.conv[:, 2:3], None, ALU.mult).then_inc(conved.sem, 1)
                for lag in (1, 2):
                    dve.wait_ge(conved.sem, conved.at(t, lag))
                    nc.vector.scalar_tensor_tensor(c[:, :, lag:], h[:, :, :SEQ - lag], k.conv[:, 2 - lag:3 - lag],
                                                   c[:, :, lag:], ALU.mult, ALU.add).then_inc(conved.sem, 1)

            def rotate(t, first):
                if not live(t):
                    return
                for j in (first, first + 1):
                    dve.wait_ge(projected.sem, projected.at(t, j + 1))
                    dve.wait_ge(summed.sem, summed.at(t - 1, first // 2 + 1))
                    nc.vector.tensor_tensor(by_batch(part[:, j, :]), by_batch((bank_l, bank_r)[j % 2][:, :]),
                                            over_batches(k.rope_d[:, j % 2, :]), ALU.mult).then_inc(rotated.sem, 1)

            def shift(t, n):
                if not live(t):
                    return
                scores = bank_s[n % 2][:, :].rearrange("p (h s) -> p h s", s=SEQ)
                dve.wait_ge(scored.sem, scored.at(t, n + 1))
                nc.vector.tensor_reduce(top[:, n % 2, :], scores, AX.X, ALU.max).then_inc(topped.sem, 1)
                dve.wait_ge(topped.sem, topped.at(t, 2 * n + 1))
                dve.wait_ge(p_turned.sem, p_turned.at(t, n - 1))
                nc.vector.tensor_tensor(prob[:, n % 2, :].rearrange("p (h s) -> p h s", s=SEQ), scores,
                                        top[:, n % 2, :].unsqueeze(2).broadcast_to([P, 8, SEQ]), ALU.subtract
                                        ).then_inc(topped.sem, 1)

            def divide(t, r):
                if not live(t):
                    return
                got = bank_o[:, 0:PAIRS * VW].rearrange("p (j w) -> p j w", w=VW)
                dve.wait_ge(mixed.sem, mixed.at(t, 2 * r + 2))
                nc.vector.reciprocal(inverse[:, :, :], got[:, :, 2 * HD:]).then_inc(divided.sem, 1)
                dve.wait_ge(divided.sem, divided.at(t, 2 * r + 1))
                if r == 0:
                    dve.wait_ge(o_turned.sem, o_turned.at(t - 1))
                nc.vector.tensor_tensor(tiles(o, r).rearrange("p (j e d) -> p j e d", j=PAIRS, e=2),
                                        got[:, :, 0:2 * HD].rearrange("p j (e d) -> p j e d", e=2),
                                        inverse[:, :, :].unsqueeze(3).broadcast_to([P, PAIRS, 2, HD]), ALU.mult
                                        ).then_inc(divided.sem, 1)

            def unit_rows(t):
                if not live(t):
                    return
                for r in range(GR):
                    i = bass.ds(t * GR + r, 1)
                    last = nc.vector.tensor_scalar(tiles(u, r), k.x[:, i, :], k.mean[:, i], k.rstd[:, i],
                                                   ALU.subtract, ALU.mult)
                last.then_inc(updated.sem, 1)

            def update(t):
                if not live(t):
                    return
                dve.wait_ge(out.sem, out.at(t))
                dve.wait_ge(updated.sem, updated.at(t, 1))
                dst = k.u[:, group(t), :]
                nc.vector.tensor_tensor(dst, bank_t[:, :].rearrange("p (r c) -> p r c", c=C),
                                        u[:, :].rearrange("p (r c) -> p r c", c=C), ALU.add).then_inc(updated.sem, 1)

            def take(t):
                if not live(t):
                    return
                dve.wait_ge(updated.sem, updated.at(t))
                for r in range(GR):
                    i = bass.ds(t * GR + r, 1)
                    nc.vector.bn_stats(k.stats[:, i, :], k.u[:, i, :])

            def step(s, odd):
                t = s - 2
                shift(t, 0)
                divide(s - 3, 3)
                convolve(s - 1)
                shift(t, 1)
                unit_rows(s - 3)
                shift(t, 2)
                update(s - 3)
                rotate(s - 1, 0)
                shift(t, 3)
                divide(t, 0)
                shift(t, 4)
                norm(s)
                shift(t, 5)
                divide(t, 1)
                rotate(s - 1, 2)
                shift(t, 6)
                take(s - 3)
                shift(t, 7)
                divide(t, 2)
            pipelined(dve, 3, step)

        @block.tensor
        def _(pe):
            for c in (turned, projected, scored, p_turned, mixed, o_turned, out):
                c.start(pe)
            pe.wait_ge(blank, 3)

            def turn(t):
                if not live(t):
                    return
                pe.wait_ge(normed.sem, normed.at(t))
                pe.wait_ge(updated.sem, updated.at(t - 3))
                for r in range(GR):
                    last = nc.tensor.transpose(tiles(bank_t, r), tiles(xn, r), k.ident[:, :])
                last.then_inc(turned.sem, 1)

            def project(t, first):
                if not live(t):
                    return
                j = 1 - first // 2
                if first == 0:
                    pe.wait_ge(conved.sem, conved.at(t))
                    pe.wait_ge(v_copied.sem, v_copied.at(t - 1))
                else:
                    pe.wait_ge(rotated.sem, rotated.at(t, 2))
                nc.tensor.matmul(bank_l[:, :], k.qkv[:, j, :], cT[:, :], start=True, stop=True).then_inc(projected.sem, 1)
                nc.tensor.matmul(bank_r[:, :], k.qk_rot[:, j, :], cT[:, :], start=True, stop=True
                                 ).then_inc(projected.sem, 1)

            def values(t):
                if not live(t):
                    return
                pe.wait_ge(rotated.sem, rotated.at(t))
                pe.wait_ge(doubled.sem, doubled.at(t))
                for i in range(GB):
                    bank = (bank_l, bank_r)[i // 4]
                    last = nc.tensor.matmul(tiles(bank, i % 4), tiles(cTT, i), k.qkv[:, 2, :], start=True, stop=True)
                last.then_inc(projected.sem, 1)

            def score(t, b, n):
                if not live(t):
                    return
                r, half = n // 2, n % 2
                bank = bank_s[n % 2]
                if n == 0:
                    pe.wait_ge(summed.sem, summed.at(t))
                    pe.wait_ge(keys_in[b], (t - b) * 8 * HEADS + 16 * HEADS)
                pe.wait_ge(topped.sem, topped.at(t, 2 * n - 2))
                nc.tensor.matmul(bank[:, :], k.ident_bf[:, :], k.masks_bf[:, 0, :], start=True, stop=False,
                                 skip_group_check=True)
                for e in range(2):
                    i = 2 * r + e
                    last = nc.tensor.matmul(bank[e * SEQ:(e + 1) * SEQ, :], qT[:, b, i * SEQ:(i + 1) * SEQ],
                                            keys[:, b, i, half * 8:half * 8 + 8, :], start=False, stop=True,
                                            tile_position=(0, e * SEQ), skip_group_check=True)
                last.then_inc(scored.sem, 1)

            def turn_prob(t, n):
                if not live(t):
                    return
                pe.wait_ge(powered.sem, powered.at(t, n + 1))
                pe.wait_ge(p_copied.sem, p_copied.at(t, n - 1))
                for j in range(4):
                    last = nc.tensor.transpose(tiles(bank_pt[n % 2], j), tiles(prob[:, n % 2, :], j), k.ident[:, :])
                last.then_inc(p_turned.sem, 1)

            def mix(t, b, n):
                if not live(t):
                    return
                r, half = n // 2, n % 2
                pe.wait_ge(p_copied.sem, p_copied.at(t, n + 1))
                if n == 0:
                    pe.wait_ge(v_copied.sem, v_copied.at(t))
                if half == 0:
                    pe.wait_ge(divided.sem, divided.at(t, 2 * r))
                for j in range(4):
                    pair = half * 4 + j
                    for e in range(2):
                        last = nc.tensor.matmul(bank_o[e * SEQ:(e + 1) * SEQ, pair * VW:(pair + 1) * VW],
                                                probT[:, n % 2, j * P + e * SEQ:j * P + (e + 1) * SEQ],
                                                vals[:, b, 2 * r + e, pair, :], start=True, stop=True,
                                                tile_position=(0, e * SEQ))
                last.then_inc(mixed.sem, 1)

            def turn_out(t):
                if not live(t):
                    return
                pe.wait_ge(divided.sem, divided.at(t))
                pe.wait_ge(h_copied.sem, h_copied.at(t + 2))
                for r in range(GR):
                    last = nc.tensor.transpose(tiles(bank_t, r), tiles(o, r), k.ident[:, :])
                last.then_inc(o_turned.sem, 1)

            def project_out(t):
                if not live(t):
                    return
                pe.wait_ge(o_copied.sem, o_copied.at(t))
                for r in range(GR):
                    last = nc.tensor.matmul(tiles(bank_t, r), tiles(oT, r), k.proj[:, :], start=True, stop=True)
                last.then_inc(out.sem, 1)

            def step(s, odd):
                t, b = s - 2, odd
                score(t, b, 0)
                turn(s - 1)
                score(t, b, 1)
                turn_out(s - 3)
                turn_prob(t, 0)
                for n in range(2, UNITS):
                    score(t, b, n)
                    if n == 2:
                        project_out(s - 3)
                    mix(t, b, n - 2)
                    if n == 3:
                        project(s - 1, 0)
                    if n == 5:
                        project(s - 1, 2)
                    turn_prob(t, n - 1)
                mix(t, b, UNITS - 2)
                values(s - 1)
                turn_prob(t, UNITS - 1)
                mix(t, b, UNITS - 1)
            pipelined(pe, 3, step)

        @block.scalar
        def _(act):
            for c in (h_copied, doubled, v_copied, powered, p_copied, o_copied):
                c.start(act)
            act.wait_ge(blank, 3)

            def copy_h(t):
                if not live(t):
                    return
                act.wait_ge(turned.sem, turned.at(t))
                act.wait_ge(conved.sem, conved.at(t - 1))
                nc.scalar.activation(hT[:, :], bank_t[:, :], ACT.Identity, bias=k.ln1_b[:, 0:1], scale=k.ln1_w[:, 0:1]
                                     ).then_inc(h_copied.sem, 1)

            def double(t):
                if not live(t):
                    return
                act.wait_ge(conved.sem, conved.at(t))
                act.wait_ge(projected.sem, projected.at(t - 1))
                nc.scalar.copy(cTT[:, :].rearrange("p (b e s) -> p b e s", e=2, s=SEQ),
                               by_batch(cT[:, :]).unsqueeze(2).broadcast_to([P, GB, 2, SEQ])).then_inc(doubled.sem, 1)

            def copy_v(t, b):
                if not live(t):
                    return
                act.wait_ge(projected.sem, projected.at(t))
                act.wait_ge(mixed.sem, mixed.at(t - 2))
                for n, bank in enumerate((bank_l, bank_r)):
                    for e in range(2):
                        rows = slice(e * SEQ, (e + 1) * SEQ)
                        got = bank[rows, :].rearrange("p (i j e d) -> p i j e d", i=4, j=PAIRS, e=2)
                        last = nc.scalar.copy(vals[rows, b, 4 * n:4 * n + 4, :, e * HD:(e + 1) * HD], got[:, :, :, e, :])
                last.then_inc(v_copied.sem, 1)

            def power(t, n):
                if not live(t):
                    return
                act.wait_ge(topped.sem, topped.at(t, 2 * n + 2))
                nc.scalar.activation(prob[:, n % 2, :], prob[:, n % 2, :], ACT.Exp, scale=SCALE).then_inc(powered.sem, 1)

            def copy_prob(t, n):
                if not live(t):
                    return
                act.wait_ge(p_turned.sem, p_turned.at(t, n + 1))
                act.wait_ge(mixed.sem, mixed.at(t, n - 1))
                nc.scalar.copy(probT[:, n % 2, :], bank_pt[n % 2][:, :]).then_inc(p_copied.sem, 1)

            def copy_out(t):
                if not live(t):
                    return
                act.wait_ge(o_turned.sem, o_turned.at(t))
                act.wait_ge(out.sem, out.at(t - 1))
                nc.scalar.copy(oT[:, :], bank_t[:, :]).then_inc(o_copied.sem, 1)

            def step(s, odd):
                t = s - 2
                copy_h(s - 1)
                power(t, 0)
                copy_out(s - 3)
                copy_prob(t, 0)
                for n in range(1, UNITS):
                    power(t, n)
                    if n == 2:
                        double(s - 1)
                    if n < UNITS - 1:
                        copy_prob(t, n)
                copy_v(s - 1, 1 - odd)
                copy_prob(t, UNITS - 1)
            pipelined(act, 3, step)

        @block.gpsimd
        def _(pool):
            nc.gpsimd.memset(keys[:], 0.0).then_inc(blank, 1)
            pool.wait_ge(blank, 2)
            for e in range(2):
                last = nc.gpsimd.memset(vals[e * SEQ:(e + 1) * SEQ, :, :, :, 2 * HD + e], 1.0)
            last.then_inc(blank, 1)
            for c in (summed, added):
                c.start(pool)

            def sum_parts(t, b):
                if not live(t):
                    return
                pool.wait_ge(rotated.sem, rotated.at(t, 2))
                if isinstance(t, int):
                    if t > 0:
                        pool.wait_ge(keys_in[1 - b], 16 * HEADS * ((t - 1) // 2 + 1))
                else:
                    pool.wait_ge(keys_in[1 - b], (t - 1 - (1 - b)) * 8 * HEADS + 16 * HEADS)
                nc.gpsimd.tensor_tensor(kT[:, :], part[:, 0, :], part[:, 1, :], ALU.add).then_inc(summed.sem, 1)
                pool.wait_ge(rotated.sem, rotated.at(t))
                pool.wait_ge(scored.sem, scored.at(t - 2))
                nc.gpsimd.tensor_tensor(qT[:, b, :], part[:, 2, :], part[:, 3, :], ALU.add).then_inc(summed.sem, 1)

            def add(t):
                if not live(t):
                    return
                pool.wait_ge(updated.sem, updated.at(t))
                x = k.x[:, group(t), :]
                nc.gpsimd.tensor_tensor(x, x, k.u[:, group(t), :], ALU.add).then_inc(added.sem, 1)

            def step(s, odd):
                sum_parts(s - 1, 1 - odd)
                add(s - 3)
            pipelined(pool, 3, step)


def gate(m, k, moe, rows):
    nc = m.nc
    E, top2, affine = moe.E, moe.top == 2, moe.affine
    name = f"gate{E}"
    xn, xT = m.sb(name + "_xn", [P, GT]), m.sb(name + "_xT", [P, 2, GT])
    score = m.sb(name + "_score", [P, RT, E])
    moe.pick = [m.sb(f"{name}_pick{i}", [P, RT, E]) for i in range(moe.top)]
    moe.share = [m.sb(f"{name}_share{i}", [P, RT]) for i in range(2)]
    bank_t, bank_l = k.bank[0], k.bank[1:3]
    normed, turned, copied = (m.count(f"{name}_{n}") for n in ("normed", "turned", "copied"))
    scored, kept = (m.count(f"{name}_{n}") for n in ("scored", "kept"))

    with nc.Block() as block:
        @block.vector
        def _(dve):
            normed.start(dve)
            kept.start(dve)

            def step(s, odd):
                if live(s):
                    dve.wait_ge(turned.sem, turned.at(s - 1))
                    for r in range(GR):
                        i = bass.ds(s * GR + r, 1)
                        last = nc.vector.tensor_scalar(tiles(xn, r), rows[:, i, :], k.mean[:, i], k.rstd[:, i],
                                                       ALU.subtract, ALU.mult)
                    last.then_inc(normed.sem, 1)
                if live(s - 2):
                    dve.wait_ge(scored.sem, scored.at(s - 2))
                    nc.vector.tensor_copy(score[:, group(s - 2), :],
                                          bank_l[odd][:, 0:GR * E].rearrange("p (r e) -> p r e", e=E)
                                          ).then_inc(kept.sem, 1)
            pipelined(dve, 2, step)

        @block.tensor
        def _(pe):
            turned.start(pe)
            scored.start(pe)

            def step(s, odd):
                if live(s):
                    pe.wait_ge(normed.sem, normed.at(s))
                    pe.wait_ge(copied.sem, copied.at(s - 1))
                    for r in range(GR):
                        last = nc.tensor.transpose(tiles(bank_t, r), tiles(xn, r), k.ident[:, :])
                    last.then_inc(turned.sem, 1)
                if live(s - 1):
                    b = 1 - odd
                    pe.wait_ge(copied.sem, copied.at(s - 1))
                    pe.wait_ge(kept.sem, kept.at(s - 3))
                    for r in range(GR):
                        last = nc.tensor.matmul(bank_l[b][:, r * E:(r + 1) * E], tiles(xT[:, b, :], r), k.gate_w[:, :],
                                                start=True, stop=True)
                    last.then_inc(scored.sem, 1)
            pipelined(pe, 1, step)

        @block.scalar
        def _(act):
            copied.start(act)

            def step(s, odd):
                act.wait_ge(turned.sem, turned.at(s))
                act.wait_ge(scored.sem, scored.at(s - 2))
                if affine:
                    ins = nc.scalar.activation(xT[:, odd, :], bank_t[:, :], ACT.Identity, bias=k.ln2_b[:, 0:1],
                                               scale=k.ln2_w[:, 0:1])
                else:
                    ins = nc.scalar.copy(xT[:, odd, :], bank_t[:, :])
                ins.then_inc(copied.sem, 1)
            pipelined(act, 0, step)

    w = m.sb(name + "_work", [P, 4, RT, E])
    n = m.sb(name + "_narrow", [P, 6, RT])
    prefer = m.sb(name + "_prefer", [P, E])
    ready = m.sem(name + "_prefer_ready")
    chosen, powered = m.sem(name + "_chosen"), m.sem(name + "_powered")
    with nc.Block() as block:
        @block.gpsimd
        def _(pool):
            nc.gpsimd.iota(prefer[:, :], [[-1, E]], base=E, channel_multiplier=0, allow_small_or_imprecise_dtypes=True
                           ).then_inc(ready, 1)

        @block.vector
        def _(dve):
            v, at = nc.vector, [0]

            def link(ins):
                at[0] += 1
                ins.then_inc(chosen, 1)
                dve.wait_ge(chosen, at[0])

            def wide(a):
                return a.unsqueeze(2).broadcast_to([P, RT, E])

            def pick(scores, top, out):
                link(v.tensor_reduce(top, scores, AX.X, ALU.max))
                link(v.tensor_tensor(w[:, 2, :, :], scores, wide(top), ALU.is_equal))
                link(v.tensor_tensor(w[:, 2, :, :], w[:, 2, :, :], prefer[:, :].unsqueeze(1).broadcast_to([P, RT, E]),
                                     ALU.mult))
                link(v.tensor_reduce(n[:, 5, :], w[:, 2, :, :], AX.X, ALU.max))
                link(v.tensor_tensor(out, w[:, 2, :, :], wide(n[:, 5, :]), ALU.is_equal))

            dve.wait_ge(ready, 1)
            pick(score[:, :, :], n[:, 0, :], moe.pick[0][:, :, :])
            if not top2:
                return
            link(v.scalar_tensor_tensor(w[:, 3, :, :], moe.pick[0][:, :, :], -3e38, score[:, :, :], ALU.mult, ALU.add))
            pick(w[:, 3, :, :], n[:, 1, :], moe.pick[1][:, :, :])
            link(v.tensor_tensor(n[:, 2, :], n[:, 1, :], n[:, 0, :], ALU.subtract))
            dve.wait_ge(powered, 1)
            link(v.tensor_scalar(n[:, 4, :], n[:, 3, :], 1.0, None, ALU.add))
            link(v.reciprocal(moe.share[0][:, :], n[:, 4, :]))
            link(v.tensor_tensor(moe.share[1][:, :], moe.share[0][:, :], n[:, 3, :], ALU.mult))

        if top2:
            @block.scalar
            def _(act):
                act.wait_ge(chosen, 12)
                nc.scalar.activation(n[:, 3, :], n[:, 2, :], ACT.Exp).then_inc(powered, 1)



class Moe:
    CAP = TOK + GT

    def __init__(self, E, top, NK, gated, affine, extra):
        self.E, self.top, self.NK, self.gated, self.affine, self.extra = E, top, NK, gated, affine, extra
        self.W = C + extra + 1
        self.fill = top * TOK // GT
        self.NT = (top * TOK + E * (GT - 1)) // GT
        self.spare = self.NT - self.fill
        self.rows = E * self.CAP + self.spare * GT
        self.dst_rows = top * TOK + (E + self.spare) * GT


def fresh(kind):
    if kind == "B":
        return Moe(8, 2, 2, False, False, 1)
    return Moe(4, 1, 4, True, True, C)


def place(m, k, moe):
    nc = m.nc
    E, NT, top, CAP, W = moe.E, moe.NT, moe.top, moe.CAP, moe.W
    name = f"place{E}"
    sb = lambda n, shape, dt=F32: m.sb(f"{name}_{n}", shape, dt)
    moe.slot = [sb(f"slot{i}", [P, RT]) for i in range(top)]
    moe.token = sb("token", [P, RT])
    fill_row = sb("fill_row", [1, E], mybir.dt.int32)
    both = sb("both", [P, RT, E], BF16)
    before, ones = sb("before", [P, P], BF16), sb("ones", [P, P], BF16)
    cum = sb("cum", [P, 2, RT, E])
    w = sb("w", [P, RT, E])
    base = sb("base", [P, E])
    steps_512 = sb("steps_512", [P, RT // GR])
    tile_no = sb("tile_no", [P, NT])
    over = sb("over", [P, E, RT // GR])
    n, start = sb("n", [P, E]), sb("start", [P, E + 1])
    end_row, jump = sb("end_row", [P, E]), sb("jump", [P, E])
    ge, gj = sb("ge", [P, NT, E]), sb("gj", [P, NT, E])
    te, tr, tr2 = sb("te", [P, NT]), sb("tr", [P, NT]), sb("tr2", [P, NT])
    pad = sb("pad", [P, E + moe.spare, GR, W])
    bank_p, bank_n = k.bank[0], k.bank[1]
    zeroed, made, steps, ranked, filled = (m.sem(f"{name}_{n}") for n in ("zeroed", "made", "steps", "ranked", "filled"))
    TABLES = 8

    with nc.Block() as block:
        @block.gpsimd
        def _(pool):
            def iota(t, pattern, start, per_partition=0):
                nc.gpsimd.iota(t, pattern, base=start, channel_multiplier=per_partition,
                               allow_small_or_imprecise_dtypes=True).then_inc(made, 1)
            nc.gpsimd.memset(before[:, :], 1.0).then_inc(zeroed, 1)
            nc.gpsimd.memset(ones[:, :], 1.0).then_inc(made, 1)
            iota(base[:, :], [[CAP, E]], 0)
            iota(steps_512[:, :], [[GT, RT // GR]], 0)
            iota(tile_no[:, :], [[1, NT]], 0)
            iota(moe.token[:, :], [[P, RT]], 0, 1)
            nc.gpsimd.memset(start[:, :], 0.0).then_inc(made, 1)
            pool.wait_ge(zeroed, 1)
            nc.gpsimd.affine_select(out=before[:, :], in_=before[:, :], compare_op=ALU.is_gt, fill=0.0, base=0,
                                    pattern=[[1, P]], channel_multiplier=-1).then_inc(made, 1)
            nc.gpsimd.memset(pad[:, :, :, 0:W - 1], 0.0).then_inc(made, 1)
            iota(pad[:, :, :, W - 1], [[GT, E + moe.spare], [P, GR]], top * TOK, 1)

        @block.vector
        def _(dve):
            v, at = nc.vector, [0]

            def link(ins):
                at[0] += 1
                ins.then_inc(steps, 1)
                dve.wait_ge(steps, at[0])

            def wide(a):
                return a.unsqueeze(1).broadcast_to([P, RT, E])
            if top == 2:
                link(v.tensor_tensor(both[:, :, :], moe.pick[0][:, :, :], moe.pick[1][:, :, :], ALU.add))
            else:
                link(v.tensor_copy(both[:, :, :], moe.pick[0][:, :, :]))
            dve.wait_ge(ranked, 2)
            dve.wait_ge(made, TABLES)
            totals = bank_n[:, 0:RT * E].rearrange("p (r e) -> p r e", e=E)
            link(v.tensor_copy(cum[:, 0, :, :], totals))
            a, d = 0, 1
            while d < RT:
                v.tensor_copy(cum[:, 1 - a, 0:d, :], cum[:, a, 0:d, :])
                link(v.tensor_tensor(cum[:, 1 - a, d:RT, :], cum[:, a, d:RT, :], cum[:, a, 0:RT - d, :], ALU.add))
                a, d = 1 - a, 2 * d
            total = cum[:, a, RT - 1, :]
            link(v.tensor_tensor(cum[:, 1 - a, :, :], cum[:, a, :, :], totals, ALU.subtract))
            link(v.tensor_tensor(w[:, :, :], cum[:, 1 - a, :, :],
                                 bank_p[:, 0:RT * E].rearrange("p (r e) -> p r e", e=E), ALU.add))
            link(v.tensor_tensor(cum[:, 1 - a, :, :], w[:, :, :], wide(base[:, :]), ALU.add))
            for i in range(top):
                link(v.tensor_tensor(w[:, :, :], cum[:, 1 - a, :, :], moe.pick[i][:, :, :], ALU.mult))
                link(v.tensor_reduce(moe.slot[i][:, :], w[:, :, :], AX.X, ALU.add))
            link(v.tensor_tensor(end_row[:, :], base[:, :], total, ALU.add))
            v.tensor_copy(fill_row[:, :], end_row[0:1, :]).then_inc(filled, 1)
            link(v.tensor_tensor(over[:, :, :], total.unsqueeze(2).broadcast_to([P, E, RT // GR]),
                                 steps_512[:, :].unsqueeze(1).broadcast_to([P, E, RT // GR]), ALU.is_gt))
            link(v.tensor_reduce(n[:, :], over[:, :, :], AX.X, ALU.add))
            for e in range(E):
                link(v.tensor_tensor(start[:, e + 1:e + 2], start[:, e:e + 1], n[:, e:e + 1], ALU.add))
            link(v.tensor_scalar(jump[:, :], n[:, :], -float(GT), float(CAP), ALU.mult, ALU.add))
            link(v.tensor_tensor(ge[:, :, :], tile_no[:, :].unsqueeze(2).broadcast_to([P, NT, E]),
                                 start[:, 1:E + 1].unsqueeze(1).broadcast_to([P, NT, E]), ALU.is_ge))
            link(v.tensor_tensor(gj[:, :, :], ge[:, :, :], jump[:, :].unsqueeze(1).broadcast_to([P, NT, E]), ALU.mult))
            link(v.tensor_reduce(te[:, :], ge[:, :, :], AX.X, ALU.add))
            link(v.tensor_reduce(tr[:, :], gj[:, :, :], AX.X, ALU.add))
            link(v.scalar_tensor_tensor(tr2[:, :], tile_no[:, :], float(GT), tr[:, :], ALU.mult, ALU.add))
            v.tensor_copy(moe.tile_row[:, :], tr2[0:1, :])
            v.tensor_scalar(moe.tile_expert[:, :], te[0:1, :], float(E - 1), None, ALU.min)

        @block.tensor
        def _(pe):
            pe.wait_ge(steps, 1)
            pe.wait_ge(made, TABLES)
            flat = both[:, :, :].rearrange("p r e -> p (r e)")
            nc.tensor.matmul(bank_p[:, 0:RT * E], before[:, :], flat, start=True, stop=True).then_inc(ranked, 1)
            nc.tensor.matmul(bank_n[:, 0:RT * E], ones[:, :], flat, start=True, stop=True).then_inc(ranked, 1)

        @block.sync
        def _(sp):
            written = m.sem(name + "_written")
            sp.wait_ge(made, TABLES + 1)
            for s in range(moe.spare):
                at = E * CAP + s * GT
                sp.dma_start(moe.dram_rows[at:at + GT, :].rearrange("(r p) w -> p r w", p=P), pad[:, E + s, :, :]
                             ).then_inc(written, 16)
            sp.wait_ge(filled, 1)
            for e in range(E):
                at = sp.value_load(fill_row[0:1, e:e + 1], min_val=e * CAP, max_val=e * CAP + TOK)
                sp.dma_start(moe.dram_rows[bass.ds(at, GT), :].rearrange("(r p) w -> p r w", p=P), pad[:, e, :, :]
                             ).then_inc(written, 16)
            sp.wait_ge(written, 16 * (E + moe.spare))


def scatter(m, k, moe, rows):
    nc = m.nc
    top, W, E = moe.top, moe.W, moe.E
    name = f"scatter{E}"
    row = m.sb(name + "_row", [P, 2, top, GR, W])
    index = [[[m.sb(f"{name}_index{b}{i}{r}", [P, 1], mybir.dt.int32) for r in range(GR)] for i in range(top)]
             for b in range(2)]
    normed, labelled = m.count(name + "_normed"), m.count(name + "_labelled")
    sent = [m.sem(f"{name}_sent{b}") for b in range(2)]
    begun = m.sem(name + "_begun")
    per = 16 * GR * top

    with nc.Block() as block:
        @block.vector
        def _(dve):
            normed.start(dve)

            def step(s, odd):
                if not isinstance(s, int) or s >= 2:
                    dve.wait_ge(sent[odd], (s - odd) * (per // 2))
                for r in range(GR):
                    at = bass.ds(s * GR + r, 1)
                    nc.vector.tensor_scalar(row[:, odd, 0, r, 0:C], rows[:, at, :], k.mean[:, at], k.rstd[:, at],
                                            ALU.subtract, ALU.mult)
                    for i in range(top):
                        last = nc.vector.tensor_copy(index[odd][i][r][:, :], moe.slot[i][:, at])
                last.then_inc(normed.sem, 1)
            pipelined(dve, 0, step)

        @block.scalar
        def _(act):
            labelled.start(act)

            def step(s, odd):
                if not isinstance(s, int) or s >= 2:
                    act.wait_ge(sent[odd], (s - odd) * (per // 2))
                if moe.extra == C:
                    last = nc.scalar.copy(row[:, odd, 0, :, C:2 * C], k.x[:, group(s), :])
                for i in range(top):
                    if moe.extra == 1:
                        last = nc.scalar.copy(row[:, odd, i, :, C], moe.share[i][:, group(s)])
                    last = nc.scalar.activation(row[:, odd, i, :, W - 1], moe.token[:, group(s)], ACT.Copy,
                                                bias=float(i * TOK))
                if top == 2:
                    act.wait_ge(normed.sem, normed.at(s))
                    last = nc.scalar.copy(row[:, odd, 1, :, 0:C], row[:, odd, 0, :, 0:C])
                last.then_inc(labelled.sem, 1)
            pipelined(act, 0, step)

        @block.gpsimd
        def _(pool):
            def step(s, odd):
                pool.wait_ge(normed.sem, normed.at(s))
                pool.wait_ge(labelled.sem, labelled.at(s))
                pool.sem_inc(begun, 1)
                for i in range(top):
                    for r in range(GR):
                        pool.indirect_dma_start(moe.dram_rows[:, :],
                                                bass.IndirectOffsetOnAxis(ap=index[odd][i][r][:, 0:1], axis=0),
                                                row[:, odd, i, r, :], None).then_inc(sent[odd], 16)
            pipelined(pool, 0, step)
            for b in range(2):
                pool.wait_ge(sent[b], NG // 2 * per)


def run_tiles(m, k, moe, up_dram, down_dram):
    nc = m.nc
    E, NK, NT, W, gated = moe.E, moe.NK, moe.NT, moe.W, moe.gated
    HU = NK * P * (2 if gated else 1)
    name = f"tile{E}"
    rows = m.sb(name + "_rows", [P, 4, GR, W])
    up_w, down_w = m.sb(name + "_up", [P, 2, HU]), m.sb(name + "_down", [P, 4, NK, C])
    xT = m.sb(name + "_xT", [P, 2, GT])
    silu = m.sb(name + "_silu", [P, 2, GT])
    hidden = m.sb(name + "_hidden", [P, 2, NK, GT])
    y = m.sb(name + "_y", [P, 4, GR, C])
    index = [[m.sb(f"{name}_index{q}{r}", [P, 1], mybir.dt.int32) for r in range(GR)] for q in range(4)]
    bank_t, bank_g, bank_u, bank_y = k.bank[0], k.bank[1:3], k.bank[3:5], k.bank[5:7]
    rows_loaded = [m.sem(f"{name}_rows_loaded{q}") for q in range(4)]
    up_loaded = [m.sem(f"{name}_up_loaded{b}") for b in range(2)]
    down_loaded = [m.sem(f"{name}_down_loaded{q}") for q in range(4)]
    sent = [m.sem(f"{name}_sent{q}") for q in range(4)]
    turned, copied = m.count(name + "_turned", 1, NT), m.count(name + "_copied", 1, NT)
    raised, silued = m.count(name + "_raised", NK, NT), m.count(name + "_silued", NK, NT)
    bent = m.count(name + "_bent", NK, NT) if gated else silued
    lowered = m.count(name + "_lowered", 1, NT)
    begun = m.sem(name + "_begun")
    finished = m.count(name + "_finished", 1, NT)

    def loads(t, b, per=16, buffers=2):
        return (t - b) * (per // buffers) + per

    with nc.Block() as block:
        @block.sync
        def _(sp):
            def load_rows(t, q):
                if not live(t, NT):
                    return
                at = sp.value_load(moe.tile_row[0:1, bass.ds(t, 1)], min_val=0, max_val=moe.rows - GT)
                if not isinstance(t, int) or t >= 4:
                    sp.wait_ge(turned.sem, turned.at(t - 4))
                    sp.wait_ge(finished.sem, finished.at(t - 4))
                sp.dma_start(rows[:, q, :, :], moe.dram_rows[bass.ds(at, GT), :].rearrange("(r p) w -> p r w", p=P)
                             ).then_inc(rows_loaded[q], 16)

            def load_weights(t, q):
                b = q % 2
                if not live(t, NT):
                    return
                e = sp.value_load(moe.tile_expert[0:1, bass.ds(t, 1)], min_val=0, max_val=E - 1)
                sp.wait_ge(raised.sem, raised.at(t - 2))
                sp.dma_start(up_w[:, b:b + 1, :], up_dram[bass.ds(e, 1), :, :].rearrange("e c h -> c e h")
                             ).then_inc(up_loaded[b], 16)
                if not isinstance(t, int) or t >= 4:
                    sp.wait_ge(lowered.sem, lowered.at(t - 4))
                sp.dma_start(down_w[:, q, :, :], down_dram[bass.ds(e, 1), :, :].rearrange("e (k h) c -> h (e k) c", h=P)
                             ).then_inc(down_loaded[q], 16)

            def step(s, q):
                load_rows(s, q)
                load_weights(s - 1, (q - 1) % 4)
            pipelined(sp, 1, step, NT, 4)

        @block.tensor
        def _(pe):
            for c in (turned, raised, lowered):
                c.start(pe)

            def turn(t, q):
                if not live(t, NT):
                    return
                pe.wait_ge(rows_loaded[q], loads(t, q, 16, 4))
                pe.wait_ge(copied.sem, copied.at(t - 1))
                for r in range(GR):
                    last = nc.tensor.transpose(tiles(bank_t, r), rows[:, q, r, 0:C], k.ident[:, :])
                last.then_inc(turned.sem, 1)

            def up(t, b, j):
                if not live(t, NT):
                    return
                i = (b * NK + j) % 2
                if j == 0:
                    pe.wait_ge(up_loaded[b], loads(t, b))
                    pe.wait_ge(copied.sem, copied.at(t))
                pe.wait_ge(bent.sem, bent.at(t, j - 1))
                last = nc.tensor.matmul(bank_g[i][:, :], up_w[:, b, j * P:(j + 1) * P], xT[:, b, :],
                                        start=True, stop=True)
                if gated:
                    last = nc.tensor.matmul(bank_u[i][:, :], up_w[:, b, (NK + j) * P:(NK + j + 1) * P], xT[:, b, :],
                                            start=True, stop=True)
                last.then_inc(raised.sem, 1)

            def down(t, q, j):
                b = q % 2
                if not live(t, NT):
                    return
                if j == 0:
                    pe.wait_ge(down_loaded[q], loads(t, q, 16, 4))
                    pe.wait_ge(finished.sem, finished.at(t - 2))
                pe.wait_ge(bent.sem, bent.at(t, j + 1))
                for r in range(GR):
                    last = nc.tensor.matmul(tiles(bank_y[b], r), tiles(hidden[:, b, j, :], r), down_w[:, q, j, :],
                                            start=j == 0 and r == 0, stop=j == NK - 1, skip_group_check=True)
                if j == NK - 1:
                    last.then_inc(lowered.sem, 1)

            def step(s, q):
                odd = q % 2
                for j in range(NK):
                    up(s - 1, 1 - odd, j)
                    if j == 0:
                        turn(s, q)
                    down(s - 2, (q - 2) % 4, j)
            pipelined(pe, 2, step, NT, 4)

        @block.scalar
        def _(act):
            copied.start(act)
            silued.start(act)

            def copy(t, b):
                if not live(t, NT):
                    return
                act.wait_ge(turned.sem, turned.at(t))
                act.wait_ge(raised.sem, raised.at(t - 2))
                if moe.affine:
                    ins = nc.scalar.activation(xT[:, b, :], bank_t[:, :], ACT.Identity, bias=k.ln2_b[:, 0:1],
                                               scale=k.ln2_w[:, 0:1])
                else:
                    ins = nc.scalar.copy(xT[:, b, :], bank_t[:, :])
                ins.then_inc(copied.sem, 1)

            def activate(t, b, j):
                if not live(t, NT):
                    return
                i = (b * NK + j) % 2
                act.wait_ge(raised.sem, raised.at(t, j + 1))
                if gated:
                    act.wait_ge(bent.sem, bent.at(t, j - 1))
                    dst = silu[:, i, :]
                else:
                    act.wait_ge(lowered.sem, lowered.at(t - 2))
                    dst = hidden[:, b, j, :]
                nc.scalar.activation(dst, bank_g[i][:, :], ACT.Silu).then_inc(silued.sem, 1)

            def step(s, q):
                odd = q % 2
                for j in range(NK):
                    activate(s - 1, 1 - odd, j)
                    if j == 0:
                        copy(s, odd)
            pipelined(act, 1, step, NT, 4)

        @block.vector
        def _(dve):
            finished.start(dve)
            if gated:
                bent.start(dve)

            def finish(t, q):
                b = q % 2
                if not live(t, NT):
                    return
                dve.wait_ge(lowered.sem, lowered.at(t))
                if not isinstance(t, int) or t >= 4:
                    dve.wait_ge(sent[q], loads(t, q, 16 * GR, 4) - 16 * GR)
                for r in range(GR):
                    nc.vector.tensor_copy(index[q][r][:, :], rows[:, q, r, W - 1:W])
                bank = bank_y[b][:, :].rearrange("p (r c) -> p r c", c=C)
                if moe.extra == 1:
                    last = nc.vector.tensor_tensor(y[:, q, :, :], bank, rows[:, q, :, C:C + 1].broadcast_to([P, GR, C]),
                                                   ALU.mult)
                else:
                    last = nc.vector.tensor_tensor(y[:, q, :, :], bank, rows[:, q, :, C:2 * C], ALU.add)
                last.then_inc(finished.sem, 1)

            def bend(t, b, j):
                if not live(t, NT):
                    return
                i = (b * NK + j) % 2
                dve.wait_ge(silued.sem, silued.at(t, j + 1))
                if j == 0:
                    dve.wait_ge(lowered.sem, lowered.at(t - 2))
                nc.vector.tensor_tensor(hidden[:, b, j, :], silu[:, i, :], bank_u[i][:, :], ALU.mult
                                        ).then_inc(bent.sem, 1)

            def step(s, q):
                odd = q % 2
                if gated:
                    for j in range(NK):
                        bend(s - 1, 1 - odd, j)
                finish(s - 2, (q - 2) % 4)
            pipelined(dve, 2, step, NT, 4)

        @block.gpsimd
        def _(pool):
            def step(s, q):
                pool.wait_ge(finished.sem, finished.at(s))
                pool.sem_inc(begun, 1)
                for r in range(GR):
                    pool.indirect_dma_start(moe.dst[:, :], bass.IndirectOffsetOnAxis(ap=index[q][r][:, 0:1], axis=0),
                                            y[:, q, r, :], None).then_inc(sent[q], 16)
            pipelined(pool, 0, step, NT, 4)
            for q in range(4):
                pool.wait_ge(sent[q], len(range(q, NT, 4)) * 16 * GR)


def combine(m, k, moe):
    nc = m.nc
    got = m.sb("combine_got", [P, 3, 2, GR, C])
    loaded = [m.sem(f"combine_loaded{b}") for b in range(2)]
    summed, added = m.count("combine_summed"), m.count("combine_added", 1)
    src = moe.dst[0:2 * TOK, :].rearrange("(i r p) c -> p i r c", i=2, p=P)
    with nc.Block() as block:
        @block.sync
        def _(sp):
            def step(s, odd):
                sp.wait_ge(summed.sem, summed.at(s - 2))
                for i in range(2):
                    sp.dma_start(got[:, odd, i, :, :], src[:, i, group(s), :]).then_inc(loaded[odd], 16)
            pipelined(sp, 0, step)

        @block.gpsimd
        def _(pool):
            summed.start(pool)

            def step(s, odd):
                pool.wait_ge(loaded[odd], (s - odd) * 16 + 32)
                pool.wait_ge(added.sem, added.at(s - 2))
                nc.gpsimd.tensor_tensor(got[:, 2, odd, :, :], got[:, odd, 0, :, :], got[:, odd, 1, :, :], ALU.add
                                        ).then_inc(summed.sem, 1)
            pipelined(pool, 0, step)

        @block.vector
        def _(dve):
            added.start(dve)

            def step(s, odd):
                dve.wait_ge(summed.sem, summed.at(s))
                x = k.x[:, group(s), :]
                nc.vector.tensor_tensor(x, got[:, 2, odd, :, :], x, ALU.add).then_inc(added.sem, 1)
                dve.wait_ge(added.sem, added.at(s))
                for r in range(GR):
                    at = bass.ds(s * GR + r, 1)
                    nc.vector.bn_stats(k.stats[:, at, :], k.x[:, at, :])
            pipelined(dve, 0, step)


def phase_b(m, k, dram):
    moe = fresh("B")
    moe.tile_expert, moe.tile_row = (m.sb(f"tile_{n}_b", [1, moe.NT], mybir.dt.int32) for n in ("expert", "row"))
    moe.dram_rows, moe.dst = dram["rows_b"], dram["results_b"]
    with ExitStack() as own:
        mine = Machine(m.nc, own)
        gate(mine, k, moe, k.x)
        place(mine, k, moe)
        scatter(mine, k, moe, k.x)
        mine.clear()
    run_tiles(m, k, moe, dram["L0_ffn_W1"], dram["L0_ffn_W2"])
    combine(m, k, moe)


def phase_e(m, k, dram):
    moe = fresh("E")
    moe.tile_expert, moe.tile_row = (m.sb(f"tile_{n}_e", [1, moe.NT], mybir.dt.int32) for n in ("expert", "row"))
    moe.dram_rows, moe.dst = dram["rows_e"], dram["out"]
    with ExitStack() as own:
        mine = Machine(m.nc, own)
        gate(mine, k, moe, k.u)
        place(mine, k, moe)
        scatter(mine, k, moe, k.u)
        mine.clear()
    run_tiles(m, k, moe, dram["L1_ffn_expert_wv"], dram["L1_ffn_expert_proj"])


PHASES = {"A": phase_a, "B": phase_b, "C": phase_c, "D": phase_d, "E": phase_e}


def build(nc, dram, out, phases="ABCDE"):
    b = fresh("B")
    dram = dict(dram, out=out, rows_b=nc.dram_tensor("rows_b", [b.rows, b.W], F32, kind="Internal").ap(),
                results_b=nc.dram_tensor("results_b", [b.dst_rows, C], F32, kind="Internal").ap(),
                rows_e=nc.dram_tensor("rows_e", [fresh("E").rows, fresh("E").W], F32, kind="Internal").ap())
    with ExitStack() as ctx:
        m = Machine(nc, ctx)

        class Kept:
            pass
        k = Kept()
        k.x = m.sb("x_rows", [P, RT, C])
        k.u = m.sb("u_rows", [P, RT, C])
        k.stats = m.sb("stats", [P, RT, 6])
        k.mean = m.sb("mean", [P, RT])
        k.rstd = m.sb("rstd", [P, RT])
        k.rstd2 = m.sb("rstd2", [P, RT])
        k.work = m.sb("work", [P, 10, RT])
        k.eps = m.sb("eps", [P, 1])
        k.bank = [m.psum(f"bank{i}") for i in range(8)]
        k.ident = m.sb("ident", [P, P])
        k.ident_bf = m.sb("ident_bf", [P, P], BF16)
        load_phase(m, k, dram)
        for phase in phases:
            with ExitStack() as own:
                mine = Machine(nc, own)
                constants(mine, k, dram, phase)
                statistics(mine, k, phase)
                PHASES[phase](mine, k, dram)
                mine.clear()
        if phases[-1] == "E":
            return
        stored = m.sem("stored")
        with nc.Block() as block:
            @block.sync
            def _(sp):
                sp.dma_start(dram["out"][0:TOK, :].rearrange("(r p) c -> p r c", p=P), k.x[:, :, :]).then_inc(stored, 16)
                sp.wait_ge(stored, 16)




def shape_tables():
    import numpy as np
    f32 = np.float32
    pos = np.arange(SEQ, dtype=f32)
    half = C // 2
    scale = ((np.arange(0, C, 2, dtype=f32) + f32(0.4 * C)) / f32(1.4 * C))[None, :] ** (pos / f32(512.0))[:, None]
    freqs = f32(1.0) / f32(10000.0) ** (np.arange(half, dtype=f32) / f32(half))
    angle = pos[:, None] * freqs[None, :]
    cos, sin = np.cos(angle), np.sin(angle)
    rope_a = np.stack([np.repeat(t, 2, axis=1).T for t in (cos * scale, sin * scale, cos / scale, sin / scale)], 1)
    tok = np.arange(P)
    same = (tok[:, None] // SEQ) == (tok[None, :] // SEQ)
    diff = (tok[None, :] - tok[:, None]).astype(f32)
    decay = np.where(same & (diff >= 0), f32(0.96875) ** np.maximum(diff, 0), f32(0.0)).astype(f32)
    causal = tok[:, None] >= tok[None, :]
    self_mask = np.where(same & causal, f32(0), f32(MASKED))
    cross_mask = np.where(same, f32(0), f32(MASKED))
    head_mask = np.where((tok[:, None] % SEQ) >= np.arange(SEQ)[None, :], f32(0), f32(MASKED))
    masks = np.stack([np.tile(self_mask, (1, GR)), np.tile(cross_mask, (1, GR)), np.tile(head_mask, (1, 8))], 1)
    inv = f32(1.0) / f32(10000.0) ** (np.arange(0, 8, 2, dtype=f32) / f32(8))
    emb = np.concatenate([pos[:, None] * inv[None, :]] * 2, axis=1)
    rope_d = np.stack([np.tile(np.cos(emb).T, (16, 1)), np.tile(np.sin(emb).T, (16, 1))], 1)
    return {n: np.ascontiguousarray(t.astype(f32)) for n, t in
            (("rope_a", rope_a), ("decay", decay), ("masks", masks), ("rope_d", rope_d))}


def kernel(**inputs):
    import numpy as np
    import concourse.bacc as bacc
    from concourse.bass_utils import run_bass_kernel_spmd

    nc = bacc.Bacc("TRN2", target_bir_lowering=False, num_devices=1)
    arrays = {n: np.ascontiguousarray(a) for n, a in inputs.items()} | shape_tables()
    dram = {n: nc.dram_tensor(n + "_dram", a.shape, mybir.dt.from_np(a.dtype), kind="ExternalInput").ap()
            for n, a in arrays.items()}
    out = nc.dram_tensor("out_dram", [fresh("E").dst_rows, C], F32, kind="ExternalOutput").ap()
    build(nc, dram, out)
    got = run_bass_kernel_spmd(nc, [{n + "_dram": a for n, a in arrays.items()}], core_ids=[0])
    return got.results[0]["out_dram"][:TOK].reshape(BATCHES, SEQ, C)
```

```python
import concourse.bass as bass
from concourse import mybir
from contextlib import ExitStack

F32 = mybir.dt.float32
BF16 = mybir.dt.bfloat16
F32R = mybir.dt.float32r
ALU = mybir.AluOpType
ACT = mybir.ActivationFunctionType
AX = mybir.AxisListType

P = 128
C = 128
BATCHES = 128
SEQ = 64
TOK = BATCHES * SEQ
RT = TOK // P
GR = 4
GT = GR * P
NG = TOK // GT
GB = GT // SEQ
EPS = 1e-5
MASKED = -1e30


def pipelined(eng, depth, step, n=NG, unroll=2, peeled=0):
    head = depth + (n - depth) % unroll
    while head < peeled:
        head += unroll
    for s in range(head):
        step(s, s % unroll)
    with eng.Fori(head, n - unroll + 1, unroll) as s:
        for i in range(unroll):
            step(s + i, (head + i) % unroll)
    for s in range(n, n + depth):
        step(s, s % unroll)


def live(t, n=NG):
    return not isinstance(t, int) or 0 <= t < n


def group(t):
    return bass.ds(t * GR, GR)


class Count:

    def __init__(self, sem, per=1, n=NG):
        self.sem, self.per, self.n = sem, per, n

    def start(self, eng):
        eng.sem_inc(self.sem, 2 * self.per)

    def at(self, t, done=None):
        if isinstance(t, int) and t >= self.n:
            t, done = self.n - 1, self.per
        return (t + 2) * self.per + (self.per if done is None else done)


class Machine:

    def __init__(self, nc, ctx):
        self.nc, self.ctx, self.sems = nc, ctx, []

    def sb(self, name, shape, dt=F32):
        return self.ctx.enter_context(self.nc.sbuf_tensor(name, shape, dt))

    def psum(self, name, shape=(P, 512), dt=F32):
        return self.ctx.enter_context(self.nc.psum_tensor(name, list(shape), dt))

    def sem(self, name):
        self.sems.append(self.nc.alloc_semaphore(name))
        return self.sems[-1]

    def clear(self):
        self.nc.all_engine_barrier()
        self.nc.clear_and_free_semaphores(self.sems)
        self.nc.all_engine_barrier()

    def count(self, name, per=1, n=NG):
        return Count(self.sem(name), per, n)


def tiles(buf, r):
    return buf[:, r * P:(r + 1) * P]


def over_batches(table):
    return table.unsqueeze(1).broadcast_to([P, GB, SEQ])


def by_batch(buf):
    return buf.rearrange("p (b s) -> p b s", s=SEQ)


def newton_rsqrt(vec, link, var, guess, a, b, out):
    link(vec.scalar_tensor_tensor(a, var, EPS, guess, ALU.add, ALU.mult))
    link(vec.scalar_tensor_tensor(b, a, -0.5, guess, ALU.mult, ALU.mult))
    link(vec.scalar_tensor_tensor(out, b, 1.5, guess, ALU.add, ALU.mult))


def moments(vec, link, st, tmp, mean, var):
    total, apart, squares, spread = tmp
    vec.tensor_tensor(total, st[:, :, 1], st[:, :, 4], ALU.add)
    vec.tensor_tensor(apart, st[:, :, 1], st[:, :, 4], ALU.subtract)
    link(vec.tensor_tensor(squares, st[:, :, 2], st[:, :, 5], ALU.add))
    vec.tensor_scalar(mean, total, 0.5, None, ALU.mult)
    link(vec.scalar_tensor_tensor(spread, apart, 0.25, apart, ALU.mult, ALU.mult))
    link(vec.scalar_tensor_tensor(var, squares, 1.0 / C, spread, ALU.mult, ALU.add))


def constants(m, k, dram, phase):
    k.loads = []

    def load(name, shape, src):
        t = m.sb(name, shape)
        k.loads.append((t[:], src))
        return t

    def row(name, key):
        return load(name, [P, P], dram[key].unsqueeze(0).broadcast_to([P, P]))

    if phase == "A":
        k.w_qk = m.sb("w_qk", [P, 4, P])
        k.loads += [(k.w_qk[:, 0, :], dram["L0_xattn_Wq"]), (k.w_qk[:, 2, :], dram["L0_xattn_Wk"])]
        k.wv = load("wv", [P, P], dram["L0_xattn_Wv"])
        k.rope_a = load("rope_a", [P, 4, SEQ], dram["rope_a"])
        k.decay = load("decay", [P, P], dram["decay"])
    if phase == "B":
        k.gate_w = load("gate1_w", [P, 8], dram["L0_ffn_Wg"])
    if phase == "C":
        k.w1 = load("w1", [P, 512], dram["L1_xattn_w1"])
        k.w2 = load("w2", [P, 4, P], dram["L1_xattn_w2"].rearrange("(k h) c -> h k c", h=P))
        k.b1 = load("b1", [P, 4], dram["L1_xattn_b1"].rearrange("(k h) -> h k", h=P))
        k.b2 = row("b2", "L1_xattn_b2")
        k.gamma = [row(f"gamma{i}", f"L1_xattn_g{i}") for i in (1, 2, 3)]
        k.beta = [row(f"beta{i}", f"L1_xattn_beta{i}") for i in (1, 2, 3)]
        k.masks = load("masks_c", [P, 2, GT], dram["masks"][:, 0:2, :])
        k.masks_bf = m.sb("masks_c_bf", [P, 2, GT], BF16)
    if phase == "D":
        k.ln1_w = load("ln1_w", [P, 1], dram["L1_ffn_ln1_w"].unsqueeze(1))
        k.ln1_b = load("ln1_b", [P, 1], dram["L1_ffn_ln1_b"].unsqueeze(1))
        k.conv = load("conv", [P, 3], dram["L1_ffn_conv_w"].rearrange("c a k -> c (a k)"))
        k.qkv = load("qkv", [P, 3, P], dram["L1_ffn_attn_w"].rearrange("c (j n) -> c j n", j=3))
        k.qk_rot = m.sb("qk_rot", [P, 2, P])
        k.rope_d = load("rope_d", [P, 2, SEQ], dram["rope_d"])
        k.proj = load("proj", [P, P], dram["L1_ffn_proj_w"])
        k.masks = load("masks_d", [P, 1, GT], dram["masks"][:, 2:3, :])
        k.masks_bf = m.sb("masks_d_bf", [P, 1, GT], BF16)
    if phase == "E":
        k.ln2_w = load("ln2_w", [P, 1], dram["L1_ffn_ln2_w"].unsqueeze(1))
        k.ln2_b = load("ln2_b", [P, 1], dram["L1_ffn_ln2_b"].unsqueeze(1))
        k.gate_w = load("gate2_w", [P, 4], dram["L1_ffn_router_w"])


def prepare(nc, k, phase):
    if phase == "A":
        for j in (0, 2):
            src, dst = (k.w_qk[:, i, :].rearrange("p (i two) -> p i two", two=2) for i in (j, j + 1))
            nc.scalar.mul(dst[:, :, 0], src[:, :, 1], -1.0)
            nc.scalar.copy(dst[:, :, 1], src[:, :, 0])
    if phase == "D":
        for j in range(2):
            src, dst = (z[:, j, :].rearrange("p (h two d) -> p h two d", two=2, d=4) for z in (k.qkv, k.qk_rot))
            nc.scalar.mul(dst[:, :, 0, :], src[:, :, 1, :], -1.0)
            nc.scalar.copy(dst[:, :, 1, :], src[:, :, 0, :])
    if phase in "CD":
        nc.scalar.copy(k.masks_bf[:, :, :], k.masks[:, :, :])


def load_phase(m, k, dram):
    nc = m.nc
    CH = 8
    x_loaded = [m.sem(f"x_loaded{n}") for n in range(RT // CH)]
    zeroed, made = m.sem("ident_zeroed"), m.sem("ident_made")
    xs = dram["x"].rearrange("(r two) s c -> (two s) r c", two=2)
    with nc.Block() as block:
        @block.sync
        def _(sp):
            for n, loaded in enumerate(x_loaded):
                sp.dma_start(k.x[:, n * CH:(n + 1) * CH, :], xs[:, n * CH:(n + 1) * CH, :]).then_inc(loaded, 16)

        @block.gpsimd
        def _(pool):
            nc.gpsimd.memset(k.ident[:, :], 0.0).then_inc(zeroed, 1)
            nc.gpsimd.memset(k.ident_bf[:, :], 0.0).then_inc(zeroed, 1)
            nc.gpsimd.memset(k.eps[:, :], EPS)
            pool.wait_ge(zeroed, 2)
            for t in (k.ident, k.ident_bf):
                nc.gpsimd.affine_select(out=t[:, :], in_=t[:, :], compare_op=ALU.not_equal, fill=1.0, base=0,
                                        pattern=[[-1, P]], channel_multiplier=1).then_inc(made, 1)

        @block.vector
        def _(dve):
            for r in range(RT):
                if r % CH == 0:
                    dve.wait_ge(x_loaded[r // CH], 16)
                nc.vector.bn_stats(k.stats[:, r, :], k.x[:, r, :])


def statistics(m, k, phase):
    nc = m.nc
    twice = phase == "D"
    steps, guessed, loaded = (m.sem(f"stats_{phase}_{n}") for n in ("steps", "guessed", "loaded"))
    st, w = k.stats, k.work
    with nc.Block() as block:
        @block.sync
        def _(sp):
            with nc.allow_non_contiguous_dma(reason="columns of small vectors"):
                for t, src in k.loads:
                    sp.dma_start(t, src).then_inc(loaded, 16)

        @block.vector
        def _(dve):
            n = [0]

            def link(ins):
                n[0] += 1
                ins.then_inc(steps, 1)
                dve.wait_ge(steps, n[0])

            v = nc.vector
            moments(v, link, st, [w[:, i, :] for i in range(4)], k.mean[:, :], w[:, 4, :])
            dve.wait_ge(guessed, 2)
            newton_rsqrt(v, link, w[:, 4, :], w[:, 6, :], w[:, 7, :], w[:, 8, :], k.rstd[:, :])
            if twice:
                link(v.tensor_tensor(w[:, 0, :], k.rstd[:, :], k.rstd[:, :], ALU.mult))
                link(v.tensor_tensor(w[:, 1, :], w[:, 0, :], w[:, 4, :], ALU.mult))
                dve.wait_ge(guessed, 4)
                newton_rsqrt(v, link, w[:, 1, :], w[:, 3, :], w[:, 7, :], w[:, 8, :], w[:, 9, :])
                link(v.tensor_tensor(k.rstd2[:, :], w[:, 9, :], k.rstd[:, :], ALU.mult))

        @block.scalar
        def _(act):
            if phase != "B" and phase != "E":
                nc.scalar.preload_act_table_set("natural_log_exp_and_others")
            act.wait_ge(steps, 3)
            nc.scalar.activation(w[:, 5, :], w[:, 4, :], ACT.Ln, bias=k.eps[:, 0:1]).then_inc(guessed, 1)
            act.wait_ge(guessed, 1)
            nc.scalar.activation(w[:, 6, :], w[:, 5, :], ACT.Exp, scale=-0.5).then_inc(guessed, 1)
            if twice:
                act.wait_ge(steps, 8)
                nc.scalar.activation(w[:, 2, :], w[:, 1, :], ACT.Ln, bias=k.eps[:, 0:1]).then_inc(guessed, 1)
                act.wait_ge(guessed, 3)
                nc.scalar.activation(w[:, 3, :], w[:, 2, :], ACT.Exp, scale=-0.5).then_inc(guessed, 1)
            act.wait_ge(loaded, 16 * len(k.loads))
            prepare(nc, k, phase)


def phase_a(m, k, dram):
    nc = m.nc
    ctx = dram["ctx_1024"].rearrange("(r two) s c -> (two s) r c", two=2)
    xn, z = m.sb("a_xn", [P, 2, GT]), m.sb("a_z", [P, 2, GT])
    xT, zT = m.sb("a_xT", [P, 2, GT]), m.sb("a_zT", [P, 2, GT])
    w_high, w_rest = m.sb("a_w_high", [P, 4, P], F32R), m.sb("a_w_rest", [P, 4, P], F32R)
    high = m.sb("a_high", [P, 2, 2, GT], F32R)
    rest = m.sb("a_rest", [P, 2, 2, GT], F32R)
    v = m.sb("a_v", [P, 2, GT])
    part = m.sb("a_part", [P, 4, GT])
    qk = m.sb("a_qk", [P, 2, 2, GT])
    pm = m.sb("a_pm", [P, 2, GT])
    bank_t, bank_v, bank_s, bank_o = k.bank[0], k.bank[5], k.bank[6], k.bank[7]
    bank_qk = k.bank[1:5]

    z_loaded = [m.sem(f"a_z_loaded{b}") for b in range(2)]
    normed = m.count("a_normed")
    turned = m.count("a_turned", 2)
    w_split = m.sem("a_w_split")
    copied = m.count("a_copied", 2)
    rounded = m.count("a_rounded", 2)
    split = m.count("a_split", 2)
    projected = m.count("a_projected", 5)
    v_copied = m.count("a_v_copied")
    rotated = m.count("a_rotated", 4)
    summed = m.count("a_summed", 2)
    scored = m.count("a_scored")
    masked = m.count("a_masked")
    mixed = m.count("a_mixed")
    added = m.count("a_added")

    with nc.Block() as block:
        @block.sync
        def _(sp):
            def step(s, odd):
                sp.wait_ge(turned.sem, turned.at(s - 2))
                sp.dma_start(z[:, odd, :].rearrange("p (r c) -> p r c", c=C), ctx[:, group(s), :]
                             ).then_inc(z_loaded[odd], 16)
            pipelined(sp, 0, step)

        @block.vector
        def _(dve):
            for c in (normed, rotated, masked, added):
                c.start(dve)
            nc.vector.tensor_copy(w_high[:, :, :], k.w_qk[:, :, :]).then_inc(w_split, 1)
            dve.wait_ge(w_split, 1)
            nc.vector.tensor_tensor(w_rest[:, :, :], k.w_qk[:, :, :], w_high[:, :, :], ALU.subtract
                                    ).then_inc(w_split, 1)

            def norm(t, b):
                if not live(t):
                    return
                dve.wait_ge(turned.sem, turned.at(t - 2))
                for r in range(GR):
                    i = bass.ds(t * GR + r, 1)
                    last = nc.vector.tensor_scalar(tiles(xn[:, b, :], r), k.x[:, i, :], k.mean[:, i], k.rstd[:, i],
                                                   ALU.subtract, ALU.mult)
                last.then_inc(normed.sem, 1)

            def rotate(t, b):
                if not live(t):
                    return
                for j in range(4):
                    dve.wait_ge(projected.sem, projected.at(t, j + 1))
                    if j % 2 == 0:
                        dve.wait_ge(summed.sem, summed.at(t - 1, j // 2 + 1))
                    nc.vector.tensor_tensor(by_batch(part[:, j, :]), by_batch(bank_qk[j][:, :]),
                                            over_batches(k.rope_a[:, j, :]), ALU.mult).then_inc(rotated.sem, 1)

            def mask(t, b):
                if not live(t):
                    return
                dve.wait_ge(scored.sem, scored.at(t))
                dve.wait_ge(mixed.sem, mixed.at(t - 2))
                nc.vector.tensor_tensor(pm[:, b, :].rearrange("p (r q) -> p r q", q=P),
                                        bank_s[:, :].rearrange("p (r q) -> p r q", q=P),
                                        k.decay[:, :].unsqueeze(1).broadcast_to([P, GR, P]), ALU.mult
                                        ).then_inc(masked.sem, 1)

            def add(t, b):
                if not live(t):
                    return
                dve.wait_ge(mixed.sem, mixed.at(t))
                x = k.x[:, group(t), :]
                nc.vector.tensor_tensor(x, bank_o[:, :].rearrange("p (r c) -> p r c", c=C), x, ALU.add
                                        ).then_inc(added.sem, 1)
                dve.wait_ge(added.sem, added.at(t))
                for r in range(GR):
                    i = bass.ds(t * GR + r, 1)
                    nc.vector.bn_stats(k.stats[:, i, :], k.x[:, i, :])

            def step(s, odd):
                rotate(s - 2, odd)
                mask(s - 3, 1 - odd)
                norm(s, odd)
                add(s - 3, 1 - odd)
            pipelined(dve, 3, step)

        @block.tensor
        def _(pe):
            for c in (turned, projected, scored, mixed):
                c.start(pe)

            def turn(t, b):
                if not live(t):
                    return
                pe.wait_ge(normed.sem, normed.at(t))
                pe.wait_ge(copied.sem, copied.at(t - 1))
                for r in range(GR):
                    last = nc.tensor.transpose(tiles(bank_t, r), tiles(xn[:, b, :], r), k.ident[:, :])
                last.then_inc(turned.sem, 1)

            def turn_z(t, b):
                if not live(t):
                    return
                pe.wait_ge(z_loaded[b], (t - b) * 8 + 16)
                pe.wait_ge(copied.sem, copied.at(t, 1))
                for r in range(GR):
                    last = nc.tensor.transpose(tiles(bank_t, r), tiles(z[:, b, :], r), k.ident[:, :])
                last.then_inc(turned.sem, 1)

            def project(t, b, n):
                if not live(t):
                    return
                pe.wait_ge(rounded.sem, rounded.at(t, n + 1))
                pe.wait_ge(split.sem, split.at(t, n + 1))
                for j in (2 * n, 2 * n + 1):
                    pe.wait_ge(rotated.sem, rotated.at(t - 1, j + 1))
                    bank = bank_qk[j][:, :]
                    nc.tensor.matmul(bank, w_high[:, j, :], rest[:, b, n, :], start=True, stop=False)
                    nc.tensor.matmul(bank, w_rest[:, j, :], high[:, b, n, :], start=False, stop=False)
                    nc.tensor.matmul(bank, w_high[:, j, :], high[:, b, n, :], start=False, stop=True
                                     ).then_inc(projected.sem, 1)

            def project_v(t, b):
                if not live(t):
                    return
                pe.wait_ge(v_copied.sem, v_copied.at(t - 1))
                for r in range(GR):
                    last = nc.tensor.matmul(tiles(bank_v, r), tiles(zT[:, b, :], r), k.wv[:, :], start=True, stop=True)
                last.then_inc(projected.sem, 1)

            def score(t, b):
                if not live(t):
                    return
                pe.wait_ge(summed.sem, summed.at(t))
                pe.wait_ge(masked.sem, masked.at(t - 1))
                for r in range(GR):
                    last = nc.tensor.matmul(tiles(bank_s, r), tiles(qk[:, b, 1, :], r), tiles(qk[:, b, 0, :], r),
                                            start=True, stop=True)
                last.then_inc(scored.sem, 1)

            def mix(t, b):
                if not live(t):
                    return
                pe.wait_ge(masked.sem, masked.at(t))
                pe.wait_ge(v_copied.sem, v_copied.at(t))
                pe.wait_ge(added.sem, added.at(t - 1))
                for r in range(GR):
                    last = nc.tensor.matmul(tiles(bank_o, r), tiles(pm[:, b, :], r), tiles(v[:, b, :], r),
                                            start=True, stop=True)
                last.then_inc(mixed.sem, 1)

            pe.wait_ge(w_split, 2)

            def step(s, odd):
                project(s - 2, odd, 0)
                turn(s - 1, 1 - odd)
                score(s - 3, 1 - odd)
                project(s - 2, odd, 1)
                turn_z(s - 1, 1 - odd)
                project_v(s - 2, odd)
                mix(s - 3, 1 - odd)
            pipelined(pe, 3, step)

        @block.scalar
        def _(act):
            for c in (copied, rounded, v_copied):
                c.start(act)

            def copy_turned(t, b):
                if not live(t):
                    return
                act.wait_ge(projected.sem, projected.at(t - 2))
                for j, dst in enumerate((xT, zT)):
                    act.wait_ge(turned.sem, turned.at(t, j + 1))
                    nc.scalar.copy(dst[:, b, :], bank_t[:, :]).then_inc(copied.sem, 1)
                    act.wait_ge(copied.sem, copied.at(t, j + 1))
                    nc.scalar.copy(high[:, b, j, :], dst[:, b, :]).then_inc(rounded.sem, 1)

            def copy_v(t, b):
                if not live(t):
                    return
                act.wait_ge(projected.sem, projected.at(t))
                act.wait_ge(mixed.sem, mixed.at(t - 2))
                nc.scalar.copy(v[:, b, :], bank_v[:, :]).then_inc(v_copied.sem, 1)

            def step(s, odd):
                copy_turned(s - 1, 1 - odd)
                copy_v(s - 2, odd)
            pipelined(act, 2, step)

        @block.gpsimd
        def _(pool):
            summed.start(pool)
            split.start(pool)

            def take_rest(t, b, j):
                if not live(t):
                    return
                pool.wait_ge(projected.sem, projected.at(t - 2))
                pool.wait_ge(rounded.sem, rounded.at(t, j + 1))
                nc.gpsimd.tensor_tensor(rest[:, b, j, :], (xT, zT)[j][:, b, :], high[:, b, j, :], ALU.subtract
                                        ).then_inc(split.sem, 1)

            def add_parts(t, b, j):
                if not live(t):
                    return
                pool.wait_ge(rotated.sem, rotated.at(t, 2 * j + 2))
                pool.wait_ge(scored.sem, scored.at(t - 2))
                nc.gpsimd.tensor_tensor(qk[:, b, j, :], part[:, 2 * j, :], part[:, 2 * j + 1, :], ALU.add
                                        ).then_inc(summed.sem, 1)

            def step(s, odd):
                for j in range(2):
                    add_parts(s - 1, 1 - odd, j)
                    take_rest(s, odd, j)
            pipelined(pool, 1, step)


class LayerNorm:

    def __init__(self, m, k, name, steps, first):
        self.m, self.k, self.nc, self.first = m, k, m.nc, first
        self.rows = m.sb(name + "_rows", [P, GT])
        self.unit = m.sb(name + "_unit", [P, GT])
        self.scaled = m.sb(name + "_scaled", [P, GT])
        self.stats = m.sb(name + "_stats", [P, GR, 6])
        self.mean, self.var = m.sb(name + "_mean", [P, GR]), m.sb(name + "_var", [P, GR])
        self.tmp = m.sb(name + "_tmp", [P, 6, GR])
        self.done = m.count(name + "_done", steps)
        self.guessed = m.count(name + "_guessed", 2)
        self.affine = m.count(name + "_affine", 2)

    def take(self, dve, t):
        c, nc = self.done, self.nc
        for r in range(GR):
            last = nc.vector.bn_stats(self.stats[:, r, :], tiles(self.rows, r))
        last.then_inc(c.sem, 1)
        dve.wait_ge(c.sem, c.at(t, self.first + 1))
        n = [self.first + 1]

        def link(ins):
            n[0] += 1
            ins.then_inc(c.sem, 1)
            dve.wait_ge(c.sem, c.at(t, n[0]))

        moments(nc.vector, link, self.stats, [self.tmp[:, i, :] for i in range(2, 6)], self.mean[:, :], self.var[:, :])

    def guess(self, act, t):
        act.wait_ge(self.done.sem, self.done.at(t, self.first + 4))
        self.nc.scalar.activation(self.tmp[:, 0, :], self.var[:, :], ACT.Ln, bias=self.k.eps[:, 0:1]
                                  ).then_inc(self.guessed.sem, 1)
        act.wait_ge(self.guessed.sem, self.guessed.at(t, 1))
        self.nc.scalar.activation(self.tmp[:, 1, :], self.tmp[:, 0, :], ACT.Exp, scale=-0.5
                                  ).then_inc(self.guessed.sem, 1)

    def apply(self, dve, t):
        c, nc, w = self.done, self.nc, self.tmp
        n = [self.first + 4]

        def link(ins):
            n[0] += 1
            ins.then_inc(c.sem, 1)
            dve.wait_ge(c.sem, c.at(t, n[0]))

        dve.wait_ge(self.guessed.sem, self.guessed.at(t))
        newton_rsqrt(nc.vector, link, self.var[:, :], w[:, 1, :], w[:, 2, :], w[:, 3, :], w[:, 4, :])
        dve.wait_ge(self.affine.sem, self.affine.at(t - 1, 1))
        for r in range(GR):
            last = nc.vector.tensor_scalar(tiles(self.unit, r), tiles(self.rows, r), self.mean[:, r:r + 1],
                                           w[:, 4, r:r + 1], ALU.subtract, ALU.mult)
        last.then_inc(c.sem, 1)

    def scale_shift(self, pool, t, out, gamma, beta, free):
        def by_tile(a):
            return a.rearrange("p (r c) -> p r c", c=C)

        def row(a):
            return a[:, :].unsqueeze(1).broadcast_to([P, GR, C])

        a = self.affine
        pool.wait_ge(self.done.sem, self.done.at(t))
        self.nc.gpsimd.tensor_tensor(by_tile(self.scaled[:, :]), by_tile(self.unit[:, :]), row(gamma), ALU.mult
                                     ).then_inc(a.sem, 1)
        pool.wait_ge(a.sem, a.at(t, 1))
        free()
        self.nc.gpsimd.tensor_tensor(by_tile(out), by_tile(self.scaled[:, :]), row(beta), ALU.add).then_inc(a.sem, 1)


class Attention:

    SCALE = float(C) ** -0.5

    def __init__(self, m, k, name, mask, bank_s, bank_pt, bank_o):
        self.nc, self.k, self.mask = m.nc, k, mask
        self.bank_s, self.bank_pt, self.bank_o = bank_s, bank_pt, bank_o
        self.p, self.pT = m.sb(name + "_p", [P, GT]), m.sb(name + "_pT", [P, GT])
        self.top = m.sb(name + "_top", [P, 2, GR])
        self.sums = m.sb(name + "_sums", [P, GR])
        self.inverse = m.sb(name + "_inverse", [P, GR])
        self.scored = m.count(name + "_scored")
        self.topped = m.count(name + "_topped", 2)
        self.powered = m.count(name + "_powered")
        self.turned = m.count(name + "_turned")
        self.copied = m.count(name + "_copied")
        self.mixed = m.count(name + "_mixed")

    def score(self, pe, t, qT, kT):
        nc = self.nc
        pe.wait_ge(self.powered.sem, self.powered.at(t - 1))
        nc.tensor.matmul(self.bank_s[:, :], self.k.ident_bf[:, :], self.mask, start=True, stop=False)
        for r in range(GR):
            last = nc.tensor.matmul(tiles(self.bank_s, r), tiles(qT, r), tiles(kT, r), start=False, stop=r == GR - 1)
        last.then_inc(self.scored.sem, 1)

    def find_top(self, dve, t):
        nc, c = self.nc, self.topped
        dve.wait_ge(self.scored.sem, self.scored.at(t))
        nc.vector.tensor_reduce(self.top[:, 0, :], self.bank_s[:, :].rearrange("p (r q) -> p r q", q=P), AX.X, ALU.max
                                ).then_inc(c.sem, 1)
        dve.wait_ge(c.sem, c.at(t, 1))
        dve.wait_ge(self.powered.sem, self.powered.at(t - 1))
        nc.vector.tensor_scalar(self.top[:, 1, :], self.top[:, 0, :], -self.SCALE, None, ALU.mult).then_inc(c.sem, 1)

    def power(self, act, t):
        nc = self.nc
        act.wait_ge(self.topped.sem, self.topped.at(t))
        act.wait_ge(self.turned.sem, self.turned.at(t - 1))
        for r in range(GR):
            last = nc.scalar.activation(tiles(self.p, r), tiles(self.bank_s, r), ACT.Exp, bias=self.top[:, 1, r:r + 1],
                                        scale=self.SCALE, accum_out=self.sums[:, r:r + 1])
        last.then_inc(self.powered.sem, 1)

    def turn(self, pe, t, bank_free):
        pe.wait_ge(self.powered.sem, self.powered.at(t))
        bank_free()
        for r in range(GR):
            last = self.nc.tensor.transpose(tiles(self.bank_pt, r), tiles(self.p, r), self.k.ident[:, :])
        last.then_inc(self.turned.sem, 1)

    def copy(self, act, t):
        act.wait_ge(self.turned.sem, self.turned.at(t))
        act.wait_ge(self.mixed.sem, self.mixed.at(t - 1))
        self.nc.scalar.copy(self.pT[:, :], self.bank_pt[:, :]).then_inc(self.copied.sem, 1)

    def mix(self, pe, t, v, bank_free):
        pe.wait_ge(self.copied.sem, self.copied.at(t))
        bank_free()
        for r in range(GR):
            last = self.nc.tensor.matmul(tiles(self.bank_o, r), tiles(self.pT, r), tiles(v, r), start=True, stop=True)
        last.then_inc(self.mixed.sem, 1)

    def finish(self, dve, t, rows, residual, count):
        nc = self.nc
        dve.wait_ge(self.mixed.sem, self.mixed.at(t))
        nc.vector.reciprocal(self.inverse[:, :], self.sums[:, :]).then_inc(count.sem, 1)
        dve.wait_ge(count.sem, count.at(t, 1))
        for r in range(GR):
            last = nc.vector.scalar_tensor_tensor(tiles(rows, r), tiles(self.bank_o, r), self.inverse[:, r:r + 1],
                                                  tiles(residual, r), ALU.mult, ALU.add)
        last.then_inc(count.sem, 1)
        dve.wait_ge(count.sem, count.at(t, 2))


def phase_c(m, k, dram):
    nc = m.nc
    ctx = dram["ctx_1024"].rearrange("(r two) s c -> (two s) r c", two=2)
    NK = 4
    y, z, y1, y2 = (m.sb("c_" + n, [P, 2, GT]) for n in ("y", "z", "y1", "y2"))
    yT, zT, y1T, y2T = (m.sb("c_" + n, [P, GT]) for n in ("yT", "zT", "y1T", "y2T"))
    hidden = m.sb("c_hidden", [P, NK, GT])
    y2b = m.sb("c_y2b", [P, GT])
    y3 = m.sb("c_y3", [P, GT])
    bank_t, bank_t2, bank_sa, bank_sc, bank_pt, bank_o, bank_h, bank_f = k.bank

    own = Attention(m, k, "c_self", k.masks_bf[:, 0, :], bank_sa, bank_pt, bank_o)
    cross = Attention(m, k, "c_cross", k.masks_bf[:, 1, :], bank_sc, bank_pt, bank_o)
    ln1 = LayerNorm(m, k, "c_ln1", 10, 2)
    ln2 = LayerNorm(m, k, "c_ln2", 10, 2)
    ln3 = LayerNorm(m, k, "c_ln3", 9, 1)
    z_loaded = [m.sem(f"c_z_loaded{b}") for b in range(2)]
    normed = m.count("c_normed")
    turned = {n: m.count("c_turned_" + n) for n in ("y", "z", "y1", "y2")}
    copied = {n: m.count("c_copied_" + n) for n in ("y", "z", "y1", "y2")}
    raised = m.count("c_raised", NK)
    bent = m.count("c_bent", NK)
    lowered = m.count("c_lowered")
    biased = m.count("c_biased")
    added = m.count("c_added")

    with nc.Block() as block:
        @block.sync
        def _(sp):
            def step(s, odd):
                sp.wait_ge(cross.mixed.sem, cross.mixed.at(s - 2))
                sp.dma_start(z[:, odd, :].rearrange("p (r c) -> p r c", c=C), ctx[:, group(s), :]
                             ).then_inc(z_loaded[odd], 16)
            pipelined(sp, 0, step)

        @block.vector
        def _(dve):
            for c in (normed, own.topped, cross.topped, ln1.done, ln2.done, ln3.done):
                c.start(dve)

            def step(s, odd):
                even = 1 - odd
                if live(s - 1):
                    own.find_top(dve, s - 1)
                if live(s - 3):
                    ln2.apply(dve, s - 3)
                if live(s - 5):
                    dve.wait_ge(added.sem, added.at(s - 5))
                    for r in range(GR):
                        i = bass.ds((s - 5) * GR + r, 1)
                        nc.vector.bn_stats(k.stats[:, i, :], k.x[:, i, :])
                if live(s - 2):
                    cross.find_top(dve, s - 2)
                if live(s):
                    dve.wait_ge(own.mixed.sem, own.mixed.at(s - 2))
                    for r in range(GR):
                        i = bass.ds(s * GR + r, 1)
                        last = nc.vector.tensor_scalar(tiles(y[:, odd, :], r), k.x[:, i, :], k.mean[:, i],
                                                       k.rstd[:, i], ALU.subtract, ALU.mult)
                    last.then_inc(normed.sem, 1)
                if live(s - 4):
                    t = s - 4
                    dve.wait_ge(lowered.sem, lowered.at(t))
                    dve.wait_ge(biased.sem, biased.at(t))
                    nc.vector.tensor_tensor(ln3.rows[:, :], bank_f[:, :], y2b[:, :], ALU.add).then_inc(ln3.done.sem, 1)
                    dve.wait_ge(ln3.done.sem, ln3.done.at(t, 1))
                    ln3.take(dve, t)
                if live(s - 1):
                    own.finish(dve, s - 1, ln1.rows, y[:, even, :], ln1.done)
                    ln1.take(dve, s - 1)
                if live(s - 1):
                    ln1.apply(dve, s - 1)
                if live(s - 4):
                    ln3.apply(dve, s - 4)
                if live(s - 2):
                    cross.finish(dve, s - 2, ln2.rows, y1[:, odd, :], ln2.done)
                    ln2.take(dve, s - 2)
            pipelined(dve, 5, step)

        @block.tensor
        def _(pe):
            for c in (*turned.values(), own.scored, own.turned, own.mixed, cross.scored, cross.turned, cross.mixed,
                      raised, lowered):
                c.start(pe)

            def turn(name, t, src, bank, other, other_t):
                pe.wait_ge(copied[other].sem, copied[other].at(other_t))
                for r in range(GR):
                    last = nc.tensor.transpose(tiles(bank, r), tiles(src, r), k.ident[:, :])
                last.then_inc(turned[name].sem, 1)

            def up(t, j):
                if not live(t):
                    return
                pe.wait_ge(copied["y2"].sem, copied["y2"].at(t))
                pe.wait_ge(bent.sem, bent.at(t, j - 1))
                nc.tensor.matmul((bank_h, bank_sc)[j % 2][:, :], k.w1[:, j * P:(j + 1) * P], y2T[:, :], start=True, stop=True
                                 ).then_inc(raised.sem, 1)

            def down(t, j):
                if not live(t):
                    return
                if j == 0:
                    pe.wait_ge(ln3.done.sem, ln3.done.at(t - 1, 1))
                pe.wait_ge(bent.sem, bent.at(t, j + 1))
                for r in range(GR):
                    last = nc.tensor.matmul(tiles(bank_f, r), tiles(hidden[:, j, :], r), k.w2[:, j, :],
                                            start=j == 0 and r == 0, stop=j == NK - 1, skip_group_check=True)
                if j == NK - 1:
                    last.then_inc(lowered.sem, 1)

            def step(s, odd):
                even = 1 - odd
                if live(s - 1):
                    pe.wait_ge(normed.sem, normed.at(s - 1))
                    turn("y", s - 1, y[:, even, :], bank_t, "y1", s - 3)
                if live(s - 2):
                    pe.wait_ge(z_loaded[odd], (s - 2 - odd) * 8 + 16)
                    turn("z", s - 2, z[:, odd, :], bank_t2, "y2", s - 4)
                down(s - 4, 0)
                if live(s - 1):
                    pe.wait_ge(copied["y"].sem, copied["y"].at(s - 1))
                    own.score(pe, s - 1, yT, yT)
                if live(s - 2):
                    pe.wait_ge(ln1.affine.sem, ln1.affine.at(s - 2))
                    turn("y1", s - 2, y1[:, odd, :], bank_t, "y", s - 1)
                down(s - 4, 1)
                if live(s - 2):
                    pe.wait_ge(copied["z"].sem, copied["z"].at(s - 2))
                    pe.wait_ge(copied["y1"].sem, copied["y1"].at(s - 2))
                    pe.wait_ge(bent.sem, bent.at(s - 4))
                    cross.score(pe, s - 2, y1T, zT)
                down(s - 4, 2)
                if live(s - 1):
                    own.turn(pe, s - 1, lambda: pe.wait_ge(cross.copied.sem, cross.copied.at(s - 3)))
                down(s - 4, 3)
                if live(s - 1):
                    own.mix(pe, s - 1, y[:, even, :], lambda: pe.wait_ge(ln2.done.sem, ln2.done.at(s - 3, 2)))
                if live(s - 3):
                    pe.wait_ge(ln2.affine.sem, ln2.affine.at(s - 3))
                    turn("y2", s - 3, y2[:, even, :], bank_t2, "z", s - 2)
                if live(s - 2):
                    cross.turn(pe, s - 2, lambda: pe.wait_ge(own.copied.sem, own.copied.at(s - 1)))
                up(s - 3, 0)
                up(s - 3, 1)
                if live(s - 2):
                    cross.mix(pe, s - 2, z[:, odd, :], lambda: pe.wait_ge(ln1.done.sem, ln1.done.at(s - 1, 2)))
                up(s - 3, 2)
                up(s - 3, 3)
            pipelined(pe, 4, step)

        @block.scalar
        def _(act):
            for c in (*copied.values(), own.powered, own.copied, cross.powered, cross.copied, bent,
                      ln1.guessed, ln2.guessed, ln3.guessed):
                c.start(act)

            def copy(name, t, dst, bank, reader, count):
                if not live(t):
                    return
                act.wait_ge(turned[name].sem, turned[name].at(t))
                act.wait_ge(reader.sem, count)
                nc.scalar.copy(dst[:, :], bank[:, :]).then_inc(copied[name].sem, 1)

            def relu(t, j):
                if not live(t):
                    return
                act.wait_ge(raised.sem, raised.at(t, j + 1))
                act.wait_ge(lowered.sem, lowered.at(t - 1))
                nc.scalar.activation(hidden[:, j, :], (bank_h, bank_sc)[j % 2][:, :], ACT.Relu, bias=k.b1[:, j:j + 1]
                                     ).then_inc(bent.sem, 1)

            def step(s, odd):
                copy("y", s - 1, yT, bank_t, own.scored, own.scored.at(s - 2))
                copy("z", s - 2, zT, bank_t2, cross.scored, cross.scored.at(s - 3))
                if live(s - 3):
                    ln2.guess(act, s - 3)
                copy("y1", s - 2, y1T, bank_t, cross.scored, cross.scored.at(s - 3))
                if live(s - 1):
                    own.power(act, s - 1)
                    own.copy(act, s - 1)
                if live(s - 2):
                    cross.power(act, s - 2)
                copy("y2", s - 3, y2T, bank_t2, raised, raised.at(s - 4))
                if live(s - 2):
                    cross.copy(act, s - 2)
                if live(s - 4):
                    ln3.guess(act, s - 4)
                relu(s - 3, 0)
                relu(s - 3, 1)
                if live(s - 1):
                    ln1.guess(act, s - 1)
                relu(s - 3, 2)
                relu(s - 3, 3)
            pipelined(act, 4, step)

        @block.gpsimd
        def _(pool):
            for c in (ln1.affine, ln2.affine, ln3.affine, biased, added):
                c.start(pool)

            def step(s, odd):
                even = 1 - odd
                if live(s - 3):
                    ln2.scale_shift(pool, s - 3, y2[:, even, :], k.gamma[1], k.beta[1],
                                    lambda: pool.wait_ge(turned["y2"].sem, turned["y2"].at(s - 5)))
                if live(s - 1):
                    ln1.scale_shift(pool, s - 1, y1[:, even, :], k.gamma[0], k.beta[0],
                                    lambda: pool.wait_ge(ln2.done.sem, ln2.done.at(s - 3, 2)))
                if live(s - 4):
                    t = s - 4
                    ln3.scale_shift(pool, t, y3[:, :], k.gamma[2], k.beta[2], lambda: None)
                    pool.wait_ge(ln3.affine.sem, ln3.affine.at(t))
                    x = k.x[:, group(t), :]
                    nc.gpsimd.tensor_tensor(x, x, y3[:, :].rearrange("p (r c) -> p r c", c=C), ALU.add
                                            ).then_inc(added.sem, 1)
                if live(s - 3):
                    t = s - 3
                    pool.wait_ge(ln2.affine.sem, ln2.affine.at(t))
                    pool.wait_ge(ln3.done.sem, ln3.done.at(t - 1, 1))
                    nc.gpsimd.tensor_tensor(y2b[:, :].rearrange("p (r c) -> p r c", c=C),
                                            y2[:, even, :].rearrange("p (r c) -> p r c", c=C),
                                            k.b2[:, :].unsqueeze(1).broadcast_to([P, GR, C]), ALU.add
                                            ).then_inc(biased.sem, 1)
            pipelined(pool, 4, step)


def phase_d(m, k, dram):
    nc = m.nc
    HEADS, HD = 16, 8
    UNITS = 2 * GR
    PAIRS = HEADS // 2
    VW = 2 * HD + 2
    SCALE = float(HD) ** -0.5
    xn, hT, cT = m.sb("d_xn", [P, GT]), m.sb("d_hT", [P, GT]), m.sb("d_cT", [P, GT])
    cTT = m.sb("d_cTT", [P, GB * P])
    part = m.sb("d_part", [P, 4, GT])
    kT, qT = m.sb("d_kT", [P, GT]), m.sb("d_qT", [P, 2, GT])
    keys = m.sb("d_keys", [P, 2, GB, HEADS, SEQ])
    vals = m.sb("d_vals", [P, 2, GB, PAIRS, VW])
    prob, probT = m.sb("d_prob", [P, 4, 512]), m.sb("d_probT", [P, 2, 512])
    top = m.sb("d_top", [P, 4, 8])
    inverse = m.sb("d_inverse", [P, PAIRS, 2])
    o, oT, u = m.sb("d_o", [P, GT]), m.sb("d_oT", [P, GT]), m.sb("d_u", [P, GT])
    bank_t, bank_l, bank_r, bank_s, bank_pt, bank_o = k.bank[0], k.bank[1], k.bank[2], k.bank[3:5], k.bank[5:7], k.bank[7]

    blank = m.sem("d_blank")
    normed = m.count("d_normed")
    turned = m.count("d_turned")
    h_copied = m.count("d_h_copied")
    conved = m.count("d_conved", 3)
    doubled = m.count("d_doubled")
    projected = m.count("d_projected", 5)
    rotated = m.count("d_rotated", 4)
    summed = m.count("d_summed", 2)
    keys_in = [m.sem(f"d_keys_in{b}") for b in range(2)]
    v_copied = m.count("d_v_copied")
    scored = m.count("d_scored", UNITS)
    topped = m.count("d_topped", 2 * UNITS)
    powered = m.count("d_powered", UNITS)
    p_turned = m.count("d_p_turned", UNITS)
    p_copied = m.count("d_p_copied", UNITS)
    mixed = m.count("d_mixed", UNITS)
    divided = m.count("d_divided", 2 * GR)
    o_turned = m.count("d_o_turned")
    o_copied = m.count("d_o_copied")
    out = m.count("d_out")
    updated = m.count("d_updated", 2)
    added = m.count("d_added")

    def unit(t, n):
        return t + n // UNITS, n % UNITS

    with nc.Block() as block:
        @block.sync
        def _(sp):
            sp.wait_ge(blank, 4)

            def step(s, odd):
                t, b = s, odd
                sp.wait_ge(summed.sem, summed.at(t, 1))
                sp.wait_ge(scored.sem, scored.at(t - 2))
                for h in range(HEADS):
                    rows = slice(h * HD, (h + 1) * HD)
                    sp.dma_start(keys[rows, b, :, h, :], by_batch(kT[rows, :])).then_inc(keys_in[b], 16)
            pipelined(sp, 0, step)

        @block.vector
        def _(dve):
            for c in (normed, conved, rotated, topped, divided, updated):
                c.start(dve)

            def norm(t):
                if not live(t):
                    return
                dve.wait_ge(turned.sem, turned.at(t - 1))
                for r in range(GR):
                    i = bass.ds(t * GR + r, 1)
                    last = nc.vector.tensor_scalar(tiles(xn, r), k.x[:, i, :], k.mean[:, i], k.rstd2[:, i],
                                                   ALU.subtract, ALU.mult)
                last.then_inc(normed.sem, 1)

            def convolve(t):
                if not live(t):
                    return
                h, c = by_batch(hT[:, :]), by_batch(cT[:, :])
                dve.wait_ge(h_copied.sem, h_copied.at(t))
                dve.wait_ge(projected.sem, projected.at(t - 1, 4))
                dve.wait_ge(doubled.sem, doubled.at(t - 1))
                nc.vector.tensor_scalar(c, h, k.conv[:, 2:3], None, ALU.mult).then_inc(conved.sem, 1)
                for lag in (1, 2):
                    dve.wait_ge(conved.sem, conved.at(t, lag))
                    nc.vector.scalar_tensor_tensor(c[:, :, lag:], h[:, :, :SEQ - lag], k.conv[:, 2 - lag:3 - lag],
                                                   c[:, :, lag:], ALU.mult, ALU.add).then_inc(conved.sem, 1)

            def rotate(t, first):
                if not live(t):
                    return
                for j in (first, first + 1):
                    dve.wait_ge(projected.sem, projected.at(t, j + 1))
                    dve.wait_ge(summed.sem, summed.at(t - 1, first // 2 + 1))
                    nc.vector.tensor_tensor(by_batch(part[:, j, :]), by_batch((bank_l, bank_r)[j % 2][:, :]),
                                            over_batches(k.rope_d[:, j % 2, :]), ALU.mult).then_inc(rotated.sem, 1)

            def shift(t, n):
                if not live(t):
                    return
                scores = bank_s[n % 2][:, :].rearrange("p (h s) -> p h s", s=SEQ)
                dve.wait_ge(scored.sem, scored.at(t, n + 1))
                nc.vector.tensor_reduce(top[:, n % 4, :], scores, AX.X, ALU.max).then_inc(topped.sem, 1)
                dve.wait_ge(topped.sem, topped.at(t, 2 * n + 1))
                dve.wait_ge(p_turned.sem, p_turned.at(t, n - 3))
                nc.vector.tensor_tensor(prob[:, n % 4, :].rearrange("p (h s) -> p h s", s=SEQ), scores,
                                        top[:, n % 4, :].unsqueeze(2).broadcast_to([P, 8, SEQ]), ALU.subtract
                                        ).then_inc(topped.sem, 1)

            def divide(t, r):
                if not live(t):
                    return
                got = bank_o[:, 0:PAIRS * VW].rearrange("p (j w) -> p j w", w=VW)
                dve.wait_ge(mixed.sem, mixed.at(t, 2 * r + 2))
                nc.vector.reciprocal(inverse[:, :, :], got[:, :, 2 * HD:]).then_inc(divided.sem, 1)
                dve.wait_ge(divided.sem, divided.at(t, 2 * r + 1))
                if r == 0:
                    dve.wait_ge(o_turned.sem, o_turned.at(t - 1))
                nc.vector.tensor_tensor(tiles(o, r).rearrange("p (j e d) -> p j e d", j=PAIRS, e=2),
                                        got[:, :, 0:2 * HD].rearrange("p j (e d) -> p j e d", e=2),
                                        inverse[:, :, :].unsqueeze(3).broadcast_to([P, PAIRS, 2, HD]), ALU.mult
                                        ).then_inc(divided.sem, 1)

            def unit_rows(t):
                if not live(t):
                    return
                for r in range(GR):
                    i = bass.ds(t * GR + r, 1)
                    last = nc.vector.tensor_scalar(tiles(u, r), k.x[:, i, :], k.mean[:, i], k.rstd[:, i],
                                                   ALU.subtract, ALU.mult)
                last.then_inc(updated.sem, 1)

            def update(t):
                if not live(t):
                    return
                dve.wait_ge(out.sem, out.at(t))
                dve.wait_ge(updated.sem, updated.at(t, 1))
                dst = k.u[:, group(t), :]
                nc.vector.tensor_tensor(dst, bank_t[:, :].rearrange("p (r c) -> p r c", c=C),
                                        u[:, :].rearrange("p (r c) -> p r c", c=C), ALU.add).then_inc(updated.sem, 1)

            def take(t):
                if not live(t):
                    return
                dve.wait_ge(updated.sem, updated.at(t))
                for r in range(GR):
                    i = bass.ds(t * GR + r, 1)
                    nc.vector.bn_stats(k.stats[:, i, :], k.u[:, i, :])

            def step(s, odd):
                t = s - 2
                shift(t, 0)
                divide(s - 3, 2)
                rotate(s - 1, 0)
                shift(t, 1)
                shift(t, 2)
                divide(s - 3, 3)
                shift(t, 3)
                rotate(s - 1, 2)
                shift(t, 4)
                divide(t, 0)
                unit_rows(s - 3)
                norm(s)
                shift(t, 5)
                update(s - 3)
                shift(t, 6)
                divide(t, 1)
                take(s - 3)
                shift(t, 7)
                convolve(s)
            pipelined(dve, 3, step)

        @block.tensor
        def _(pe):
            for c in (turned, projected, scored, p_turned, mixed, o_turned, out):
                c.start(pe)

            def turn(t):
                if not live(t):
                    return
                pe.wait_ge(normed.sem, normed.at(t))
                pe.wait_ge(updated.sem, updated.at(t - 3))
                for r in range(GR):
                    last = nc.tensor.transpose(tiles(bank_t, r), tiles(xn, r), k.ident[:, :])
                last.then_inc(turned.sem, 1)

            def project(t, first):
                if not live(t):
                    return
                j = 1 - first // 2
                if first == 0:
                    pe.wait_ge(conved.sem, conved.at(t))
                    pe.wait_ge(v_copied.sem, v_copied.at(t - 1))
                else:
                    pe.wait_ge(rotated.sem, rotated.at(t, 2))
                nc.tensor.matmul(bank_l[:, :], k.qkv[:, j, :], cT[:, :], start=True, stop=True).then_inc(projected.sem, 1)
                nc.tensor.matmul(bank_r[:, :], k.qk_rot[:, j, :], cT[:, :], start=True, stop=True
                                 ).then_inc(projected.sem, 1)

            def values(t):
                if not live(t):
                    return
                pe.wait_ge(rotated.sem, rotated.at(t))
                pe.wait_ge(doubled.sem, doubled.at(t))
                for i in range(GB):
                    bank = (bank_l, bank_r)[i // 4]
                    last = nc.tensor.matmul(tiles(bank, i % 4), tiles(cTT, i), k.qkv[:, 2, :], start=True, stop=True)
                last.then_inc(projected.sem, 1)

            def score(t, b, n):
                if not live(t):
                    return
                r, half = n // 2, n % 2
                bank = bank_s[n % 2]
                if n == 0:
                    if isinstance(t, int) and t == 0:
                        pe.wait_ge(blank, 4)
                    pe.wait_ge(summed.sem, summed.at(t))
                    pe.wait_ge(keys_in[b], (t - b) * 8 * HEADS + 16 * HEADS)
                pe.wait_ge(topped.sem, topped.at(t, 2 * n - 2))
                nc.tensor.matmul(bank[:, :], k.ident_bf[:, :], k.masks_bf[:, 0, :], start=True, stop=False,
                                 skip_group_check=True)
                for e in range(2):
                    i = 2 * r + e
                    last = nc.tensor.matmul(bank[e * SEQ:(e + 1) * SEQ, :], qT[:, b, i * SEQ:(i + 1) * SEQ],
                                            keys[:, b, i, half * 8:half * 8 + 8, :], start=False, stop=True,
                                            tile_position=(0, e * SEQ), skip_group_check=True)
                last.then_inc(scored.sem, 1)

            def turn_prob(t, n):
                if not live(t):
                    return
                pe.wait_ge(powered.sem, powered.at(t, n + 1))
                pe.wait_ge(p_copied.sem, p_copied.at(t, n - 1))
                for j in range(4):
                    last = nc.tensor.transpose(tiles(bank_pt[n % 2], j), tiles(prob[:, n % 4, :], j), k.ident[:, :])
                last.then_inc(p_turned.sem, 1)

            def mix(t, b, n):
                if not live(t):
                    return
                r, half = n // 2, n % 2
                pe.wait_ge(p_copied.sem, p_copied.at(t, n + 1))
                if n == 0:
                    pe.wait_ge(v_copied.sem, v_copied.at(t))
                if half == 0:
                    pe.wait_ge(divided.sem, divided.at(t, 2 * r))
                for j in range(4):
                    pair = half * 4 + j
                    for e in range(2):
                        last = nc.tensor.matmul(bank_o[e * SEQ:(e + 1) * SEQ, pair * VW:(pair + 1) * VW],
                                                probT[:, n % 2, j * P + e * SEQ:j * P + (e + 1) * SEQ],
                                                vals[:, b, 2 * r + e, pair, :], start=True, stop=True,
                                                tile_position=(0, e * SEQ))
                last.then_inc(mixed.sem, 1)

            def turn_out(t):
                if not live(t):
                    return
                pe.wait_ge(divided.sem, divided.at(t))
                pe.wait_ge(h_copied.sem, h_copied.at(t + 2))
                for r in range(GR):
                    last = nc.tensor.transpose(tiles(bank_t, r), tiles(o, r), k.ident[:, :])
                last.then_inc(o_turned.sem, 1)

            def project_out(t):
                if not live(t):
                    return
                pe.wait_ge(o_copied.sem, o_copied.at(t))
                for r in range(GR):
                    last = nc.tensor.matmul(tiles(bank_t, r), tiles(oT, r), k.proj[:, :], start=True, stop=True)
                last.then_inc(out.sem, 1)

            def step(s, odd):
                t, b = s - 2, odd
                for n in range(UNITS):
                    score(t, b, n)
                    before, i = unit(t, n - 3)
                    mix(before, b if n >= 3 else 1 - b, i)
                    if n == 0:
                        project(s - 1, 0)
                    if n == 2:
                        project(s - 1, 2)
                    if n == 3:
                        turn_out(s - 3)
                    if n == 4:
                        values(s - 1)
                        project_out(s - 3)
                    if n == 6:
                        turn(s)
                    turn_prob(*unit(t, n - 2))
            pipelined(pe, 3, step)

        @block.scalar
        def _(act):
            for c in (h_copied, doubled, v_copied, powered, p_copied, o_copied):
                c.start(act)

            def copy_h(t):
                if not live(t):
                    return
                act.wait_ge(turned.sem, turned.at(t))
                act.wait_ge(conved.sem, conved.at(t - 1))
                nc.scalar.activation(hT[:, :], bank_t[:, :], ACT.Identity, bias=k.ln1_b[:, 0:1], scale=k.ln1_w[:, 0:1]
                                     ).then_inc(h_copied.sem, 1)

            def double(t):
                if not live(t):
                    return
                act.wait_ge(conved.sem, conved.at(t))
                act.wait_ge(projected.sem, projected.at(t - 1))
                nc.scalar.copy(cTT[:, :].rearrange("p (b e s) -> p b e s", e=2, s=SEQ),
                               by_batch(cT[:, :]).unsqueeze(2).broadcast_to([P, GB, 2, SEQ])).then_inc(doubled.sem, 1)

            def copy_v(t, b):
                if not live(t):
                    return
                if isinstance(t, int) and t == 0:
                    act.wait_ge(blank, 4)
                act.wait_ge(projected.sem, projected.at(t))
                act.wait_ge(mixed.sem, mixed.at(t - 2))
                for n, bank in enumerate((bank_l, bank_r)):
                    for e in range(2):
                        rows = slice(e * SEQ, (e + 1) * SEQ)
                        got = bank[rows, :].rearrange("p (i j e d) -> p i j e d", i=4, j=PAIRS, e=2)
                        last = nc.scalar.copy(vals[rows, b, 4 * n:4 * n + 4, :, e * HD:(e + 1) * HD], got[:, :, :, e, :])
                last.then_inc(v_copied.sem, 1)

            def power(t, n):
                if not live(t):
                    return
                act.wait_ge(topped.sem, topped.at(t, 2 * n + 2))
                nc.scalar.activation(prob[:, n % 4, :], prob[:, n % 4, :], ACT.Exp, scale=SCALE).then_inc(powered.sem, 1)

            def copy_prob(t, n):
                if not live(t):
                    return
                act.wait_ge(p_turned.sem, p_turned.at(t, n + 1))
                act.wait_ge(mixed.sem, mixed.at(t, n - 1))
                nc.scalar.copy(probT[:, n % 2, :], bank_pt[n % 2][:, :]).then_inc(p_copied.sem, 1)

            def copy_out(t):
                if not live(t):
                    return
                act.wait_ge(o_turned.sem, o_turned.at(t))
                act.wait_ge(out.sem, out.at(t - 1))
                nc.scalar.copy(oT[:, :], bank_t[:, :]).then_inc(o_copied.sem, 1)

            def step(s, odd):
                t = s - 2
                for n in range(UNITS):
                    power(t, n)
                    copy_prob(*unit(t, n - 2))
                    if n == 0:
                        double(s - 1)
                    if n == 3:
                        copy_out(s - 3)
                    if n == 4:
                        copy_v(s - 1, 1 - odd)
                    if n == 6:
                        copy_h(s)
            pipelined(act, 3, step)

        @block.gpsimd
        def _(pool):
            nc.gpsimd.memset(keys[:], 0.0).then_inc(blank, 1)
            nc.gpsimd.memset(vals[:], 0.0).then_inc(blank, 1)
            pool.wait_ge(blank, 2)
            for e in range(2):
                nc.gpsimd.memset(vals[e * SEQ:(e + 1) * SEQ, :, :, :, 2 * HD + e], 1.0).then_inc(blank, 1)
            pool.wait_ge(blank, 4)
            for c in (summed, added):
                c.start(pool)

            def sum_parts(t, b):
                if not live(t):
                    return
                pool.wait_ge(rotated.sem, rotated.at(t, 2))
                if isinstance(t, int):
                    if t > 0:
                        pool.wait_ge(keys_in[1 - b], 16 * HEADS * ((t - 1) // 2 + 1))
                else:
                    pool.wait_ge(keys_in[1 - b], (t - 1 - (1 - b)) * 8 * HEADS + 16 * HEADS)
                nc.gpsimd.tensor_tensor(kT[:, :], part[:, 0, :], part[:, 1, :], ALU.add).then_inc(summed.sem, 1)
                pool.wait_ge(rotated.sem, rotated.at(t))
                pool.wait_ge(scored.sem, scored.at(t - 2))
                nc.gpsimd.tensor_tensor(qT[:, b, :], part[:, 2, :], part[:, 3, :], ALU.add).then_inc(summed.sem, 1)

            def add(t):
                if not live(t):
                    return
                pool.wait_ge(updated.sem, updated.at(t))
                x = k.x[:, group(t), :]
                nc.gpsimd.tensor_tensor(x, x, k.u[:, group(t), :], ALU.add).then_inc(added.sem, 1)

            def step(s, odd):
                sum_parts(s - 1, 1 - odd)
                add(s - 3)
            pipelined(pool, 3, step)


class Moe:
    CAP = TOK + GT

    def __init__(self, E, top, NK, gated, affine, extra):
        self.E, self.top, self.NK, self.gated, self.affine, self.extra = E, top, NK, gated, affine, extra
        self.W = C + extra + 1
        self.fill = top * TOK // GT
        self.NT = (top * TOK + E * (GT - 1)) // GT
        self.spare = self.NT - self.fill
        self.rows = E * self.CAP + self.spare * GT
        self.dst_rows = top * TOK + (E + self.spare) * GT


def fresh(kind):
    if kind == "B":
        return Moe(8, 2, 2, False, False, 1)
    return Moe(4, 1, 4, True, True, C)


def plan(m, moe):
    nc = m.nc
    E, NT, CAP, W = moe.E, moe.NT, moe.CAP, moe.W
    name = f"plan{E}"
    sb = lambda n, shape, dt=F32: m.sb(f"{name}_{n}", shape, dt)
    end_row = sb("end_row", [1, E], mybir.dt.int32)
    steps_512 = sb("steps_512", [1, RT // GR])
    tile_no = sb("tile_no", [1, NT])
    over = sb("over", [1, E, RT // GR])
    total, n, start, jump = sb("total", [1, E]), sb("n", [1, E]), sb("start", [1, E + 1]), sb("jump", [1, E])
    ge, gj = sb("ge", [1, NT, E]), sb("gj", [1, NT, E])
    te, tr, tr2 = sb("te", [1, NT]), sb("tr", [1, NT]), sb("tr2", [1, NT])
    made, steps, ended, written = (m.sem(f"{name}_{n}") for n in ("made", "steps", "ended", "written"))

    def tables(pool):
        for t, size, gap in ((steps_512, RT // GR, GT), (tile_no, NT, 1)):
            nc.gpsimd.iota(t[:, :], [[gap, size]], base=0, channel_multiplier=0,
                           allow_small_or_imprecise_dtypes=True).then_inc(made, 1)
        nc.gpsimd.memset(start[:, :], 0.0).then_inc(made, 1)

    def work_out(dve):
        v, at = nc.vector, [0]

        def link(ins):
            at[0] += 1
            ins.then_inc(steps, 1)
            dve.wait_ge(steps, at[0])

        v.tensor_copy(end_row[:, :], moe.end[0:1, :]).then_inc(ended, 1)
        link(v.tensor_tensor(total[:, :], moe.end[0:1, :], moe.base[0:1, :], ALU.subtract))
        dve.wait_ge(made, 3)
        link(v.tensor_tensor(over[:, :, :], total[:, :].unsqueeze(2).broadcast_to([1, E, RT // GR]),
                             steps_512[:, :].unsqueeze(1).broadcast_to([1, E, RT // GR]), ALU.is_gt))
        link(v.tensor_reduce(n[:, :], over[:, :, :], AX.X, ALU.add))
        for e in range(E):
            link(v.tensor_tensor(start[:, e + 1:e + 2], start[:, e:e + 1], n[:, e:e + 1], ALU.add))
        link(v.tensor_scalar(jump[:, :], n[:, :], -float(GT), float(CAP), ALU.mult, ALU.add))
        link(v.tensor_tensor(ge[:, :, :], tile_no[:, :].unsqueeze(2).broadcast_to([1, NT, E]),
                             start[:, 1:E + 1].unsqueeze(1).broadcast_to([1, NT, E]), ALU.is_ge))
        link(v.tensor_tensor(gj[:, :, :], ge[:, :, :], jump[:, :].unsqueeze(1).broadcast_to([1, NT, E]), ALU.mult))
        link(v.tensor_reduce(te[:, :], ge[:, :, :], AX.X, ALU.add))
        link(v.tensor_reduce(tr[:, :], gj[:, :, :], AX.X, ALU.add))
        link(v.scalar_tensor_tensor(tr2[:, :], tile_no[:, :], float(GT), tr[:, :], ALU.mult, ALU.add))
        v.tensor_copy(moe.tile_row[:, :], tr2[:, :])
        v.tensor_scalar(moe.tile_expert[:, :], te[:, :], float(E - 1), None, ALU.min)

    def fill(sp):
        for s in range(moe.spare):
            at = E * CAP + s * GT
            sp.dma_start(moe.dram_rows[at:at + GT, :].rearrange("(r p) w -> p r w", p=P),
                         moe.fill_rows[:, E + s, :, :]).then_inc(written, 16)
        sp.wait_ge(ended, 1)
        for e in range(E):
            at = sp.value_load(end_row[0:1, e:e + 1], min_val=e * CAP, max_val=e * CAP + TOK)
            sp.dma_start(moe.dram_rows[bass.ds(at, GT), :].rearrange("(r p) w -> p r w", p=P),
                         moe.fill_rows[:, e, :, :]).then_inc(written, 16)
        sp.wait_ge(written, 16 * (E + moe.spare))
    return tables, work_out, fill


def route(m, k, moe, rows):
    nc = m.nc
    E, top, W, CAP = moe.E, moe.top, moe.W, moe.CAP
    name = f"route{E}"
    sb = lambda n, shape, dt=F32: m.sb(f"{name}_{n}", shape, dt)
    row = sb("row", [P, 4, top, GR, W])
    index = [sb(f"index{q}", [P, top, GR], mybir.dt.int32) for q in range(4)]
    xT = sb("xT", [P, 2, GT])
    result_row = sb("result_row", [P, RT])
    prefer = sb("prefer", [P, E])
    before, ones = sb("before", [P, P], BF16), sb("ones", [P, P], BF16)
    pick = sb("pick", [P, top, GR, E])
    picked, slot = sb("picked", [P, top, GR, E]), sb("slot", [P, top, GR])
    w, rest, slots = sb("w", [P, GR, E]), sb("rest", [P, GR, E]), sb("slots", [P, GR, E])
    both = sb("both", [P, GR * E], BF16)
    best, narrow = sb("best", [P, top, GR]), sb("narrow", [P, 4, GR])
    bank_t, bank_l, bank_r = k.bank[0], k.bank[1:3], k.bank[3]

    plan_tables, plan_tiles, fill = plan(m, moe)
    zeroed, made = m.sem(name + "_zeroed"), m.sem(name + "_made")
    begun = m.sem(name + "_begun")
    normed = m.count(name + "_normed")
    labelled = m.count(name + "_labelled")
    turned, copied = m.count(name + "_turned"), m.count(name + "_copied")
    scored = m.count(name + "_scored")
    CHOICE = 5 * top + (1 if top == 2 else 0) + 1
    chosen = m.count(name + "_chosen", CHOICE + (4 if top == 2 else 0))
    powered = m.count(name + "_powered")
    ranked = m.count(name + "_ranked")
    placed = m.count(name + "_placed", 5)
    sent = [m.sem(f"{name}_sent{q}") for q in range(4)]
    per = 16 * GR * top
    TABLES = 7

    with nc.Block() as block:
        @block.gpsimd
        def _(pool):
            def iota(t, pattern, start, per_partition=0):
                nc.gpsimd.iota(t, pattern, base=start, channel_multiplier=per_partition,
                               allow_small_or_imprecise_dtypes=True).then_inc(made, 1)
            nc.gpsimd.memset(before[:, :], 1.0).then_inc(zeroed, 1)
            nc.gpsimd.memset(ones[:, :], 1.0).then_inc(made, 1)
            iota(prefer[:, :], [[-1, E]], E)
            iota(result_row[:, :], [[top * P, RT]], 0, top)
            iota(moe.base[:, :], [[CAP, E]], 0)
            iota(moe.end[:, :], [[CAP, E]], 0)
            iota(moe.fill_rows[:, :, :, W - 1], [[GT, E + moe.spare], [P, GR]], top * TOK, 1)
            pool.wait_ge(zeroed, 1)
            nc.gpsimd.affine_select(out=before[:, :], in_=before[:, :], compare_op=ALU.is_gt, fill=0.0, base=0,
                                    pattern=[[1, P]], channel_multiplier=-1).then_inc(made, 1)
            nc.gpsimd.memset(moe.fill_rows[:, :, :, 0:W - 1], 0.0).then_inc(made, 1)
            plan_tables(pool)
            pool.wait_ge(made, TABLES + 1)

            def step(s, q):
                t, q = s - 2, (q - 2) % 4
                if not live(t):
                    return
                pool.wait_ge(labelled.sem, labelled.at(t))
                pool.wait_ge(placed.sem, placed.at(t))
                pool.sem_inc(begun, 1)
                for i in range(top):
                    for r in range(GR):
                        pool.indirect_dma_start(moe.dram_rows[:, :],
                                                bass.IndirectOffsetOnAxis(ap=index[q][:, i, r:r + 1], axis=0),
                                                row[:, q, i, r, :], None).then_inc(sent[q], 16)
            pipelined(pool, 2, step, NG, 4)
            for q in range(4):
                pool.wait_ge(sent[q], NG // 4 * per)

        @block.vector
        def _(dve):
            v = nc.vector
            for c in (normed, chosen, placed):
                c.start(dve)
            dve.wait_ge(made, TABLES)

            def linked(count, t):
                n = [0]

                def link(ins):
                    n[0] += 1
                    ins.then_inc(count.sem, 1)
                    dve.wait_ge(count.sem, count.at(t, n[0]))
                return link, n

            def wide(a):
                return a.unsqueeze(2).broadcast_to([P, GR, E])

            def norm(t, q):
                if not live(t):
                    return
                if not isinstance(t, int) or t >= 4:
                    dve.wait_ge(sent[q], (t - q) * (per // 4))
                for r in range(GR):
                    at = bass.ds(t * GR + r, 1)
                    last = v.tensor_scalar(row[:, q, 0, r, 0:C], rows[:, at, :], k.mean[:, at], k.rstd[:, at],
                                           ALU.subtract, ALU.mult)
                last.then_inc(normed.sem, 1)

            def place(t, q):
                if not live(t):
                    return
                link, n = linked(placed, t)
                dve.wait_ge(ranked.sem, ranked.at(t))
                link(v.tensor_tensor(slots[:, :, :], bank_r[:, 0:GR * E].rearrange("p (r e) -> p r e", e=E),
                                     moe.end[:, :].unsqueeze(1).broadcast_to([P, GR, E]), ALU.add))
                link(v.tensor_tensor(moe.end[:, :], moe.end[:, :], bank_r[:, GR * E:(GR + 1) * E], ALU.add))
                link(v.tensor_tensor(picked[:, :, :, :], slots[:, :, :].unsqueeze(1).broadcast_to([P, top, GR, E]),
                                     pick[:, :, :, :], ALU.mult))
                link(v.tensor_reduce(slot[:, :, :], picked[:, :, :, :], AX.X, ALU.add))
                link(v.tensor_copy(index[q][:, :, :], slot[:, :, :]))
                assert n[0] == placed.per

            def choose(t, b, q):
                if not live(t):
                    return
                link, n = linked(chosen, t)
                dve.wait_ge(scored.sem, scored.at(t))
                score = bank_l[b][:, 0:GR * E].rearrange("p (r e) -> p r e", e=E)

                def find(scores, i):
                    link(v.tensor_reduce(best[:, i, :], scores, AX.X, ALU.max))
                    link(v.tensor_tensor(w[:, :, :], scores, wide(best[:, i, :]), ALU.is_equal))
                    link(v.tensor_tensor(w[:, :, :], w[:, :, :], prefer[:, :].unsqueeze(1).broadcast_to([P, GR, E]),
                                         ALU.mult))
                    link(v.tensor_reduce(narrow[:, 3, :], w[:, :, :], AX.X, ALU.max))
                    link(v.tensor_tensor(pick[:, i, :, :], w[:, :, :], wide(narrow[:, 3, :]), ALU.is_equal))

                by_row = both[:, :].rearrange("p (r e) -> p r e", e=E)
                find(score, 0)
                if top == 2:
                    link(v.scalar_tensor_tensor(rest[:, :, :], pick[:, 0, :, :], -3e38, score, ALU.mult, ALU.add))
                    find(rest[:, :, :], 1)
                dve.wait_ge(ranked.sem, ranked.at(t - 1))
                if top == 1:
                    link(v.tensor_copy(by_row, pick[:, 0, :, :]))
                else:
                    link(v.tensor_tensor(by_row, pick[:, 0, :, :], pick[:, 1, :, :], ALU.add))
                    assert n[0] == CHOICE
                    link(v.tensor_tensor(narrow[:, 0, :], best[:, 1, :], best[:, 0, :], ALU.subtract))
                    dve.wait_ge(powered.sem, powered.at(t))
                    link(v.tensor_scalar(narrow[:, 2, :], narrow[:, 1, :], 1.0, None, ALU.add))
                    link(v.reciprocal(row[:, q, 0, :, C], narrow[:, 2, :]))
                    link(v.tensor_tensor(row[:, q, 1, :, C], row[:, q, 0, :, C], narrow[:, 1, :], ALU.mult))
                assert n[0] == chosen.per

            def step(s, q):
                norm(s, q)
                place(s - 2, (q - 2) % 4)
                choose(s - 1, (q - 1) % 2, (q - 1) % 4)
            pipelined(dve, 2, step, NG, 4)
            plan_tiles(dve)

        @block.sync
        def _(sp):
            sp.wait_ge(made, TABLES + 1)
            fill(sp)

        @block.tensor
        def _(pe):
            for c in (turned, scored, ranked):
                c.start(pe)
            pe.wait_ge(made, TABLES)

            def step(s, q):
                if live(s):
                    pe.wait_ge(normed.sem, normed.at(s))
                    pe.wait_ge(copied.sem, copied.at(s - 1))
                    for r in range(GR):
                        last = nc.tensor.transpose(tiles(bank_t, r), row[:, q, 0, r, 0:C], k.ident[:, :])
                    last.then_inc(turned.sem, 1)
                    pe.wait_ge(copied.sem, copied.at(s))
                    pe.wait_ge(chosen.sem, chosen.at(s - 2))
                    for r in range(GR):
                        last = nc.tensor.matmul(bank_l[q % 2][:, r * E:(r + 1) * E], tiles(xT[:, q % 2, :], r),
                                                k.gate_w[:, :], start=True, stop=True)
                    last.then_inc(scored.sem, 1)
                if live(s - 1):
                    t = s - 1
                    pe.wait_ge(chosen.sem, chosen.at(t, CHOICE))
                    pe.wait_ge(placed.sem, placed.at(t - 1, 2))
                    nc.tensor.matmul(bank_r[:, 0:GR * E], before[:, :], both[:, :], start=True, stop=False,
                                     skip_group_check=True)
                    for d in range(1, GR + 1):
                        last = nc.tensor.matmul(bank_r[:, d * E:(GR + 1) * E], ones[:, :], both[:, 0:(GR + 1 - d) * E],
                                                start=False, stop=d == GR, skip_group_check=True)
                    last.then_inc(ranked.sem, 1)
            pipelined(pe, 1, step, NG, 4)

        @block.scalar
        def _(act):
            for c in (copied, labelled, powered):
                c.start(act)
            act.wait_ge(made, TABLES)

            def step(s, q):
                if live(s):
                    if not isinstance(s, int) or s >= 4:
                        act.wait_ge(sent[q], (s - q) * (per // 4))
                    act.wait_ge(turned.sem, turned.at(s))
                    act.wait_ge(scored.sem, scored.at(s - 2))
                    if moe.affine:
                        ins = nc.scalar.activation(xT[:, q % 2, :], bank_t[:, :], ACT.Identity, bias=k.ln2_b[:, 0:1],
                                                   scale=k.ln2_w[:, 0:1])
                    else:
                        ins = nc.scalar.copy(xT[:, q % 2, :], bank_t[:, :])
                    ins.then_inc(copied.sem, 1)
                    if moe.extra == C:
                        nc.scalar.copy(row[:, q, 0, :, C:2 * C], k.x[:, group(s), :])
                    if top == 2:
                        nc.scalar.copy(row[:, q, 1, :, 0:C], row[:, q, 0, :, 0:C])
                    for i in range(top):
                        last = nc.scalar.activation(row[:, q, i, :, W - 1], result_row[:, group(s)], ACT.Copy,
                                                    bias=float(i))
                    last.then_inc(labelled.sem, 1)
                if top == 2 and live(s - 1):
                    act.wait_ge(chosen.sem, chosen.at(s - 1, CHOICE + 1))
                    nc.scalar.activation(narrow[:, 1, :], narrow[:, 0, :], ACT.Exp).then_inc(powered.sem, 1)
            pipelined(act, 1, step, NG, 4)


def run_tiles(m, k, moe, up_dram, down_dram):
    nc = m.nc
    E, NK, NT, W, gated = moe.E, moe.NK, moe.NT, moe.W, moe.gated
    HU = NK * P * (2 if gated else 1)
    name = f"tile{E}"
    rows = m.sb(name + "_rows", [P, 4, GR, W])
    up_w, down_w = m.sb(name + "_up", [P, 2, HU]), m.sb(name + "_down", [P, 4, NK, C])
    xT = m.sb(name + "_xT", [P, 2, GT])
    silu = m.sb(name + "_silu", [P, 2, GT])
    hidden = m.sb(name + "_hidden", [P, 2, NK, GT])
    y = m.sb(name + "_y", [P, 4, GR, C])
    index = [[m.sb(f"{name}_index{q}{r}", [P, 1], mybir.dt.int32) for r in range(GR)] for q in range(4)]
    w_high, w_rest = (m.sb(f"{name}_w_{n}", [P, 2, HU], F32R) for n in ("high", "rest"))
    x_high, x_rest = (m.sb(f"{name}_x_{n}", [P, 2, GT], F32R) for n in ("high", "rest"))
    w_rounded = m.count(name + "_w_rounded", 1, NT)
    split = m.count(name + "_split", 3, NT)
    bank_t, bank_g, bank_u, bank_y = k.bank[0], k.bank[1:3], k.bank[3:5], k.bank[5:7]
    rows_loaded = [m.sem(f"{name}_rows_loaded{q}") for q in range(4)]
    up_loaded = [m.sem(f"{name}_up_loaded{b}") for b in range(2)]
    down_loaded = [m.sem(f"{name}_down_loaded{q}") for q in range(4)]
    sent = [m.sem(f"{name}_sent{q}") for q in range(4)]
    turned, copied = m.count(name + "_turned", 1, NT), m.count(name + "_copied", 1, NT)
    raised, silued = m.count(name + "_raised", NK, NT), m.count(name + "_silued", NK, NT)
    bent = m.count(name + "_bent", NK, NT) if gated else silued
    lowered = m.count(name + "_lowered", 1, NT)
    begun = m.sem(name + "_begun")
    finished = m.count(name + "_finished", 1, NT)

    def loads(t, b, per=16, buffers=2):
        return (t - b) * (per // buffers) + per

    with nc.Block() as block:
        @block.sync
        def _(sp):
            def load_rows(t, q):
                if not live(t, NT):
                    return
                at = sp.value_load(moe.tile_row[0:1, bass.ds(t, 1)], min_val=0, max_val=moe.rows - GT)
                if not isinstance(t, int) or t >= 4:
                    sp.wait_ge(turned.sem, turned.at(t - 4))
                    sp.wait_ge(finished.sem, finished.at(t - 4))
                sp.dma_start(rows[:, q, :, :], moe.dram_rows[bass.ds(at, GT), :].rearrange("(r p) w -> p r w", p=P)
                             ).then_inc(rows_loaded[q], 16)

            def load_weights(t, q):
                b = q % 2
                if not live(t, NT):
                    return
                e = sp.value_load(moe.tile_expert[0:1, bass.ds(t, 1)], min_val=0, max_val=E - 1)
                sp.wait_ge(w_rounded.sem, w_rounded.at(t - 2))
                sp.wait_ge(split.sem, split.at(t - 2))
                sp.dma_start(up_w[:, b:b + 1, :], up_dram[bass.ds(e, 1), :, :].rearrange("e c h -> c e h")
                             ).then_inc(up_loaded[b], 16)
                if not isinstance(t, int) or t >= 4:
                    sp.wait_ge(lowered.sem, lowered.at(t - 4))
                sp.dma_start(down_w[:, q, :, :], down_dram[bass.ds(e, 1), :, :].rearrange("e (k h) c -> h (e k) c", h=P)
                             ).then_inc(down_loaded[q], 16)

            def step(s, q):
                load_weights(s, q)
                load_rows(s, q)
            pipelined(sp, 0, step, NT, 4)

        @block.tensor
        def _(pe):
            for c in (turned, raised, lowered):
                c.start(pe)

            def turn(t, q):
                if not live(t, NT):
                    return
                pe.wait_ge(rows_loaded[q], loads(t, q, 16, 4))
                pe.wait_ge(copied.sem, copied.at(t - 1))
                for r in range(GR):
                    last = nc.tensor.transpose(tiles(bank_t, r), rows[:, q, r, 0:C], k.ident[:, :])
                last.then_inc(turned.sem, 1)

            def up(t, b, j):
                if not live(t, NT):
                    return
                i = (b * NK + j) % 2
                if j == 0:
                    pe.wait_ge(w_rounded.sem, w_rounded.at(t))
                    pe.wait_ge(split.sem, split.at(t))
                pe.wait_ge(bent.sem, bent.at(t, j - 1))
                for bank, block in ((bank_g[i], j), (bank_u[i], NK + j))[:2 if gated else 1]:
                    cols = slice(block * P, (block + 1) * P)
                    nc.tensor.matmul(bank[:, :], w_high[:, b, cols], x_rest[:, b, :], start=True, stop=False)
                    nc.tensor.matmul(bank[:, :], w_rest[:, b, cols], x_high[:, b, :], start=False, stop=False)
                    last = nc.tensor.matmul(bank[:, :], w_high[:, b, cols], x_high[:, b, :], start=False, stop=True)
                last.then_inc(raised.sem, 1)

            def down(t, q, j):
                b = q % 2
                if not live(t, NT):
                    return
                if j == 0:
                    pe.wait_ge(down_loaded[q], loads(t, q, 16, 4))
                    pe.wait_ge(finished.sem, finished.at(t - 2))
                pe.wait_ge(bent.sem, bent.at(t, j + 1))
                for r in range(GR):
                    last = nc.tensor.matmul(tiles(bank_y[b], r), tiles(hidden[:, b, j, :], r), down_w[:, q, j, :],
                                            start=j == 0 and r == 0, stop=j == NK - 1, skip_group_check=True)
                if j == NK - 1:
                    last.then_inc(lowered.sem, 1)

            def step(s, q):
                odd = q % 2
                for j in range(NK):
                    up(s - 1, 1 - odd, j)
                    if j == 0:
                        turn(s, q)
                    down(s - 2, (q - 2) % 4, j)
            pipelined(pe, 2, step, NT, 4)

        @block.scalar
        def _(act):
            copied.start(act)
            silued.start(act)
            w_rounded.start(act)

            def round_weights(t, b):
                if not live(t, NT):
                    return
                act.wait_ge(up_loaded[b], loads(t, b))
                act.wait_ge(raised.sem, raised.at(t - 2))
                nc.scalar.copy(w_high[:, b, :], up_w[:, b, :]).then_inc(w_rounded.sem, 1)

            def copy(t, b):
                if not live(t, NT):
                    return
                act.wait_ge(turned.sem, turned.at(t))
                act.wait_ge(raised.sem, raised.at(t - 2))
                if moe.affine:
                    ins = nc.scalar.activation(xT[:, b, :], bank_t[:, :], ACT.Identity, bias=k.ln2_b[:, 0:1],
                                               scale=k.ln2_w[:, 0:1])
                else:
                    ins = nc.scalar.copy(xT[:, b, :], bank_t[:, :])
                ins.then_inc(copied.sem, 1)

            def activate(t, b, j):
                if not live(t, NT):
                    return
                i = (b * NK + j) % 2
                act.wait_ge(raised.sem, raised.at(t, j + 1))
                if gated:
                    act.wait_ge(bent.sem, bent.at(t, j - 1))
                    dst = silu[:, i, :]
                else:
                    act.wait_ge(lowered.sem, lowered.at(t - 2))
                    dst = hidden[:, b, j, :]
                nc.scalar.activation(dst, bank_g[i][:, :], ACT.Silu).then_inc(silued.sem, 1)

            def step(s, q):
                odd = q % 2
                round_weights(s, odd)
                for j in range(NK):
                    activate(s - 1, 1 - odd, j)
                    if j == 0:
                        copy(s, odd)
            pipelined(act, 1, step, NT, 4)

        @block.vector
        def _(dve):
            finished.start(dve)
            split.start(dve)
            if gated:
                bent.start(dve)

            def split_weights(t, b):
                if not live(t, NT):
                    return
                dve.wait_ge(w_rounded.sem, w_rounded.at(t))
                dve.wait_ge(raised.sem, raised.at(t - 2))
                nc.vector.tensor_tensor(w_rest[:, b, :], up_w[:, b, :], w_high[:, b, :], ALU.subtract
                                        ).then_inc(split.sem, 1)

            def split_rows(t, b):
                if not live(t, NT):
                    return
                dve.wait_ge(copied.sem, copied.at(t))
                nc.vector.tensor_copy(x_high[:, b, :], xT[:, b, :]).then_inc(split.sem, 1)
                dve.wait_ge(split.sem, split.at(t, 2))
                nc.vector.tensor_tensor(x_rest[:, b, :], xT[:, b, :], x_high[:, b, :], ALU.subtract
                                        ).then_inc(split.sem, 1)

            def finish(t, q):
                b = q % 2
                if not live(t, NT):
                    return
                dve.wait_ge(lowered.sem, lowered.at(t))
                if not isinstance(t, int) or t >= 4:
                    dve.wait_ge(sent[q], loads(t, q, 16 * GR, 4) - 16 * GR)
                for r in range(GR):
                    nc.vector.tensor_copy(index[q][r][:, :], rows[:, q, r, W - 1:W])
                bank = bank_y[b][:, :].rearrange("p (r c) -> p r c", c=C)
                if moe.extra == 1:
                    last = nc.vector.tensor_tensor(y[:, q, :, :], bank, rows[:, q, :, C:C + 1].broadcast_to([P, GR, C]),
                                                   ALU.mult)
                else:
                    last = nc.vector.tensor_tensor(y[:, q, :, :], bank, rows[:, q, :, C:2 * C], ALU.add)
                last.then_inc(finished.sem, 1)

            def bend(t, b, j):
                if not live(t, NT):
                    return
                i = (b * NK + j) % 2
                dve.wait_ge(silued.sem, silued.at(t, j + 1))
                if j == 0:
                    dve.wait_ge(lowered.sem, lowered.at(t - 2))
                nc.vector.tensor_tensor(hidden[:, b, j, :], silu[:, i, :], bank_u[i][:, :], ALU.mult
                                        ).then_inc(bent.sem, 1)

            def step(s, q):
                odd = q % 2
                for j in range(NK):
                    if gated:
                        bend(s - 1, 1 - odd, j)
                    if j == 0:
                        split_weights(s, odd)
                    if j == 1:
                        split_rows(s, odd)
                finish(s - 2, (q - 2) % 4)
            pipelined(dve, 2, step, NT, 4)

        @block.gpsimd
        def _(pool):
            def step(s, q):
                pool.wait_ge(finished.sem, finished.at(s))
                pool.sem_inc(begun, 1)
                for r in range(GR):
                    pool.indirect_dma_start(moe.dst[:, :], bass.IndirectOffsetOnAxis(ap=index[q][r][:, 0:1], axis=0),
                                            y[:, q, r, :], None).then_inc(sent[q], 16)
            pipelined(pool, 0, step, NT, 4)
            for q in range(4):
                pool.wait_ge(sent[q], len(range(q, NT, 4)) * 16 * GR)


def combine(m, k, moe):
    nc = m.nc
    got = m.sb("combine_got", [P, 4, GR, 2 * C])
    total = m.sb("combine_total", [P, 2, GR, C])
    loaded = [m.sem(f"combine_loaded{q}") for q in range(4)]
    summed, added = m.count("combine_summed"), m.count("combine_added")
    src = moe.dst[0:2 * TOK, :].rearrange("(r p i) c -> p r (i c)", i=2, p=P)
    with nc.Block() as block:
        @block.sync
        def _(sp):
            def step(s, q):
                if not isinstance(s, int) or s >= 4:
                    sp.wait_ge(summed.sem, summed.at(s - 4))
                sp.dma_start(got[:, q, :, :], src[:, group(s), :]).then_inc(loaded[q], 16)
            pipelined(sp, 0, step, NG, 4, peeled=4)

        @block.gpsimd
        def _(pool):
            summed.start(pool)

            def step(s, q):
                pool.wait_ge(loaded[q], (s - q) * 4 + 16)
                pool.wait_ge(added.sem, added.at(s - 2))
                nc.gpsimd.tensor_tensor(total[:, q % 2, :, :], got[:, q, :, 0:C], got[:, q, :, C:2 * C], ALU.add
                                        ).then_inc(summed.sem, 1)
            pipelined(pool, 0, step, NG, 4)

        @block.vector
        def _(dve):
            added.start(dve)

            def step(s, odd):
                dve.wait_ge(summed.sem, summed.at(s))
                x = k.x[:, group(s), :]
                nc.vector.tensor_tensor(x, total[:, odd, :, :], x, ALU.add).then_inc(added.sem, 1)
                dve.wait_ge(added.sem, added.at(s))
                for r in range(GR):
                    at = bass.ds(s * GR + r, 1)
                    nc.vector.bn_stats(k.stats[:, at, :], k.x[:, at, :])
            pipelined(dve, 0, step)


def experts(m, k, moe, rows, up_dram, down_dram):
    with ExitStack() as own:
        mine = Machine(m.nc, own)
        moe.base, moe.end = (mine.sb(f"part_{n}{moe.E}", [P, moe.E]) for n in ("base", "end"))
        moe.fill_rows = mine.sb(f"fill_rows{moe.E}", [P, moe.E + moe.spare, GR, moe.W])
        route(mine, k, moe, rows)
        mine.clear()
    run_tiles(m, k, moe, up_dram, down_dram)


def phase_b(m, k, dram):
    moe = fresh("B")
    moe.dram_rows, moe.dst = dram["rows_b"], dram["results_b"]
    moe.tile_expert, moe.tile_row = (m.sb("tile_b_" + n, [1, moe.NT], mybir.dt.int32) for n in ("expert", "row"))
    experts(m, k, moe, k.x, dram["L0_ffn_W1"], dram["L0_ffn_W2"])
    combine(m, k, moe)


def phase_e(m, k, dram):
    moe = fresh("E")
    moe.dram_rows, moe.dst = dram["rows_e"], dram["out"]
    moe.tile_expert, moe.tile_row = (m.sb("tile_e_" + n, [1, moe.NT], mybir.dt.int32) for n in ("expert", "row"))
    experts(m, k, moe, k.u, dram["L1_ffn_expert_wv"], dram["L1_ffn_expert_proj"])


PHASES = {"A": phase_a, "B": phase_b, "C": phase_c, "D": phase_d, "E": phase_e}


def build(nc, dram, out, phases="ABCDE"):
    b = fresh("B")
    dram = dict(dram, out=out, rows_b=nc.dram_tensor("rows_b", [b.rows, b.W], F32, kind="Internal").ap(),
                results_b=nc.dram_tensor("results_b", [b.dst_rows, C], F32, kind="Internal").ap(),
                rows_e=nc.dram_tensor("rows_e", [fresh("E").rows, fresh("E").W], F32, kind="Internal").ap())
    with ExitStack() as ctx:
        m = Machine(nc, ctx)

        class Kept:
            pass
        k = Kept()
        k.x = m.sb("x_rows", [P, RT, C])
        k.u = m.sb("u_rows", [P, RT, C])
        k.stats = m.sb("stats", [P, RT, 6])
        k.mean = m.sb("mean", [P, RT])
        k.rstd = m.sb("rstd", [P, RT])
        k.rstd2 = m.sb("rstd2", [P, RT])
        k.work = m.sb("work", [P, 10, RT])
        k.eps = m.sb("eps", [P, 1])
        k.bank = [m.psum(f"bank{i}") for i in range(8)]
        k.ident = m.sb("ident", [P, P])
        k.ident_bf = m.sb("ident_bf", [P, P], BF16)
        load_phase(m, k, dram)
        for phase in phases:
            with ExitStack() as own:
                mine = Machine(nc, own)
                constants(mine, k, dram, phase)
                statistics(mine, k, phase)
                PHASES[phase](mine, k, dram)
                mine.clear()
        if phases[-1] == "E":
            return
        stored = m.sem("stored")
        with nc.Block() as block:
            @block.sync
            def _(sp):
                sp.dma_start(dram["out"][0:TOK, :].rearrange("(r p) c -> p r c", p=P), k.x[:, :, :]).then_inc(stored, 16)
                sp.wait_ge(stored, 16)




def shape_tables():
    import numpy as np
    f32 = np.float32
    pos = np.arange(SEQ, dtype=f32)
    half = C // 2
    scale = ((np.arange(0, C, 2, dtype=f32) + f32(0.4 * C)) / f32(1.4 * C))[None, :] ** (pos / f32(512.0))[:, None]
    freqs = f32(1.0) / f32(10000.0) ** (np.arange(half, dtype=f32) / f32(half))
    angle = pos[:, None] * freqs[None, :]
    cos, sin = np.cos(angle), np.sin(angle)
    rope_a = np.stack([np.repeat(t, 2, axis=1).T for t in (cos * scale, sin * scale, cos / scale, sin / scale)], 1)
    tok = np.arange(P)
    same = (tok[:, None] // SEQ) == (tok[None, :] // SEQ)
    diff = (tok[None, :] - tok[:, None]).astype(f32)
    decay = np.where(same & (diff >= 0), f32(0.96875) ** np.maximum(diff, 0), f32(0.0)).astype(f32)
    causal = tok[:, None] >= tok[None, :]
    self_mask = np.where(same & causal, f32(0), f32(MASKED))
    cross_mask = np.where(same, f32(0), f32(MASKED))
    head_mask = np.where((tok[:, None] % SEQ) >= np.arange(SEQ)[None, :], f32(0), f32(MASKED))
    masks = np.stack([np.tile(self_mask, (1, GR)), np.tile(cross_mask, (1, GR)), np.tile(head_mask, (1, 8))], 1)
    inv = f32(1.0) / f32(10000.0) ** (np.arange(0, 8, 2, dtype=f32) / f32(8))
    emb = np.concatenate([pos[:, None] * inv[None, :]] * 2, axis=1)
    rope_d = np.stack([np.tile(np.cos(emb).T, (16, 1)), np.tile(np.sin(emb).T, (16, 1))], 1)
    return {n: np.ascontiguousarray(t.astype(f32)) for n, t in
            (("rope_a", rope_a), ("decay", decay), ("masks", masks), ("rope_d", rope_d))}


def kernel(**inputs):
    import numpy as np
    import concourse.bacc as bacc
    from concourse.bass_utils import run_bass_kernel_spmd

    nc = bacc.Bacc("TRN2", target_bir_lowering=False, num_devices=1)
    arrays = {n: np.ascontiguousarray(a) for n, a in inputs.items()} | shape_tables()
    dram = {n: nc.dram_tensor(n + "_dram", a.shape, mybir.dt.from_np(a.dtype), kind="ExternalInput").ap()
            for n, a in arrays.items()}
    out = nc.dram_tensor("out_dram", [fresh("E").dst_rows, C], F32, kind="ExternalOutput").ap()
    build(nc, dram, out)
    got = run_bass_kernel_spmd(nc, [{n + "_dram": a for n, a in arrays.items()}], core_ids=[0])
    return got.results[0]["out_dram"][:TOK].reshape(BATCHES, SEQ, C)
```
